# Optimizing a Trainium2 kernel written in Bass

```python
import numpy as np
import jax
import jax.numpy as jnp

def _softmax(x, axis=-1):
    return jax.nn.softmax(x, axis=axis)

def _gelu(x):
    return jax.nn.gelu(x, approximate=True)

def _silu(x):
    return jax.nn.silu(x)

def _sigmoid(x):
    return jax.nn.sigmoid(x)

def _layernorm(x, axis=-1, eps=1e-05):
    m = jnp.mean(x, axis=axis, keepdims=True)
    v = jnp.var(x, axis=axis, keepdims=True)
    return (x - m) / jnp.sqrt(v + eps)

def _scatter_add(tgt, idx, src, axis=0):
    return tgt.at[idx].add(src)

def _segment_sum(src, seg, n):
    return jax.ops.segment_sum(src, seg, n)
kernel_name = 'mk_hybrid_d1_jaxref_r8_ae5fc3'

def setup_inputs(seed: int=0):
    np.random.seed(seed)
    _w = jnp.asarray

    def _L0_attn_a_setup():
        import jax, jax.numpy as jnp
        import numpy as np
        D = 128
        K = 4
        SCALE = D ** (-0.5)

        def rmsnorm(x, gamma):
            n = jnp.linalg.norm(x, axis=-1, keepdims=True)
            return x / n * (gamma / SCALE)

        def causal_dwconv(z, w, b):
            zc = jnp.transpose(z, (0, 2, 1))
            y = jax.lax.conv_general_dilated(zc, w, window_strides=(1,), padding=[(K - 1, 0)], dimension_numbers=('NCH', 'OIH', 'NCH'), feature_group_count=D)
            y = y + b[None, :, None]
            return jnp.transpose(y, (0, 2, 1))

        def hawk(x, input_w, conv_w, conv_b, gates_w, gates_b, forget_base, output_w):
            u = x @ input_w.T
            gate, z = jnp.split(u, 2, axis=-1)
            z = causal_dwconv(z, conv_w, conv_b)
            fg = z @ gates_w.T + gates_b
            forget, inp = jnp.split(fg, 2, axis=-1)
            alpha = jnp.exp(-8.0 * jax.nn.softplus(forget_base) * jax.nn.sigmoid(forget))
            beta = jnp.sqrt(1.0 - alpha ** 2 + 1e-06)
            xs = beta * jax.nn.sigmoid(inp) * z

            def combine(c1, c2):
                a1, x1 = c1
                a2, x2 = c2
                return (a1 * a2, a2 * x1 + x2)
            _, h = jax.lax.associative_scan(combine, (alpha, xs), axis=1)
            return jax.nn.gelu(gate, approximate=False) * h @ output_w.T

        def gated_mlp(x, grow_w, shrink_w):
            u = x @ grow_w.T
            gate, v = jnp.split(u, 2, axis=-1)
            return jax.nn.gelu(gate, approximate=False) * v @ shrink_w.T
        key = jax.random.key(seed)
        ks = jax.random.split(key, 9)
        B, T = (4, 512)
        H = 2 * D
        return {'x': jax.random.normal(ks[0], (B, T, D), jnp.float32), 'hawk_norm_gamma': jnp.ones((D,), jnp.float32), 'input_w': jax.random.normal(ks[1], (2 * D, D), jnp.float32) * D ** (-0.5), 'conv_w': jax.random.normal(ks[2], (D, 1, K), jnp.float32) * (1.0 / K) ** 0.5, 'conv_b': jnp.zeros((D,), jnp.float32), 'gates_w': jax.random.normal(ks[3], (2 * D, D), jnp.float32) * D ** (-0.5), 'gates_b': jnp.zeros((2 * D,), jnp.float32), 'forget_base': jnp.linspace(-4.323, -9.0, D, dtype=jnp.float32), 'output_w': jax.random.normal(ks[4], (D, D), jnp.float32) * D ** (-0.5), 'gmlp_norm_gamma': jnp.ones((D,), jnp.float32), 'grow_w': jax.random.normal(ks[5], (2 * H, D), jnp.float32) * D ** (-0.5), 'shrink_w': jax.random.normal(ks[6], (D, H), jnp.float32) * H ** (-0.5)}
    _L0_attn_a_in = _L0_attn_a_setup()

    def _L0_attn_b_setup():
        import jax, jax.numpy as jnp
        import numpy as np
        B, S, DIM, H, DH = (2, 256, 128, 16, 64)
        INNER = H * DH

        def _rmsnorm(t, gamma, scale):
            normed = t * jax.lax.rsqrt(jnp.mean(t * t, axis=-1, keepdims=True) + 1e-08)
            return normed * scale * gamma
        key = jax.random.key(seed)
        ks = jax.random.split(key, 4)
        sd = 0.02
        return {'x': jax.random.normal(ks[0], (B, S, DIM), dtype=jnp.float32), 'ln_w': jnp.ones((DIM,), jnp.float32), 'ln_b': jnp.zeros((DIM,), jnp.float32), 'Wq': jax.random.normal(ks[1], (DIM, INNER), jnp.float32) * sd, 'Wkv': jax.random.normal(ks[2], (DIM, 2 * INNER), jnp.float32) * sd, 'q_gamma': jnp.ones((H, 1, DH), jnp.float32), 'k_gamma': jnp.ones((H, 1, DH), jnp.float32), 'Wo': jax.random.normal(ks[3], (INNER, DIM), jnp.float32) * sd}
    _L0_attn_b_in = _L0_attn_b_setup()

    def _L0_ffn_setup():
        import jax, jax.numpy as jnp
        import numpy as np
        DIM = 128
        DEPTH = 6
        HEADS = 16
        DIM_HEAD = 64
        WINDOW = 32
        INNER = HEADS * DIM_HEAD
        DIM_INNER = int(DIM * 4 * 2 / 3)
        QK_SCALE = 8.0

        def shift_tokens(t):
            a, s = jnp.split(t, 2, -1)
            s = jnp.pad(s, ((0, 0), (1, 0), (0, 0)))[:, :-1]
            return jnp.concatenate([a, s], -1)

        def l2norm(t):
            return t / jnp.maximum(jnp.linalg.norm(t, axis=-1, keepdims=True), 1e-12)

        def rotate_half(x):
            x1, x2 = jnp.split(x, 2, -1)
            return jnp.concatenate([-x2, x1], -1)

        def rotary_tables(n):
            half = jnp.arange(0, DIM_HEAD, 2, dtype=jnp.float32)
            inv_freq = 1.0 / 10000.0 ** (half / DIM_HEAD)
            t = jnp.arange(n, dtype=jnp.float32)
            freqs = t[:, None] * inv_freq[None, :]
            freqs = jnp.concatenate([freqs, freqs], -1)
            base_scale = (half + 0.4 * DIM_HEAD) / (1.4 * DIM_HEAD)
            power = (t - n // 2) / (WINDOW // 2)
            scale = base_scale[None, :] ** power[:, None]
            scale = jnp.concatenate([scale, scale], -1)
            return (freqs, scale)

        def local_attention(q, k, v):
            b, h, n, d = q.shape
            w = WINDOW
            nw = n // w
            bq = q.reshape(b, h, nw, w, d)
            bk = k.reshape(b, h, nw, w, d)
            bv = v.reshape(b, h, nw, w, d)

            def look(t):
                p = jnp.pad(t, ((0, 0), (0, 0), (1, 0), (0, 0), (0, 0)))
                return jnp.concatenate([p[:, :, :nw], p[:, :, 1:]], axis=3)
            bk2, bv2 = (look(bk), look(bv))
            seq = jnp.arange(n).reshape(nw, w)
            seq_p = jnp.pad(seq, ((1, 0), (0, 0)), constant_values=-1)
            jt = jnp.concatenate([seq_p[:nw], seq_p[1:]], axis=1)
            it = seq[:, :, None]
            jb = jt[:, None, :]
            mask = (it < jb) | (it > jb + w) | (jb == -1)
            sim = jnp.einsum('bhwie,bhwje->bhwij', bq, bk2) * QK_SCALE
            sim = jnp.where(mask, -jnp.finfo(sim.dtype).max, sim)
            attn = jax.nn.softmax(sim, -1)
            out = jnp.einsum('bhwij,bhwje->bhwie', attn, bv2)
            return out.reshape(b, h, n, d)

        def attn_layer(x, Wqkv, qs, ksc, Wo):
            b, n, _ = x.shape
            qkv = x @ Wqkv
            q, k, v = jnp.split(qkv, 3, -1)
            sh = lambda t: t.reshape(b, n, HEADS, DIM_HEAD).transpose(0, 2, 1, 3)
            q, k, v = (sh(q), sh(k), sh(v))
            q = l2norm(q) * qs
            k = l2norm(k) * ksc
            freqs, scale = rotary_tables(n)
            cos, sin = (jnp.cos(freqs), jnp.sin(freqs))
            q = q * cos * scale + rotate_half(q) * sin * scale
            inv = 1.0 / scale
            k = k * cos * inv + rotate_half(k) * sin * inv
            out = local_attention(q, k, v)
            out = out.transpose(0, 2, 1, 3).reshape(b, n, INNER)
            return out @ Wo

        def ffn_layer(x, g, bln, W1, b1, W2, b2):
            mu = x.mean(-1, keepdims=True)
            var = ((x - mu) ** 2).mean(-1, keepdims=True)
            xn = (x - mu) / jnp.sqrt(var + 1e-05) * g + bln
            hg = xn @ W1 + b1
            a, gate = jnp.split(hg, 2, -1)
            return a * jax.nn.gelu(gate, approximate=False) @ W2 + b2
        key = jax.random.key(seed)
        ks = jax.random.split(key, 8)
        B, N = (2, 256)
        init = lambda k, shape: jax.random.normal(k, shape, jnp.float32) * 0.02
        return {'x': jax.random.normal(ks[0], (B, N, DIM), jnp.float32), 'Wqkv': init(ks[1], (DEPTH, DIM, 3 * INNER)), 'q_scale': jnp.ones((DEPTH, DIM_HEAD), jnp.float32), 'k_scale': jnp.ones((DEPTH, DIM_HEAD), jnp.float32), 'Wo': init(ks[2], (DEPTH, INNER, DIM)), 'ln_g': jnp.ones((DEPTH, DIM), jnp.float32), 'ln_b': jnp.zeros((DEPTH, DIM), jnp.float32), 'W1': init(ks[3], (DEPTH, DIM, 2 * DIM_INNER)), 'b1': jnp.zeros((DEPTH, 2 * DIM_INNER), jnp.float32), 'W2': init(ks[4], (DEPTH, DIM_INNER, DIM)), 'b2': jnp.zeros((DEPTH, DIM), jnp.float32)}
    _L0_ffn_in = _L0_ffn_setup()
    _d = {'L0_attn_a_x': _L0_attn_a_in['x'], 'L0_attn_a_hawk_norm_gamma': _L0_attn_a_in['hawk_norm_gamma'], 'L0_attn_a_input_w': _L0_attn_a_in['input_w'], 'L0_attn_a_conv_w': _L0_attn_a_in['conv_w'], 'L0_attn_a_conv_b': _L0_attn_a_in['conv_b'], 'L0_attn_a_gates_w': _L0_attn_a_in['gates_w'], 'L0_attn_a_gates_b': _L0_attn_a_in['gates_b'], 'L0_attn_a_forget_base': _L0_attn_a_in['forget_base'], 'L0_attn_a_output_w': _L0_attn_a_in['output_w'], 'L0_attn_a_gmlp_norm_gamma': _L0_attn_a_in['gmlp_norm_gamma'], 'L0_attn_a_grow_w': _L0_attn_a_in['grow_w'], 'L0_attn_a_shrink_w': _L0_attn_a_in['shrink_w'], 'L0_attn_b_ln_w': _L0_attn_b_in['ln_w'], 'L0_attn_b_ln_b': _L0_attn_b_in['ln_b'], 'L0_attn_b_Wq': _L0_attn_b_in['Wq'], 'L0_attn_b_Wkv': _L0_attn_b_in['Wkv'], 'L0_attn_b_q_gamma': _L0_attn_b_in['q_gamma'], 'L0_attn_b_k_gamma': _L0_attn_b_in['k_gamma'], 'L0_attn_b_Wo': _L0_attn_b_in['Wo'], 'L0_ffn_Wqkv': _L0_ffn_in['Wqkv'], 'L0_ffn_q_scale': _L0_ffn_in['q_scale'], 'L0_ffn_k_scale': _L0_ffn_in['k_scale'], 'L0_ffn_Wo': _L0_ffn_in['Wo'], 'L0_ffn_ln_g': _L0_ffn_in['ln_g'], 'L0_ffn_ln_b': _L0_ffn_in['ln_b'], 'L0_ffn_W1': _L0_ffn_in['W1'], 'L0_ffn_b1': _L0_ffn_in['b1'], 'L0_ffn_W2': _L0_ffn_in['W2'], 'L0_ffn_b2': _L0_ffn_in['b2']}
    _x0 = _d['L0_attn_a_x']
    _d['L0_attn_a_x'] = jax.random.normal(jax.random.fold_in(jax.random.key(seed), 1), (1, 2048, 128), dtype=_x0.dtype)
    del _x0
    return _d

def reference(L0_attn_a_x, L0_attn_a_hawk_norm_gamma, L0_attn_a_input_w, L0_attn_a_conv_w, L0_attn_a_conv_b, L0_attn_a_gates_w, L0_attn_a_gates_b, L0_attn_a_forget_base, L0_attn_a_output_w, L0_attn_a_gmlp_norm_gamma, L0_attn_a_grow_w, L0_attn_a_shrink_w, L0_attn_b_ln_w, L0_attn_b_ln_b, L0_attn_b_Wq, L0_attn_b_Wkv, L0_attn_b_q_gamma, L0_attn_b_k_gamma, L0_attn_b_Wo, L0_ffn_Wqkv, L0_ffn_q_scale, L0_ffn_k_scale, L0_ffn_Wo, L0_ffn_ln_g, L0_ffn_ln_b, L0_ffn_W1, L0_ffn_b1, L0_ffn_W2, L0_ffn_b2):

    def _L0_attn_a_ref(x, hawk_norm_gamma, input_w, conv_w, conv_b, gates_w, gates_b, forget_base, output_w, gmlp_norm_gamma, grow_w, shrink_w):
        import jax, jax.numpy as jnp
        import numpy as np
        D = 128
        K = 4
        SCALE = D ** (-0.5)

        def rmsnorm(x, gamma):
            n = jnp.linalg.norm(x, axis=-1, keepdims=True)
            return x / n * (gamma / SCALE)

        def causal_dwconv(z, w, b):
            zc = jnp.transpose(z, (0, 2, 1))
            y = jax.lax.conv_general_dilated(zc, w, window_strides=(1,), padding=[(K - 1, 0)], dimension_numbers=('NCH', 'OIH', 'NCH'), feature_group_count=D)
            y = y + b[None, :, None]
            return jnp.transpose(y, (0, 2, 1))

        def hawk(x, input_w, conv_w, conv_b, gates_w, gates_b, forget_base, output_w):
            u = x @ input_w.T
            gate, z = jnp.split(u, 2, axis=-1)
            z = causal_dwconv(z, conv_w, conv_b)
            fg = z @ gates_w.T + gates_b
            forget, inp = jnp.split(fg, 2, axis=-1)
            alpha = jnp.exp(-8.0 * jax.nn.softplus(forget_base) * jax.nn.sigmoid(forget))
            beta = jnp.sqrt(1.0 - alpha ** 2 + 1e-06)
            xs = beta * jax.nn.sigmoid(inp) * z

            def combine(c1, c2):
                a1, x1 = c1
                a2, x2 = c2
                return (a1 * a2, a2 * x1 + x2)
            _, h = jax.lax.associative_scan(combine, (alpha, xs), axis=1)
            return jax.nn.gelu(gate, approximate=False) * h @ output_w.T

        def gated_mlp(x, grow_w, shrink_w):
            u = x @ grow_w.T
            gate, v = jnp.split(u, 2, axis=-1)
            return jax.nn.gelu(gate, approximate=False) * v @ shrink_w.T
        x = x + hawk(rmsnorm(x, hawk_norm_gamma), input_w, conv_w, conv_b, gates_w, gates_b, forget_base, output_w)
        x = x + gated_mlp(rmsnorm(x, gmlp_norm_gamma), grow_w, shrink_w)
        return x

    def _L0_attn_b_ref(x, ln_w, ln_b, Wq, Wkv, q_gamma, k_gamma, Wo):
        import jax, jax.numpy as jnp
        import numpy as np
        B, S, DIM, H, DH = (2, 256, 128, 16, 64)
        INNER = H * DH

        def _rmsnorm(t, gamma, scale):
            normed = t * jax.lax.rsqrt(jnp.mean(t * t, axis=-1, keepdims=True) + 1e-08)
            return normed * scale * gamma
        h, dh = (q_gamma.shape[0], q_gamma.shape[-1])
        b, s, _ = x.shape
        mean = jnp.mean(x, axis=-1, keepdims=True)
        var = jnp.var(x, axis=-1, keepdims=True)
        xn = ln_w * (x - mean) / jnp.sqrt(var + 1e-05) + ln_b
        q = xn @ Wq
        k, v = jnp.split(xn @ Wkv, 2, axis=-1)
        to_heads = lambda t: t.reshape(b, s, h, dh).transpose(0, 2, 1, 3)
        q, k, v = (to_heads(q), to_heads(k), to_heads(v))
        scale = dh ** 0.5
        q = _rmsnorm(q, q_gamma, scale)
        k = _rmsnorm(k, k_gamma, scale)
        dots = jnp.einsum('bhid,bhjd->bhij', q, k)
        attn = jax.nn.softmax(dots, axis=-1)
        out = jnp.einsum('bhij,bhjd->bhid', attn, v)
        out = out.transpose(0, 2, 1, 3).reshape(b, s, h * dh)
        return out @ Wo

    def _L0_ffn_ref(x, Wqkv, q_scale, k_scale, Wo, ln_g, ln_b, W1, b1, W2, b2):
        import jax, jax.numpy as jnp
        import numpy as np
        DIM = 128
        DEPTH = 6
        HEADS = 16
        DIM_HEAD = 64
        WINDOW = 32
        INNER = HEADS * DIM_HEAD
        DIM_INNER = int(DIM * 4 * 2 / 3)
        QK_SCALE = 8.0

        def shift_tokens(t):
            a, s = jnp.split(t, 2, -1)
            s = jnp.pad(s, ((0, 0), (1, 0), (0, 0)))[:, :-1]
            return jnp.concatenate([a, s], -1)

        def l2norm(t):
            return t / jnp.maximum(jnp.linalg.norm(t, axis=-1, keepdims=True), 1e-12)

        def rotate_half(x):
            x1, x2 = jnp.split(x, 2, -1)
            return jnp.concatenate([-x2, x1], -1)

        def rotary_tables(n):
            half = jnp.arange(0, DIM_HEAD, 2, dtype=jnp.float32)
            inv_freq = 1.0 / 10000.0 ** (half / DIM_HEAD)
            t = jnp.arange(n, dtype=jnp.float32)
            freqs = t[:, None] * inv_freq[None, :]
            freqs = jnp.concatenate([freqs, freqs], -1)
            base_scale = (half + 0.4 * DIM_HEAD) / (1.4 * DIM_HEAD)
            power = (t - n // 2) / (WINDOW // 2)
            scale = base_scale[None, :] ** power[:, None]
            scale = jnp.concatenate([scale, scale], -1)
            return (freqs, scale)

        def local_attention(q, k, v):
            b, h, n, d = q.shape
            w = WINDOW
            nw = n // w
            bq = q.reshape(b, h, nw, w, d)
            bk = k.reshape(b, h, nw, w, d)
            bv = v.reshape(b, h, nw, w, d)

            def look(t):
                p = jnp.pad(t, ((0, 0), (0, 0), (1, 0), (0, 0), (0, 0)))
                return jnp.concatenate([p[:, :, :nw], p[:, :, 1:]], axis=3)
            bk2, bv2 = (look(bk), look(bv))
            seq = jnp.arange(n).reshape(nw, w)
            seq_p = jnp.pad(seq, ((1, 0), (0, 0)), constant_values=-1)
            jt = jnp.concatenate([seq_p[:nw], seq_p[1:]], axis=1)
            it = seq[:, :, None]
            jb = jt[:, None, :]
            mask = (it < jb) | (it > jb + w) | (jb == -1)
            sim = jnp.einsum('bhwie,bhwje->bhwij', bq, bk2) * QK_SCALE
            sim = jnp.where(mask, -jnp.finfo(sim.dtype).max, sim)
            attn = jax.nn.softmax(sim, -1)
            out = jnp.einsum('bhwij,bhwje->bhwie', attn, bv2)
            return out.reshape(b, h, n, d)

        def attn_layer(x, Wqkv, qs, ksc, Wo):
            b, n, _ = x.shape
            qkv = x @ Wqkv
            q, k, v = jnp.split(qkv, 3, -1)
            sh = lambda t: t.reshape(b, n, HEADS, DIM_HEAD).transpose(0, 2, 1, 3)
            q, k, v = (sh(q), sh(k), sh(v))
            q = l2norm(q) * qs
            k = l2norm(k) * ksc
            freqs, scale = rotary_tables(n)
            cos, sin = (jnp.cos(freqs), jnp.sin(freqs))
            q = q * cos * scale + rotate_half(q) * sin * scale
            inv = 1.0 / scale
            k = k * cos * inv + rotate_half(k) * sin * inv
            out = local_attention(q, k, v)
            out = out.transpose(0, 2, 1, 3).reshape(b, n, INNER)
            return out @ Wo

        def ffn_layer(x, g, bln, W1, b1, W2, b2):
            mu = x.mean(-1, keepdims=True)
            var = ((x - mu) ** 2).mean(-1, keepdims=True)
            xn = (x - mu) / jnp.sqrt(var + 1e-05) * g + bln
            hg = xn @ W1 + b1
            a, gate = jnp.split(hg, 2, -1)
            return a * jax.nn.gelu(gate, approximate=False) @ W2 + b2
        for i in range(DEPTH):
            x = attn_layer(shift_tokens(x), Wqkv[i], q_scale[i], k_scale[i], Wo[i]) + x
            x = ffn_layer(shift_tokens(x), ln_g[i], ln_b[i], W1[i], b1[i], W2[i], b2[i]) + x
        return x
    x = L0_attn_a_x
    x = x + _L0_attn_a_ref(_layernorm(x, axis=-1), L0_attn_a_hawk_norm_gamma, L0_attn_a_input_w, L0_attn_a_conv_w, L0_attn_a_conv_b, L0_attn_a_gates_w, L0_attn_a_gates_b, L0_attn_a_forget_base, L0_attn_a_output_w, L0_attn_a_gmlp_norm_gamma, L0_attn_a_grow_w, L0_attn_a_shrink_w)
    x = x + _L0_ffn_ref(_layernorm(x, axis=-1), L0_ffn_Wqkv, L0_ffn_q_scale, L0_ffn_k_scale, L0_ffn_Wo, L0_ffn_ln_g, L0_ffn_ln_b, L0_ffn_W1, L0_ffn_b1, L0_ffn_W2, L0_ffn_b2)
    x = x + _L0_attn_b_ref(_layernorm(x, axis=-1), L0_attn_b_ln_w, L0_attn_b_ln_b, L0_attn_b_Wq, L0_attn_b_Wkv, L0_attn_b_q_gamma, L0_attn_b_k_gamma, L0_attn_b_Wo)
    x = x + _L0_ffn_ref(_layernorm(x, axis=-1), L0_ffn_Wqkv, L0_ffn_q_scale, L0_ffn_k_scale, L0_ffn_Wo, L0_ffn_ln_g, L0_ffn_ln_b, L0_ffn_W1, L0_ffn_b1, L0_ffn_W2, L0_ffn_b2)
    return x

_drawn_inputs = setup_inputs


def setup_inputs(seed=0):
    import zlib

    import numpy as np

    out = dict(_drawn_inputs(seed))
    spreads = {'L0_attn_a_hawk_norm_gamma': (1.0, 0.2),
     'L0_attn_a_conv_b': (0.0, 0.1),
     'L0_attn_a_gates_b': (0.0, 0.393),
     'L0_attn_a_gmlp_norm_gamma': (1.0, 0.2),
     'L0_attn_b_ln_w': (1.0, 0.6),
     'L0_attn_b_ln_b': (0.0, 0.955),
     'L0_attn_b_q_gamma': (1.0, 0.6),
     'L0_attn_b_k_gamma': (1.0, 0.6),
     'L0_ffn_q_scale': (1.0, 0.6),
     'L0_ffn_k_scale': (1.0, 0.6),
     'L0_ffn_ln_g': (1.0, 0.6),
     'L0_ffn_ln_b': (0.0, 0.8),
     'L0_ffn_b1': (0.0, 0.737),
     'L0_ffn_b2': (0.0, 0.1)}
    factors = {'L0_ffn_W1': 3.054, 'L0_ffn_W2': 2.99}
    for name, (base, spread) in spreads.items():
        noise = np.random.default_rng([zlib.crc32(name.encode()), seed]).standard_normal(out[name].shape)
        drawn = base * np.exp(spread * noise) if base else spread * noise
        out[name] = jnp.asarray(drawn.astype(out[name].dtype))
    for name, factor in factors.items():
        out[name] = (out[name] * factor).astype(out[name].dtype)
    return out
```

```python
from contextlib import ExitStack

import numpy as np
import concourse.bass as bass
from concourse import mybir

ALU = mybir.AluOpType
ACT = mybir.ActivationFunctionType
AX = mybir.AxisListType
F32 = mybir.dt.float32
F32R = mybir.dt.float32r
BF16 = mybir.dt.bfloat16

P = 128
T = 2048
NT = T // P
H = 16
DH = 64
HP = H // 2
INNER = H * DH
WIN = 32
NW = P // WIN
DEPTH = 6
GT = 4
GW = GT * P
NG = T // GW
FF = 341
FCH = [(0, 128), (128, 128), (256, 85)]
NEG = -1e30


class Signal:

    def __init__(self, sem, per_group):
        self.sem, self.per_group = sem, per_group

    def start(self, eng):
        eng.sem_inc(self.sem, self.per_group)

    def wait(self, eng, turn, n):
        eng.wait_ge(self.sem, turn * self.per_group + (self.per_group + n + 1))


class Settle:

    def __init__(self, sem):
        self.sem = sem

    def __call__(self, eng):
        eng.sem_inc(self.sem, 1)


class Chain:

    def __init__(self, sem):
        self.sem, self.n = sem, 0

    def add(self, ins):
        self.n += 1
        ins.then_inc(self.sem, 1)

    def wait(self, eng):
        eng.wait_ge(self.sem, self.n)


def build_program(nc, d, out):
    ctx = ExitStack()
    with ctx:
        semaphores = {}

        def sem(name):
            if name not in semaphores:
                semaphores[name] = ctx.enter_context(nc.semaphore(name))
            return semaphores[name]

        stack_chain = Chain(sem("f_dve"))
        half_set = sem("half_set")
        settle = Settle(sem("settled"))

        def keep(name, shape, dt=F32):
            return ctx.enter_context(nc.sbuf_tensor(name, shape, dt))

        ps = ctx.enter_context(nc.psum_tensor("ps", [P, 8, 512], F32))
        xtok = keep("xtok", [P, NT, P])
        ident = keep("ident", [P, P])
        identb = keep("identb", [P, P], BF16)
        minus_half = keep("minus_half", [P, 64])
        small = keep("small", [P, 8, 64])

        loads_done = sem("loads_done")
        n_loads = 2
        engines = {"sync": [], "scalar": [], "vector": [], "gpsimd": [], "tensor": []}
        x_ready = [sem(f"x_ready{i}") for i in range(5)]

        def load_common(sp):
            sp.dma_start(xtok[:], d["x"].rearrange("(t p) c -> p t c", p=P)).then_inc(loads_done, 16)
            sp.dma_start(ident[:], d["ident"]).then_inc(loads_done, 16)
        engines["sync"].append(load_common)

        def set_half(pool):
            pool.memset(minus_half[:], -0.5).then_inc(half_set, 1)
        engines["gpsimd"].append(set_half)

        def add_phase(**programs):
            for name, program in programs.items():
                engines[name].append(program)

        build_recurrent_block(nc, ps, xtok, ident, minus_half, small, d, sem, add_phase,
                              (loads_done, 16 * n_loads), half_set, x_ready[1])
        build_window_stack(nc, 0, stack_chain, settle, ps, xtok, ident, identb, minus_half, small, d, sem, add_phase,
                           x_ready[1], x_ready[2])
        build_full_attention(nc, settle, ps, xtok, ident, minus_half, small, d, sem, add_phase,
                             x_ready[2], x_ready[3])
        build_window_stack(nc, 1, stack_chain, settle, ps, xtok, ident, identb, minus_half, small, d, sem, add_phase,
                           x_ready[3], x_ready[4])

        out_stored = sem("out_stored")

        def store(sp):
            sp.wait_ge(x_ready[4], 1)
            sp.dma_start(out.rearrange("(t p) c -> p t c", p=P), xtok[:]).then_inc(out_stored, 16)
            sp.wait_ge(out_stored, 16)
        engines["sync"].append(store)

        block = ctx.enter_context(nc.Block())

        @block.sync
        def _(eng):
            for program in engines["sync"]:
                program(eng)

        @block.scalar
        def _(eng):
            for program in engines["scalar"]:
                program(eng)

        @block.vector
        def _(eng):
            for program in engines["vector"]:
                program(eng)

        @block.gpsimd
        def _(eng):
            for program in engines["gpsimd"]:
                program(eng)

        @block.tensor
        def _(eng):
            for program in engines["tensor"]:
                program(eng)


def per_token(ap, n=P):
    return ap.unsqueeze(2).broadcast_to([P, NT, n])


def layernorm_vector(v, chain, variance_ready, rstd_ready, src, dst, square, small, nth=1, eps=1e-5):
    mean, var, rstd = small[:, 0, 0:NT], small[:, 1, 0:NT], small[:, 2, 0:NT]
    chain.add(v.tensor_reduce(mean, src, axis=AX.X, op=ALU.add))
    chain.wait(v)
    chain.add(v.tensor_scalar(mean, mean, 1.0 / P, None, ALU.mult))
    chain.wait(v)
    chain.add(v.tensor_tensor(dst, src, per_token(mean), ALU.subtract))
    chain.wait(v)
    chain.add(v.tensor_tensor(square, dst, dst, ALU.mult))
    chain.wait(v)
    chain.add(v.tensor_reduce(var, square, axis=AX.X, op=ALU.add))
    chain.wait(v)
    v.tensor_scalar(var, var, 1.0 / P, eps, ALU.mult, ALU.add).then_inc(variance_ready, 1)
    v.wait_ge(rstd_ready, nth)
    chain.add(v.tensor_tensor(dst, dst, per_token(rstd), ALU.mult))
    chain.wait(v)


def layernorm_gpsimd(pool, variance_ready, rstd_ready, small, minus_half, nth=1):
    pool.wait_ge(variance_ready, nth)
    pool.tensor_tensor(small[:, 2, 0:NT], small[:, 1, 0:NT], minus_half[:, 0:NT], ALU.pow) \
        .then_inc(rstd_ready, 1)


def transpose_tiles(pe, ps, src, ident, banks, ready):
    for b, bank in enumerate(banks):
        for k in range(4):
            last = pe.transpose(ps[:, bank, k * P:(k + 1) * P], src(4 * b + k), ident[:])
        last.then_inc(ready, 1)


def build_recurrent_block(nc, ps, xtok, ident, minus_half, small, d, sem, add_phase, loaded, half_set,
                          x_next):
    with ExitStack() as mem:
        def sb(name, shape, dt=F32):
            return mem.enter_context(nc.sbuf_tensor("a_" + name, shape, dt))

        atok = sb("atok", [P, NT, P])
        ntok = sb("ntok", [P, NT, P])
        nT = sb("nT", [P, T])
        square = sb("square", [P, NT, P])
        gate = sb("gate", [P, T])
        z = sb("z", [P, 3 + T])
        zc = sb("zc", [P, T])
        forget = sb("forget", [P, T])
        insig = sb("insig", [P, T])
        beta = sb("beta", [P, T])
        hid = sb("hid", [P, T])
        yT = sb("yT", [P, T])
        w_in = sb("w_in", [P, 256])
        w_gates = sb("w_gates", [P, 256])
        w_out = sb("w_out", [P, P])
        w_grow = sb("w_grow", [P, 512])
        w_shrink = sb("w_shrink", [P, 2, P])
        cols = sb("cols", [P, 16])
        cw = sb("cw", [P, 4])
        tiny = sb("tiny", [P, 12])
        G1, G2, CB, FB, BF, BI = (cols[:, i:i + 1] for i in range(6))

    w_loaded = sem("a_w_loaded")
    chain = Chain(sem("a_dve"))
    var1, rstd1, var2, rstd2, var3, rstd3 = (sem(f"a_norm{i}") for i in range(6))
    norm_ready = [sem(f"a_norm_ready{i}") for i in range(2)]
    tr = [sem(f"a_transposed{i}") for i in range(4)]
    nT_ready = [sem(f"a_nT_ready{i}") for i in range(2)]
    cols_scaled = sem("a_cols_scaled")
    u_ps, gate_sb, z_sb = sem("a_u_ps"), sem("a_gate_sb"), sem("a_z_sb")
    conv_done, fg_ps, sig_sb = sem("a_conv_done"), sem("a_fg_ps"), sem("a_sig_sb")
    softplus_done, alpha_sb, one_minus, beta_sb = (sem(f"a_{n}") for n in
                                                   ("softplus", "alpha", "one_minus", "beta_sb"))
    zpad, h_done, y_ps, y_sb, back_used = (sem(f"a_{n}") for n in ("zpad", "h", "y_ps", "y_sb", "back"))
    absx, expx = sem("a_absx"), sem("a_expx")
    m_ps, m_gelu, m_u, m_out, m_sb, m_used = (sem(f"a_m_{n}") for n in
                                              ("ps", "gelu", "u", "out", "sb", "used"))

    def sync(sp):
        n = lambda ap: ap.rearrange("(p a) -> p a", a=1)
        for dst, src in ((w_in[:], d["input_wT"]), (w_gates[:], d["gates_wT"]), (w_out[:], d["output_wT"]),
                         (w_grow[:], d["grow_wT"]),
                         (w_shrink[:], d["shrink_wT"].rearrange("(c p) n -> p c n", p=P)),
                         (cw[:], d["conv_w"]), (G1, n(d["hawk_gamma"])), (G2, n(d["gmlp_gamma"])),
                         (CB, n(d["conv_b"])), (FB, n(d["forget_base"])),
                         (BF, n(d["gates_b"][0:P])), (BI, n(d["gates_b"][P:2 * P]))):
            sp.dma_start(dst, src).then_inc(w_loaded, 16)
    n_w = 12

    def rms_vector(v, ss_ready, rinv_ready, norm_done):
        chain.add(v.tensor_tensor(square[:], atok[:], atok[:], ALU.mult))
        chain.wait(v)
        v.tensor_reduce(small[:, 1, 0:NT], square[:], axis=AX.X, op=ALU.add).then_inc(ss_ready, 1)
        v.wait_ge(rinv_ready, 1)
        v.tensor_tensor(ntok[:], atok[:], per_token(small[:, 2, 0:NT]), ALU.mult).then_inc(norm_done, 1)

    def vector(v):
        v.wait_ge(loaded[0], loaded[1])
        layernorm_vector(v, chain, var1, rstd1, xtok[:], atok[:], square[:], small)
        rms_vector(v, var2, rstd2, norm_ready[0])
        v.wait_ge(w_loaded, 16 * n_w)
        v.tensor_scalar(cols[:, 0:2], cols[:, 0:2], float(np.sqrt(P)), None, ALU.mult).then_inc(cols_scaled, 1)
        v.memset(z[:, 0:3], 0.0).then_inc(zpad, 1)
        c = lambda i: tiny[:, i:i + 1]
        chain.add(v.tensor_scalar(c(0), FB, -1.0, None, ALU.mult))
        chain.wait(v)
        v.tensor_tensor(c(1), c(0), FB, ALU.min).then_inc(absx, 1)
        v.wait_ge(expx, 1)
        chain.add(v.tensor_scalar(c(3), c(2), 2.0, None, ALU.add))
        chain.wait(v)
        chain.add(v.reciprocal(c(4), c(3)))
        chain.wait(v)
        chain.add(v.tensor_tensor(c(5), c(2), c(4), ALU.mult))
        chain.wait(v)
        chain.add(v.tensor_tensor(c(6), c(5), c(5), ALU.mult))
        chain.add(v.memset(c(7), 1.0 / 17))
        chain.wait(v)
        for k in range(15, 0, -2):
            chain.add(v.tensor_scalar(c(7), c(7), c(6), 1.0 / k, ALU.mult, ALU.add))
            chain.wait(v)
        chain.add(v.scalar_tensor_tensor(c(8), c(7), 2.0, c(5), ALU.mult, ALU.mult))
        chain.add(v.tensor_scalar(c(9), FB, 0.0, None, ALU.max))
        chain.wait(v)
        chain.add(v.tensor_tensor(c(10), c(8), c(9), ALU.add))
        chain.wait(v)
        v.tensor_scalar(c(11), c(10), -8.0, None, ALU.mult).then_inc(softplus_done, 1)
        v.wait_ge(z_sb, 4)
        chain.add(v.tensor_scalar(zc[:], z[:, 0:T], cw[:, 0:1], CB, ALU.mult, ALU.add))
        chain.wait(v)
        for k in range(1, 4):
            ins = v.scalar_tensor_tensor(zc[:], z[:, k:k + T], cw[:, k:k + 1], zc[:], ALU.mult, ALU.add)
            if k < 3:
                chain.add(ins)
                chain.wait(v)
            else:
                ins.then_inc(conv_done, 1)
        v.wait_ge(alpha_sb, 1)
        chain.add(v.tensor_tensor(beta[:], forget[:], forget[:], ALU.mult))
        chain.wait(v)
        v.tensor_scalar(beta[:], beta[:], -1.0, 1.0, ALU.mult, ALU.add).then_inc(one_minus, 1)
        v.wait_ge(beta_sb, 1)
        chain.add(v.tensor_tensor(beta[:], beta[:], insig[:], ALU.mult))
        chain.wait(v)
        chain.add(v.tensor_tensor(beta[:], beta[:], zc[:], ALU.mult))
        chain.wait(v)
        chain.add(v.tensor_tensor_scan(hid[:], forget[:], beta[:], 0.0, ALU.mult, ALU.add))
        chain.wait(v)
        v.wait_ge(gate_sb, 4)
        v.tensor_tensor(hid[:], hid[:], gate[:], ALU.mult).then_inc(h_done, 1)
        for b in range(4):
            v.wait_ge(tr[1], b + 1)
            ins = v.tensor_tensor(atok[:, 4 * b:4 * b + 4, :].rearrange("p a c -> p (a c)"),
                                  atok[:, 4 * b:4 * b + 4, :].rearrange("p a c -> p (a c)"),
                                  ps[:, 4 + b, :], ALU.add)
            chain.add(ins)
        chain.wait(v)
        rms_vector(v, var3, rstd3, norm_ready[1])
        for q in range(4):
            for c_ in range(2):
                v.wait_ge(m_gelu, 2 * q + c_ + 1)
                v.tensor_tensor(forget[:, 1024 * (q % 2) + 512 * c_:1024 * (q % 2) + 512 * c_ + 512],
                                beta[:, 512 * c_:512 * c_ + 512], ps[:, 2 * c_ + 1, :], ALU.mult) \
                    .then_inc(m_u, 1)
        for b in range(4):
            v.wait_ge(tr[3], b + 1)
            a4 = atok[:, 4 * b:4 * b + 4, :].rearrange("p a c -> p (a c)")
            x4 = xtok[:, 4 * b:4 * b + 4, :].rearrange("p a c -> p (a c)")
            chain.add(v.tensor_tensor(a4, a4, ps[:, 4 + b, :], ALU.add))
            chain.wait(v)
            chain.add(v.tensor_tensor(x4, x4, a4, ALU.add))
        chain.wait(v)
        v.sem_inc(x_next, 1)

    def gpsimd(pool):
        pool.wait_ge(half_set, 1)
        layernorm_gpsimd(pool, var1, rstd1, small, minus_half)
        layernorm_gpsimd(pool, var2, rstd2, small, minus_half)
        layernorm_gpsimd(pool, var3, rstd3, small, minus_half)

    def tensor(pe):
        pe.wait_ge(norm_ready[0], 1)
        transpose_tiles(pe, ps, lambda t: ntok[:, t, :], ident, range(4), tr[0])
        pe.wait_ge(w_loaded, 16 * n_w)
        pe.wait_ge(nT_ready[0], 4)
        for m in range(2):
            for q in range(4):
                pe.matmul(ps[:, 4 * m + q, :], w_in[:, m * P:(m + 1) * P], nT[:, 512 * q:512 * q + 512],
                          start=True, stop=True).then_inc(u_ps, 1)
        pe.wait_ge(conv_done, 1)
        pe.wait_ge(gate_sb, 4)
        for m in range(2):
            for q in range(4):
                pe.matmul(ps[:, 4 * m + q, :], w_gates[:, m * P:(m + 1) * P], zc[:, 512 * q:512 * q + 512],
                          start=True, stop=True).then_inc(fg_ps, 1)
        pe.wait_ge(h_done, 1)
        for q in range(4):
            pe.matmul(ps[:, q, :], w_out[:], hid[:, 512 * q:512 * q + 512], start=True, stop=True) \
                .then_inc(y_ps, 1)
        pe.wait_ge(y_sb, 4)
        transpose_tiles(pe, ps, lambda t: yT[:, t * P:(t + 1) * P], ident, range(4, 8), tr[1])
        pe.wait_ge(norm_ready[1], 1)
        transpose_tiles(pe, ps, lambda t: ntok[:, t, :], ident, range(4), tr[2])
        pe.wait_ge(nT_ready[1], 4)
        for q in range(4):
            for c in range(2):
                if q:
                    pe.wait_ge(m_u, 2 * (q - 1) + c + 1)
                pe.matmul(ps[:, 2 * c, :], w_grow[:, c * P:(c + 1) * P], nT[:, 512 * q:512 * q + 512],
                          start=True, stop=True)
                pe.matmul(ps[:, 2 * c + 1, :], w_grow[:, 256 + c * P:256 + (c + 1) * P],
                          nT[:, 512 * q:512 * q + 512], start=True, stop=True).then_inc(m_ps, 1)
            for c in range(2):
                pe.wait_ge(m_u, 2 * q + c + 1)
                last = pe.matmul(ps[:, 4 + q, :], w_shrink[:, c, :],
                                 forget[:, 1024 * (q % 2) + 512 * c:1024 * (q % 2) + 512 * c + 512],
                                 start=(c == 0), stop=(c == 1))
            last.then_inc(m_out, 1)
        pe.wait_ge(m_sb, 4)
        transpose_tiles(pe, ps, lambda t: yT[:, t * P:(t + 1) * P], ident, range(4, 8), tr[3])

    def scalar(act):
        act.wait_ge(cols_scaled, 1)
        for b in range(4):
            act.wait_ge(tr[0], b + 1)
            act.activation(nT[:, 512 * b:512 * b + 512], ps[:, b, :], ACT.Copy, scale=G1).then_inc(nT_ready[0], 1)
        act.wait_ge(absx, 1)
        act.activation(tiny[:, 2:3], tiny[:, 1:2], ACT.Exp).then_inc(expx, 1)
        for q in range(4):
            act.wait_ge(u_ps, 4 + q + 1)
            act.activation(z[:, 3 + 512 * q:3 + 512 * q + 512], ps[:, 4 + q, :], ACT.Copy).then_inc(z_sb, 1)
        for q in range(4):
            act.activation(gate[:, 512 * q:512 * q + 512], ps[:, q, :], ACT.Gelu).then_inc(gate_sb, 1)
        for m, dst, bias in ((0, forget, BF), (1, insig, BI)):
            for q in range(4):
                act.wait_ge(fg_ps, 4 * m + q + 1)
                act.activation(dst[:, 512 * q:512 * q + 512], ps[:, 4 * m + q, :], ACT.Sigmoid, bias=bias) \
                    .then_inc(sig_sb, 1)
        act.wait_ge(sig_sb, 8)
        act.wait_ge(softplus_done, 1)
        act.activation(forget[:], forget[:], ACT.Exp, scale=tiny[:, 11:12]).then_inc(alpha_sb, 1)
        act.wait_ge(one_minus, 1)
        act.activation(beta[:], beta[:], ACT.Sqrt, bias=eps6[:]).then_inc(beta_sb, 1)
        for q in range(4):
            act.wait_ge(y_ps, q + 1)
            act.activation(yT[:, 512 * q:512 * q + 512], ps[:, q, :], ACT.Copy).then_inc(y_sb, 1)
        for b in range(4):
            act.wait_ge(tr[2], b + 1)
            act.activation(nT[:, 512 * b:512 * b + 512], ps[:, b, :], ACT.Copy, scale=G2).then_inc(nT_ready[1], 1)
        for q in range(4):
            for c in range(2):
                act.wait_ge(m_ps, 2 * q + c + 1)
                if q:
                    act.wait_ge(m_u, 2 * (q - 1) + c + 1)
                act.activation(beta[:, 512 * c:512 * c + 512], ps[:, 2 * c, :], ACT.Gelu).then_inc(m_gelu, 1)
            act.wait_ge(m_out, q + 1)
            act.activation(yT[:, 512 * q:512 * q + 512], ps[:, 4 + q, :], ACT.Copy).then_inc(m_sb, 1)

    eps6 = small[:, 7, 0:1]
    eps_set = sem("a_eps_set")

    def gpsimd_eps(pool):
        pool.memset(small[:, 7, 0:1], 1e-6).then_inc(eps_set, 1)

    def scalar_all(act):
        act.wait_ge(eps_set, 1)
        scalar(act)

    add_phase(gpsimd=gpsimd_eps)
    add_phase(sync=sync, vector=vector, gpsimd=gpsimd, tensor=tensor, scalar=scalar_all)


WIDE_SLOTS = 3
NARROW_BANK = 6


def psum_orders():
    wide = [("q", 0), ("k", 0), ("v", 0)]
    narrow = []
    for j in range(GT):
        if j + 1 < GT:
            wide += [("q", j + 1), ("k", j + 1), ("v", j + 1)]
        narrow += [("qT", 2 * j), ("qT", 2 * j + 1), ("kT", 2 * j), ("kT", 2 * j + 1)]
        wide += [("s", j)]
        if j:
            wide += [("ctx", j - 1)]
            narrow += [("pT", 2 * j - 2), ("pT", 2 * j - 1), ("cT", 2 * j - 2), ("cT", 2 * j - 1), ("o", j - 1)]
    j = GT
    wide += [("ctx", j - 1)]
    narrow += [("pT", 2 * j - 2), ("pT", 2 * j - 1), ("cT", 2 * j - 2), ("cT", 2 * j - 1), ("o", j - 1)]
    narrow += [("ln", 0), ("xn", 0)]
    wide += [("ff", 0), ("ff", 1), ("ff", 2), ("y", 0)]
    assert len(wide) % WIDE_SLOTS == 0 and len(narrow) % 2 == 0
    return wide, narrow


def build_window_stack(nc, nth, chain, settle, ps, xtok, ident, identb, minus_half, small, d, sem, add_phase,
                       x_ready, x_next):
    wide, narrow = psum_orders()
    with ExitStack() as mem:
        def sb(name, shape, dt=F32):
            return mem.enter_context(nc.sbuf_tensor(f"f{nth}_" + name, shape, dt))

        hT = sb("hT", [P, T])
        wqkv = sb("wqkv", [P, 3 * INNER])
        wo = sb("wo", [P, HP, P])
        w1 = sb("w1", [P, 2 * FF])
        w2 = sb("w2", [P, 3, P])
        tabs = sb("tabs", [P, NT, 2, 2, DH])
        masks = sb("masks", [P, NG, 512], BF16)
        mask32 = sb("mask32", [P, 2, 2 * WIN])
        decay = sb("decay", [P, 1])
        gains = sb("gains", [P, DEPTH, 2, DH])
        vecs = sb("vecs", [P, DEPTH, 9])
        xs = sb("xs", [P, GW + 1])
        xf = sb("xf", [P, GW + 1])
        tab = [sb(f"tab{i}", [P, 2, 2, DH]) for i in range(2)]
        prod = [sb(f"prod{i}", [P, H, 2, DH]) for i in range(2)]
        sq = [sb(f"sq{i}", [P, H, DH]) for i in range(2)]
        stat = sb("stat", [P, 2, 2, H])
        qk = [[sb(f"qk{i}{u}", [P, H, DH]) for u in range(2)] for i in range(2)]
        qT = sb("qT", [P, HP, P])
        kT = [sb(f"kT{i}", [P, HP, 2, WIN + P]) for i in range(2)]
        vtok = [sb(f"vtok{i}", [P, 2, 512]) for i in range(2)]
        vbd = [sb(f"vbd{i}", [P, NW, 2, 512]) for i in range(2)]
        pr = [sb(f"pr{i}", [P, H, 2 * WIN]) for i in range(2)]
        mx = sb("mx", [P, H])
        rs = [sb(f"rs{i}", [P, H]) for i in range(2)]
        pT = sb("pT", [P, HP, P])
        cn = sb("cn", [P, INNER])
        cT = sb("cT", [P, HP, P])
        bn = sb("bn", [P, GT, 6])
        mv = sb("mv", [P, GT, 2])
        rstd = sb("rstd", [P, GT])
        xn = sb("xn", [P, GT, P])
        xnT = sb("xnT", [P, GW])
        zero = sb("zero", [P, 1])
        gl = sb("gl", [P, 2, GW])
        uT = sb("uT", [P, 3, GW])
        ntok = qk[0][0][:].rearrange("p a b -> p (a b)")
        lnsq = prod[0][:].rearrange("p a b c -> p (a b c)").rearrange("p (t c) -> p t c", c=P)
        lnx = prod[1][:].rearrange("p a b c -> p (a b c)").rearrange("p (t c) -> p t c", c=P)

    def signal(name, per_group):
        return Signal(sem(f"f_{name}"), per_group)

    proj = signal("proj", 3 * GT)
    qkT_ps = signal("qkT_ps", 4 * GT)
    s_ps = signal("s_ps", GT)
    pT_ps = signal("pT_ps", 2 * GT)
    ctx_ps = signal("ctx_ps", GT)
    cT_ps = signal("cT_ps", 2 * GT)
    o_ps = signal("o_ps", GT)
    ln_ps, xn_ps, ff_ps, y_ps = signal("ln_ps", 1), signal("xn_ps", 1), signal("ff_ps", 3), signal("y_ps", 1)
    squared = signal("squared", 2 * GT)
    v_sb = signal("v_sb", GT)
    qkT_sb = signal("qkT_sb", 4 * GT)
    exp_sb = signal("exp_sb", GT)
    pT_sb = signal("pT_sb", 2 * GT)
    cT_sb = signal("cT_sb", 2 * GT)
    xnT_sb, gelu_sb = signal("xnT_sb", 1), signal("gelu_sb", 3)
    xs_sb, xf_sb = signal("xs_sb", 1), signal("xf_sb", 1)
    xs_moved, xf_moved = signal("xs_moved", 1), signal("xf_moved", 1)
    prod_sb = signal("prod_sb", 2 * GT)
    sums = signal("sums", 2 * GT)
    normed = signal("normed", 2 * GT)
    maxed = signal("maxed", GT)
    shifted = signal("shifted", GT)
    summed = signal("summed", GT)
    inverted = signal("inverted", GT)
    ctx_sb = signal("ctx_sb", GT)
    x1 = signal("x1", GT)
    bn_done, mv_done, xn_sb = signal("bn_done", 1), signal("mv_done", 1), signal("xn_sb", 1)
    u_sb, x2 = signal("u_sb", 3), signal("x2", 1)
    tab_sb = signal("tab_sb", GT)
    clamped, rinv = signal("clamped", 2 * GT), signal("rinv", 2 * GT)
    rotated = signal("rotated", 2 * GT)
    k_prev = signal("k_prev", GT)
    rstd_a, rstd_sb = signal("rstd_a", 1), signal("rstd_sb", 1)
    carry0 = sem(f"f_carry0")
    consts = sem(f"f_consts")
    wqkv_ld, wo_ld, w1_ld, w2_ld = (sem(f"f_{n}") for n in ("wqkv_ld", "wo_ld", "w1_ld", "w2_ld"))
    v_keys = [sem(f"f_v_keys{i}") for i in range(2)]
    zeroed, var0, rstd0, n0, t0, h0, back_ps = (sem(f"f_{n}") for n in
                                               ("zeroed", "var0", "rstd0", "n0", "t0", "h0", "back"))
    V_DMAS = 10
    base = nth * DEPTH * NG

    released = {
        "q": lambda e, t, j: prod_sb.wait(e, t, 2 * j),
        "k": lambda e, t, j: prod_sb.wait(e, t, 2 * j + 1),
        "v": lambda e, t, j: v_sb.wait(e, t, j),
        "s": lambda e, t, j: shifted.wait(e, t, j),
        "ctx": lambda e, t, j: ctx_sb.wait(e, t, j),
        "ff": lambda e, t, j: u_sb.wait(e, t, j),
        "y": lambda e, t, j: x2.wait(e, t, j),
        "qT": lambda e, t, j: qkT_sb.wait(e, t, 2 * (j // 2) * 2 + j % 2),
        "kT": lambda e, t, j: qkT_sb.wait(e, t, 2 * (j // 2) * 2 + 2 + j % 2),
        "pT": lambda e, t, j: pT_sb.wait(e, t, j),
        "cT": lambda e, t, j: cT_sb.wait(e, t, j),
        "o": lambda e, t, j: x1.wait(e, t, j),
        "ln": lambda e, t, j: xn_sb.wait(e, t, j),
        "xn": lambda e, t, j: xnT_sb.wait(e, t, j),
    }
    per_turn = {"q": GT, "k": GT, "v": GT, "s": GT, "ctx": GT, "ff": 3, "y": 1, "qT": 2 * GT, "kT": 2 * GT,
                "pT": 2 * GT, "cT": 2 * GT, "o": GT, "ln": 1, "xn": 1}

    def wide_slot(use):
        i = wide.index(use)
        b = 2 * (i % WIDE_SLOTS)
        return ps[:, b:b + 2, :].rearrange("p b n -> p (b n)")

    def narrow_bank(use):
        return ps[:, NARROW_BANK + narrow.index(use) % 2, :]

    def wait_room(pe, turn, use):
        order, step = (wide, WIDE_SLOTS) if use in wide else (narrow, 2)
        i = order.index(use) - step
        if i >= 0:
            released[order[i][0]](pe, turn, order[i][1])
        else:
            what, j = order[i % len(order)]
            if what in ("q", "k", "v", "s", "ctx", "o") or what in per_turn:
                released[what](pe, turn - 1, j)

    def sync(sp):
        if nth == 0:
            for s in v_keys:
                sp.sem_inc(s, 1)
        sp.wait_ge(x_ready, 1)
        n = 0
        for dst, src in ((tabs[:], d["tabs"]), (mask32[:], d["masks"]), (decay[:], d["decay"])):
            sp.dma_start(dst, src).then_inc(consts, 16)
            n += 1
        for u, name in enumerate(("q_scale", "k_scale")):
            sp.dma_start(gains[:, :, u, :], d[name].unsqueeze(0).broadcast_to([P, DEPTH, DH])) \
                .then_inc(consts, 16)
            n += 1
        for c, name in enumerate(("ln_g", "ln_b", "b2")):
            sp.dma_start(vecs[:, :, c], d[name].rearrange("l p -> p l"),
                         allow_slow_non_contiguous=True).then_inc(consts, 16)
            n += 1
        for half in range(2):
            for c, (o, m) in enumerate(FCH):
                sp.dma_start(vecs[0:m, :, 3 + 3 * half + c],
                             d["b1"][:, half * FF + o:half * FF + o + m].rearrange("l p -> p l"),
                             allow_slow_non_contiguous=True) \
                    .then_inc(consts, 16)
                n += 1
        assert n == N_CONSTS
        with sp.Fori(0, DEPTH) as layer:
            first = base + layer * NG
            proj.wait(sp, first, -1)
            settle(sp)
            sp.dma_start(wqkv[:], d["Wqkv"][layer]).then_inc(wqkv_ld, 16)
            o_ps.wait(sp, first, -1)
            settle(sp)
            sp.dma_start(wo[:], d["Wo"][layer].rearrange("(c p) n -> p c n", p=P)).then_inc(wo_ld, 16)
            ff_ps.wait(sp, first, -1)
            settle(sp)
            sp.dma_start(w1[:], d["W1"][layer]).then_inc(w1_ld, 16)
            y_ps.wait(sp, first, -1)
            settle(sp)
            for c, (o, m) in enumerate(FCH):
                sp.dma_start(w2[0:m, c, :], d["W2"][layer][o:o + m, :]).then_inc(w2_ld, 16)
            with sp.Fori(0, NG) as g:
                turn = base + layer * NG + g
                for j in range(GT):
                    a, b = j % 2, 1 - j % 2
                    v_sb.wait(sp, turn, j)
                    settle(sp)
                    ctx_ps.wait(sp, turn, j - 2)
                    settle(sp)
                    for h2 in range(2):
                        lo = DH * h2
                        sp.dma_start(vbd[a][lo:lo + WIN, 0, h2, :], vtok[b][P - WIN:P, h2, :]) \
                            .then_inc(v_keys[a], 16)
                        sp.dma_start(vbd[a][lo + WIN:lo + DH, 0, h2, :], vtok[a][0:WIN, h2, :]) \
                            .then_inc(v_keys[a], 16)
                        for w in range(1, NW):
                            sp.dma_start(vbd[a][lo:lo + DH, w, h2, :],
                                         vtok[a][WIN * (w - 1):WIN * (w + 1), h2, :]) \
                                .then_inc(v_keys[a], 16)

    def v_keys_wait(eng, turn, j):
        eng.wait_ge(v_keys[j % 2], turn * (16 * V_DMAS * GT // 2) + (16 * V_DMAS * (j // 2 + 1) + 1))

    def tensor(pe):
        if nth == 0:
            for s in (proj, qkT_ps, s_ps, pT_ps, ctx_ps, cT_ps, o_ps, ln_ps, xn_ps, ff_ps, y_ps):
                s.start(pe)
        pe.wait_ge(n0, nth + 1)
        transpose_tiles(pe, ps, lambda t: lnx[:, t, :], ident, range(4), t0)
        pe.wait_ge(consts, 16 * N_CONSTS * (nth + 1))
        pe.wait_ge(h0, 4 * nth + 4)
        pe.wait_ge(zeroed, nth + 1)
        with pe.Fori(0, DEPTH) as layer:
            loaded = nth * DEPTH + layer + 1
            pe.wait_ge(wqkv_ld, loaded * 16)
            pe.wait_ge(wo_ld, loaded * 16)
            pe.wait_ge(w1_ld, loaded * 16)
            pe.wait_ge(w2_ld, loaded * 48)
            settle(pe)
            with pe.Fori(0, NG) as g:
                tensor_turn(pe, base + layer * NG + g, g)
        x2.wait(pe, base + DEPTH * NG - 1, 0)
        transpose_tiles(pe, ps, lambda t: hT[:, t * P:(t + 1) * P], ident, range(4), back_ps)

    def project(pe, turn, j):
        for u, what in enumerate("qkv"):
            wait_room(pe, turn, (what, j))
            dst = wide_slot((what, j))
            for half in range(2):
                if what == "v":
                    w = wqkv[:, 2 * INNER:].rearrange("p (a h c) -> p h a c", h=2, c=DH)[:, half]
                else:
                    w = wqkv[:, u * INNER + 512 * half:u * INNER + 512 * half + 512]
                last = pe.matmul(dst[:, 512 * half:512 * half + 512], xs[:, j * P:(j + 1) * P], w,
                                 start=True, stop=True)
            last.then_inc(proj.sem, 1)

    def transpose_qk(pe, turn, j):
        for u, what in enumerate(("qT", "kT")):
            normed.wait(pe, turn, 2 * j + u)
            for half in range(2):
                use = (what, 2 * j + half)
                wait_room(pe, turn, use)
                for c in range(4):
                    hp = 4 * half + c
                    src = qk[j % 2][u][:, 2 * hp:2 * hp + 2, :].rearrange("p a b -> p (a b)")
                    last = pe.transpose(narrow_bank(use)[:, c * P:(c + 1) * P], src, ident[:])
                last.then_inc(qkT_ps.sem, 1)

    def scores(pe, turn, g, j):
        wait_room(pe, turn, ("s", j))
        dst = wide_slot(("s", j))
        qkT_sb.wait(pe, turn, 4 * j + 3)
        k_prev.wait(pe, turn, j)
        for half in range(2):
            bank = dst[:, 512 * half:512 * half + 512]
            mask = masks[:, g, :] if j == 0 else masks[:, 1, :]
            pe.matmul(bank, identb[:], mask, start=True, stop=False, skip_group_check=True)
            for c in range(4):
                hp = 4 * half + c
                for w in range(NW):
                    last = pe.matmul(bank[WIN * w:WIN * (w + 1), c * P:(c + 1) * P],
                                     qT[:, hp, WIN * w:WIN * (w + 1)],
                                     kT[j % 2][:, hp, :, WIN * w:WIN * (w + 2)],
                                     start=False, stop=True, skip_group_check=True)
        last.then_inc(s_ps.sem, 1)

    def attend(pe, turn, j):
        exp_sb.wait(pe, turn, j)
        for half in range(2):
            use = ("pT", 2 * j + half)
            wait_room(pe, turn, use)
            for c in range(4):
                hp = 4 * half + c
                src = pr[j % 2][:, 2 * hp:2 * hp + 2, :].rearrange("p a b -> p (a b)")
                last = pe.transpose(narrow_bank(use)[:, c * P:(c + 1) * P], src, ident[:])
            last.then_inc(pT_ps.sem, 1)
        wait_room(pe, turn, ("ctx", j))
        dst = wide_slot(("ctx", j))
        v_keys_wait(pe, turn, j)
        for hp in range(HP):
            if hp % 4 == 0:
                pT_sb.wait(pe, turn, 2 * j + hp // 4)
            for w in range(NW):
                last = pe.matmul(dst[WIN * w:WIN * (w + 1), hp * P:(hp + 1) * P],
                                 pT[:, hp, WIN * w:WIN * (w + 1)],
                                 vbd[j % 2][:, w, :, hp * DH:(hp + 1) * DH],
                                 start=True, stop=True)
        last.then_inc(ctx_ps.sem, 1)
        ctx_sb.wait(pe, turn, j)
        for half in range(2):
            use = ("cT", 2 * j + half)
            wait_room(pe, turn, use)
            for c in range(4):
                hp = 4 * half + c
                last = pe.transpose(narrow_bank(use)[:, c * P:(c + 1) * P], cn[:, hp * P:(hp + 1) * P], ident[:])
            last.then_inc(cT_ps.sem, 1)
        wait_room(pe, turn, ("o", j))
        for hp in range(HP):
            if hp % 4 == 0:
                cT_sb.wait(pe, turn, 2 * j + hp // 4)
            last = pe.matmul(narrow_bank(("o", j))[:, 0:P], wo[:, hp, :], cT[:, hp, :],
                             start=(hp == 0), stop=(hp == HP - 1))
        last.then_inc(o_ps.sem, 1)

    def tensor_turn(pe, turn, g):
        xs_sb.wait(pe, turn, 0)
        project(pe, turn, 0)
        for j in range(GT):
            if j + 1 < GT:
                project(pe, turn, j + 1)
            transpose_qk(pe, turn, j)
            scores(pe, turn, g, j)
            if j:
                attend(pe, turn, j - 1)
        attend(pe, turn, GT - 1)
        xf_sb.wait(pe, turn, 0)
        wait_room(pe, turn, ("ln", 0))
        for j in range(GT):
            last = pe.transpose(narrow_bank(("ln", 0))[:, j * P:(j + 1) * P], xf[:, j * P:(j + 1) * P], ident[:])
        last.then_inc(ln_ps.sem, 1)
        xn_sb.wait(pe, turn, 0)
        wait_room(pe, turn, ("xn", 0))
        for j in range(GT):
            last = pe.transpose(narrow_bank(("xn", 0))[:, j * P:(j + 1) * P], xn[:, j, :], ident[:])
        last.then_inc(xn_ps.sem, 1)
        xnT_sb.wait(pe, turn, 0)
        for c, (o, m) in enumerate(FCH):
            wait_room(pe, turn, ("ff", c))
            dst = wide_slot(("ff", c))
            pe.matmul(dst[0:m, 0:GW], w1[:, FF + o:FF + o + m], xnT[:], start=True, stop=True)
            pe.matmul(dst[0:m, GW:2 * GW], w1[:, o:o + m], xnT[:], start=True, stop=True) \
                .then_inc(ff_ps.sem, 1)
        wait_room(pe, turn, ("y", 0))
        for c, (o, m) in enumerate(FCH):
            u_sb.wait(pe, turn, c)
            last = pe.matmul(wide_slot(("y", 0))[:, 0:GW], w2[0:m, c, :], uT[0:m, c, :],
                             start=(c == 0), stop=(c == 2))
        last.then_inc(y_ps.sem, 1)

    def scalar(act):
        if nth == 0:
            for s in (xs_sb, xf_sb, xs_moved, xf_moved, squared, v_sb, qkT_sb, exp_sb, pT_sb, cT_sb, xnT_sb, gelu_sb):
                s.start(act)
        for b in range(4):
            act.wait_ge(t0, 4 * nth + b + 1)
            act.activation(hT[:, 512 * b:512 * b + 512], ps[:, b, :], ACT.Copy).then_inc(h0, 1)
        act.wait_ge(zeroed, nth + 1)
        act.wait_ge(consts, 16 * N_CONSTS * (nth + 1))
        with act.Fori(0, DEPTH) as layer:
            proj.wait(act, base + layer * NG, -1)
            ln_ps.wait(act, base + layer * NG, -1)
            act.activation(xs[DH:P, GW:GW + 1], zero[DH:P, :], ACT.Copy)
            act.activation(xf[DH:P, GW:GW + 1], zero[DH:P, :], ACT.Copy).then_inc(carry0, 1)
            act.wait_ge(carry0, nth * DEPTH + layer + 1)
            with act.Fori(0, NG) as g:
                scalar_turn(act, base + layer * NG + g, layer, g)

    def scalar_turn(act, turn, layer, g):
        def shift(dst, moved, ready):
            act.activation(dst[DH:P, 0:1], dst[DH:P, GW:GW + 1], ACT.Copy).then_inc(moved.sem, 1)
            moved.wait(act, turn, 0)
            settle(act)
            act.activation(dst[0:DH, 0:GW], hT[0:DH, bass.ds(g * GW, GW)], ACT.Copy)
            act.activation(dst[DH:P, 1:GW + 1], hT[DH:P, bass.ds(g * GW, GW)], ACT.Copy).then_inc(ready.sem, 1)

        def squares_and_v(j):
            for u, what in enumerate("qk"):
                proj.wait(act, turn, 3 * j + u)
                sums.wait(act, turn, 2 * j + u - 2)
                act.activation(sq[u][:].rearrange("p a b -> p (a b)"), wide_slot((what, j)), ACT.Square) \
                    .then_inc(squared.sem, 1)
            proj.wait(act, turn, 3 * j + 2)
            v_copied(act, turn, j)
            act.activation(vtok[j % 2][:].rearrange("p a b -> p (a b)"), wide_slot(("v", j)), ACT.Copy) \
                .then_inc(v_sb.sem, 1)

        def store_qkT(j):
            s_ps.wait(act, turn, j - 1)
            for half in range(2):
                qkT_ps.wait(act, turn, 4 * j + half)
                act.activation(qT[:, 4 * half:4 * half + 4, :].rearrange("p a b -> p (a b)"),
                               narrow_bank(("qT", 2 * j + half)), ACT.Copy).then_inc(qkT_sb.sem, 1)
            s_ps.wait(act, turn, j - 2)
            k_prev.wait(act, turn, j - 1)
            for half in range(2):
                qkT_ps.wait(act, turn, 4 * j + 2 + half)
                for h2 in range(2):
                    rows = slice(DH * h2, DH * h2 + DH)
                    last = act.activation(
                        kT[j % 2][rows, 4 * half:4 * half + 4, h2, WIN:],
                        narrow_bank(("kT", 2 * j + half)).rearrange("p (a b) -> p a b", b=P)[rows], ACT.Copy)
                last.then_inc(qkT_sb.sem, 1)

        def exponentials(j):
            shifted.wait(act, turn, j)
            act.activation(pr[j % 2][:], pr[j % 2][:], ACT.Exp).then_inc(exp_sb.sem, 1)

        def store_pT_cT(j):
            ctx_ps.wait(act, turn, j - 1)
            for half in range(2):
                pT_ps.wait(act, turn, 2 * j + half)
                act.activation(pT[:, 4 * half:4 * half + 4, :].rearrange("p a b -> p (a b)"),
                               narrow_bank(("pT", 2 * j + half)), ACT.Copy).then_inc(pT_sb.sem, 1)
            o_ps.wait(act, turn, j - 1)
            for half in range(2):
                cT_ps.wait(act, turn, 2 * j + half)
                act.activation(cT[:, 4 * half:4 * half + 4, :].rearrange("p a b -> p (a b)"),
                               narrow_bank(("cT", 2 * j + half)), ACT.Copy).then_inc(cT_sb.sem, 1)

        proj.wait(act, turn, -1)
        x2.wait(act, turn, -1)
        shift(xs, xs_moved, xs_sb)
        squares_and_v(0)
        for j in range(GT):
            if j + 1 < GT:
                squares_and_v(j + 1)
            store_qkT(j)
            if j:
                store_pT_cT(j - 1)
            exponentials(j)
        store_pT_cT(GT - 1)
        ln_ps.wait(act, turn, -1)
        x1.wait(act, turn, GT - 1)
        shift(xf, xf_moved, xf_sb)
        vec = lambda c, m=P: vecs[0:m, bass.ds(layer, 1), c]
        xn_ps.wait(act, turn, 0)
        ff_ps.wait(act, turn, -1)
        settle(act)
        act.activation(xnT[:], narrow_bank(("xn", 0)), ACT.Identity, scale=vec(0), bias=vec(1)) \
            .then_inc(xnT_sb.sem, 1)
        for c, (o, m) in enumerate(FCH):
            ff_ps.wait(act, turn, c)
            u_sb.wait(act, turn, (-1, -2, 0)[c])
            settle(act)
            act.activation(gl[0:m, c % 2, :], wide_slot(("ff", c))[0:m, 0:GW], ACT.Gelu, bias=vec(6 + c, m)) \
                .then_inc(gelu_sb.sem, 1)

    def v_copied(eng, turn, j):
        if j >= 1:
            v_keys_wait(eng, turn, j - 1)
        if j == 0:
            for a in range(2):
                eng.wait_ge(v_keys[a], turn * (16 * V_DMAS * GT // 2) + 1)
        if j == 1:
            eng.wait_ge(v_keys[1], turn * (16 * V_DMAS * GT // 2) + 1)

    def vector(v):
        if nth == 0:
            for s in (prod_sb, sums, normed, maxed, shifted, summed, inverted, ctx_sb, x1, bn_done, mv_done,
                      xn_sb, u_sb, x2):
                s.start(v)
        v.wait_ge(x_ready, 1)
        layernorm_vector(v, chain, var0, rstd0, xtok[:], lnx, lnsq, small, nth=nth + 1)
        v.sem_inc(n0, 1)
        v.wait_ge(t0, 4 * nth + 4)
        v.memset(zero[:], 0.0)
        v.wait_ge(consts, 16 * N_CONSTS * (nth + 1))
        v.tensor_copy(identb[:], ident[:])
        for g in range(NG):
            v.tensor_copy(masks[:, g, :].rearrange("p (a c) -> p a c", c=2 * WIN),
                          mask32[:, min(g, 1):min(g, 1) + 1, :].broadcast_to([P, 8, 2 * WIN]))
        for buf in (vtok[0], vtok[1], vbd[0], vbd[1], kT[0], kT[1]):
            last = v.memset(buf[:], 0.0)
        last.then_inc(zeroed, 1)
        v.wait_ge(h0, 4 * nth + 4)
        v.wait_ge(consts, 16 * N_CONSTS * (nth + 1))
        with v.Fori(0, DEPTH) as layer:
            with v.Fori(0, NG) as g:
                vector_turn(v, base + layer * NG + g, layer, g)
        for b in range(4):
            v.wait_ge(back_ps, 4 * nth + b + 1)
            x4 = xtok[:, 4 * b:4 * b + 4, :].rearrange("p a c -> p (a c)")
            chain.add(v.tensor_tensor(x4, x4, ps[:, b, :], ALU.add))
        chain.wait(v)
        v.sem_inc(x_next, 1)

    def vector_turn(v, turn, layer, g):
        vec = lambda c, m=P: vecs[0:m, bass.ds(layer, 1), c]

        def products(j):
            tab_sb.wait(v, turn, j)
            for u, what in enumerate("qk"):
                proj.wait(v, turn, 3 * j + u)
                rotated.wait(v, turn, 2 * j + u - 2)
                squared.wait(v, turn, 2 * j + u)
                src = wide_slot((what, j)).rearrange("p (h c) -> p h c", c=DH)
                v.tensor_tensor(prod[u][:], src.unsqueeze(2).broadcast_to([P, H, 2, DH]),
                                tab[j % 2][:, u].unsqueeze(1).broadcast_to([P, H, 2, DH]), ALU.mult) \
                    .then_inc(prod_sb.sem, 1)
                v.tensor_reduce(stat[:, j % 2, u, :], sq[u][:], axis=AX.X, op=ALU.add).then_inc(sums.sem, 1)

        def normalise(j):
            for u in range(2):
                rotated.wait(v, turn, 2 * j + u)
                rinv.wait(v, turn, 2 * j + u)
                buf = qk[j % 2][u]
                v.tensor_tensor(buf[:], buf[:], stat[:, j % 2, u, :].unsqueeze(2).broadcast_to([P, H, DH]),
                                ALU.mult).then_inc(normed.sem, 1)

        def softmax(j):
            src = wide_slot(("s", j)).rearrange("p (h c) -> p h c", c=2 * WIN)
            s_ps.wait(v, turn, j)
            v.tensor_reduce(mx[:], src, axis=AX.X, op=ALU.max).then_inc(maxed.sem, 1)
            maxed.wait(v, turn, j)
            pT_ps.wait(v, turn, 2 * j - 3)
            v.tensor_tensor(pr[j % 2][:], src, mx[:].unsqueeze(2).broadcast_to([P, H, 2 * WIN]),
                            ALU.subtract).then_inc(shifted.sem, 1)

        def sum_up(j):
            exp_sb.wait(v, turn, j)
            v.tensor_reduce(rs[j % 2][:], pr[j % 2][:], axis=AX.X, op=ALU.add).then_inc(summed.sem, 1)
            summed.wait(v, turn, j)
            v.reciprocal(rs[j % 2][:], rs[j % 2][:]).then_inc(inverted.sem, 1)

        def divide_and_add(j):
            ctx_ps.wait(v, turn, j)
            cT_ps.wait(v, turn, 2 * j - 1)
            inverted.wait(v, turn, j)
            v.tensor_tensor(cn[:].rearrange("p (h c) -> p h c", c=DH),
                            wide_slot(("ctx", j)).rearrange("p (h c) -> p h c", c=DH),
                            rs[j % 2][:].unsqueeze(2).broadcast_to([P, H, DH]), ALU.mult) \
                .then_inc(ctx_sb.sem, 1)

        def add_attention(j):
            o_ps.wait(v, turn, j)
            if j == 0:
                xs_sb.wait(v, turn, 0)
            at = hT[:, bass.ds(g * GW + j * P, P)]
            v.tensor_tensor(at, at, narrow_bank(("o", j))[:, 0:P], ALU.add).then_inc(x1.sem, 1)

        products(0)
        normalise(0)
        for j in range(GT):
            if j + 1 < GT:
                products(j + 1)
            softmax(j)
            if j:
                divide_and_add(j - 1)
            if j + 1 < GT:
                normalise(j + 1)
            sum_up(j)
            if j:
                add_attention(j - 1)
        divide_and_add(GT - 1)
        add_attention(GT - 1)
        ln_ps.wait(v, turn, 0)
        bank = narrow_bank(("ln", 0)).rearrange("p (t c) -> p t c", c=P)
        for j in range(GT):
            last = v.bn_stats(bn[:, j, :], bank[:, j, :])
        last.then_inc(bn_done.sem, 1)
        bn_done.wait(v, turn, 0)
        settle(v)
        for j in range(GT):
            last = v.bn_aggr(mv[:, j, :], bn[:, j, :])
        last.then_inc(mv_done.sem, 1)
        rstd_sb.wait(v, turn, 0)
        mv_done.wait(v, turn, 0)
        for j in range(GT):
            last = v.tensor_scalar(xn[:, j, :], bank[:, j, :], mv[:, j, 0:1], rstd[:, j:j + 1],
                                   ALU.subtract, ALU.mult)
        last.then_inc(xn_sb.sem, 1)
        for c, (o, m) in enumerate(FCH):
            gelu_sb.wait(v, turn, c)
            y_ps.wait(v, turn, -1)
            v.scalar_tensor_tensor(uT[0:m, c, :], wide_slot(("ff", c))[0:m, GW:2 * GW], vec(3 + c, m),
                                   gl[0:m, c % 2, :], ALU.add, ALU.mult).then_inc(u_sb.sem, 1)
        y_ps.wait(v, turn, 0)
        xf_sb.wait(v, turn, 0)
        at = hT[:, bass.ds(g * GW, GW)]
        v.scalar_tensor_tensor(at, wide_slot(("y", 0))[:, 0:GW], vec(2), at, ALU.add, ALU.add) \
            .then_inc(x2.sem, 1)

    def gpsimd(pool):
        if nth == 0:
            for s in (tab_sb, clamped, rinv, rotated, k_prev, rstd_a, rstd_sb):
                s.start(pool)
        layernorm_gpsimd(pool, var0, rstd0, small, minus_half, nth + 1)
        pool.wait_ge(zeroed, nth + 1)
        pool.wait_ge(consts, 16 * N_CONSTS * (nth + 1))
        pool.wait_ge(h0, 4 * nth + 4)
        with pool.Fori(0, DEPTH) as layer:
            with pool.Fori(0, NG) as g:
                gpsimd_turn(pool, base + layer * NG + g, layer, g)

    def gpsimd_turn(pool, turn, layer, g):
        def tables(j):
            prod_sb.wait(pool, turn, 2 * j - 3)
            pool.tensor_tensor(tab[j % 2][:].rearrange("p u s c -> p (u s) c"),
                               tabs[:, bass.ds(g * GT + j, 1), :, :, :].rearrange("p t u s c -> p (t u s) c"),
                               gains4(layer), ALU.mult).then_inc(tab_sb.sem, 1)

        def gains4(layer):
            return gains[:, bass.ds(layer, 1), :, :].rearrange("p l u c -> p (l u) c") \
                .unsqueeze(2).broadcast_to([P, 2, 2, DH])

        def rotate(j):
            for u in range(2):
                sums.wait(pool, turn, 2 * j + u)
                st = stat[:, j % 2, u, :]
                settle(pool)
                pool.tensor_scalar(st, st, 1e-24, None, ALU.max).then_inc(clamped.sem, 1)
                clamped.wait(pool, turn, 2 * j + u)
                pool.tensor_tensor(st, st, minus_half[:, 0:H], ALU.pow).then_inc(rinv.sem, 1)
                prod_sb.wait(pool, turn, 2 * j + u)
                if j >= 2:
                    qkT_ps.wait(pool, turn, 4 * (j - 2) + 2 * u + 1)
                else:
                    qkT_ps.wait(pool, turn, 4 * (j - 2) + 2 * u + 1)
                half = DH // 2
                dst, src = qk[j % 2][u], prod[u]
                pool.tensor_tensor(dst[:, :, 0:half], src[:, :, 0, 0:half], src[:, :, 1, half:], ALU.add)
                pool.tensor_tensor(dst[:, :, half:], src[:, :, 0, half:], src[:, :, 1, 0:half], ALU.add) \
                    .then_inc(rotated.sem, 1)

        def previous_keys(j):
            qkT_sb.wait(pool, turn, 4 * j - 1)
            s_ps.wait(pool, turn, j - 2)
            settle(pool)
            pool.tensor_scalar(kT[j % 2][:, :, :, 0:WIN], kT[1 - j % 2][:, :, :, P:P + WIN], decay[:, 0:1],
                               None, ALU.mult).then_inc(k_prev.sem, 1)

        tables(0)
        rotate(0)
        for j in range(GT):
            if j + 1 < GT:
                tables(j + 1)
            previous_keys(j)
            if j + 1 < GT:
                rotate(j + 1)
        mv_done.wait(pool, turn, 0)
        settle(pool)
        pool.tensor_scalar(rstd[:], mv[:, :, 1], 1e-5, None, ALU.add).then_inc(rstd_a.sem, 1)
        rstd_a.wait(pool, turn, 0)
        pool.tensor_tensor(rstd[:], rstd[:], minus_half[:, 0:GT], ALU.pow).then_inc(rstd_sb.sem, 1)

    N_CONSTS = 3 + 2 + 3 + 6
    add_phase(sync=sync, tensor=tensor, scalar=scalar, vector=vector, gpsimd=gpsimd)


def build_full_attention(nc, settle, ps, xtok, ident, minus_half, small, d, sem, add_phase, x_ready, x_next):
    NS, NU = NT, 2 * NT
    NKB = T // 512
    QG = 4
    with ExitStack() as mem:
        def sb(name, shape, dt=F32):
            return mem.enter_context(nc.sbuf_tensor("b_" + name, shape, dt))

        xT = sb("xT", [P, T])
        w = [sb(f"w{i}", [P, 3, P]) for i in range(2)]
        wo = sb("wo", [P, H, P])
        qkv = sb("qkv", [P, NT, 3 * P])
        q2 = sb("q2", [P, T], F32R)
        k_hi = sb("k_hi", [P, T], F32R)
        k_lo = sb("k_lo", [P, T], F32R)
        both = sb("both", [P, 2, NT, P])
        twice = [both[:, i] for i in range(2)]
        square = both[:].rearrange("p u t c -> p (u t c)").rearrange("p (t c) -> p t c", c=2 * P)
        gam = sb("gam", [P, 2, H])
        lnv = sb("lnv", [P, 2])
        pr = [sb(f"pr{i}", [P, T]) for i in range(2)]
        v2 = sb("v2", [P, NT, 2, 2, DH], F32R)
        p_hi = sb("p_hi", [P, NT, QG, P], F32R)
        p_lo = sb("p_lo", [P, NT, QG, P], F32R)
        mx = sb("mx", [P, 2, NKB])
        nm = sb("nm", [P, 2])
        rs = sb("rs", [P, 2, QG, NKB])
        ri = sb("ri", [P, 2, 2, QG])
        cT = sb("cT", [P, QG * P])
        y = sb("y", [P, NT, P])
        ssq = sb("ssq", [P, 4 * NT])
        rinv = sb("rinv", [P, 4 * NT])
        half = sb("half", [P, 4 * NT])
        lnx = qkv[:].rearrange("p t c -> p (t c)")[:, 0:T].rearrange("p (t c) -> p t c", c=P)
        lnsq = twice[0]

    chain = Chain(sem("b_dve"))
    var1, rstd1, var2, rstd2 = (sem(f"b_norm{i}") for i in range(4))
    normed, xT_ps, xT_sb = sem("b_normed"), sem("b_xT_ps"), sem("b_xT_sb")
    consts, half_set, gam_set = sem("b_consts"), sem("b_half"), sem("b_gam")
    w_ld = [sem(f"b_w_ld{i}") for i in range(2)]
    qkv_ps, qkv_sb = sem("b_qkv_ps"), sem("b_qkv_sb")
    squared, ss_sb, rinv_sb, qk_sb = (sem(f"b_{n}") for n in ("squared", "ss", "rinv", "qk"))
    dup_ps, hi_sb, lo_sb = sem("b_dup_ps"), sem("b_hi_sb"), sem("b_lo_sb")
    s_ps, bank_max, neg_max, exp_sb = (sem(f"b_{n}") for n in ("s_ps", "bank_max", "neg_max", "exp"))
    pT_ps, p_hi_sb, p_lo_sb, c_sb, o_ps, y_sb = (sem(f"b_{n}") for n in
                                                      ("pT_ps", "p_hi", "p_lo", "c_sb", "o_ps", "y"))
    v_hi, v_lo, pv_kt = sem("b_v_hi"), sem("b_v_lo"), sem("b_pv")
    rsum, rrec, y_zero = sem("b_rsum"), sem("b_rrec"), sem("b_y_zero")
    N_CONSTS = 8

    def sync(sp):
        sp.wait_ge(x_ready, 1)
        for h2 in range(2):
            sp.dma_start(wo[DH * h2:DH * h2 + DH, :, :], d["b_Wo"].rearrange("(h c) n -> c h n", c=DH)) \
                .then_inc(consts, 16)
        for u, name in enumerate(("b_q_gamma", "b_k_gamma")):
            for h2 in range(2):
                sp.dma_start(gam[DH * h2:DH * h2 + DH, u, :], d[name].rearrange("h c -> c h"),
                             allow_slow_non_contiguous=True).then_inc(consts, 16)
        for c, name in enumerate(("b_ln_w", "b_ln_b")):
            sp.dma_start(lnv[:, c:c + 1], d[name].rearrange("(p a) -> p a", a=1)).then_inc(consts, 16)
        for hp in range(HP):
            if hp >= 2:
                sp.wait_ge(qkv_ps, NT * (hp - 1))
            for u in range(3):
                src = d["b_Wq"][:, hp * P:(hp + 1) * P] if u == 0 else \
                    d["b_Wkv"][:, (u - 1) * INNER + hp * P:(u - 1) * INNER + (hp + 1) * P]
                sp.dma_start(w[hp % 2][:, u, :], src).then_inc(w_ld[hp % 2], 16)

    def tensor(pe):
        for s in (dup_ps, o_ps):
            pe.sem_inc(s, 1)
        pe.sem_inc(pv_kt, 1 + NKB)
        pe.wait_ge(normed, 1)
        transpose_tiles(pe, ps, lambda t: lnx[:, t, :], ident, range(4), xT_ps)
        pe.wait_ge(xT_sb, 4)
        pe.wait_ge(consts, 16 * N_CONSTS)
        with pe.Fori(0, HP // 2) as hq:
            for e in range(2):
                pe.wait_ge(w_ld[e], hq * 48 + 48)
                tensor_pair(pe, 2 * hq + e, e)

    def tensor_pair(pe, hp, parity):
        pe.wait_ge(y_sb, 1 + hp * NU)
        for t in range(NT):
            if t >= 4:
                pe.wait_ge(qkv_sb, 1 + hp * NT + (t - 3))
            pe.matmul(ps[:, t % 4, 0:3 * P], xT[:, t * P:(t + 1) * P],
                      w[parity][:].rearrange("p u c -> p (u c)"), start=True, stop=True).then_inc(qkv_ps, 1)
        for h2 in range(2):
            n = 0
            if h2:
                pe.wait_ge(y_sb, 1 + hp * NU + NT)
            for u in range(2):
                pe.wait_ge(qk_sb, 1 + hp * 4 + 2 * h2 + u + 1)
                for b in range(4):
                    if u:
                        pe.wait_ge(lo_sb, hp * 16 + 8 * h2 + b + 1)
                    for k in range(4):
                        t = 4 * b + k
                        last = pe.transpose(ps[:, b, k * P:(k + 1) * P], twice[u][:, t, :], ident[:])
                    last.then_inc(dup_ps, 1)
            pe.wait_ge(lo_sb, hp * 16 + 8 * h2 + 8)
            pe.wait_ge(v_lo, hp + 1)
            for i in range(NT + 1):
                if i < NT:
                    score_unit(pe, hp, h2, i)
                if i:
                    transpose_unit(pe, hp, h2, i - 1)
                if i and i % QG == 0:
                    attend_group(pe, hp, h2, i // QG - 1)

    def unit(hp, h2, i):
        return hp * NU + (h2 * NT + i)

    def score_unit(pe, hp, h2, i):
        un = unit(hp, h2, i)
        for b in range(NKB):
            if i:
                pe.wait_ge(exp_sb, (un - 1) * NKB + b + 1)
            pe.matmul(ps[:, b, :], q2[:, i * P:(i + 1) * P], k_hi[:, 512 * b:512 * b + 512],
                      start=True, stop=False)
            pe.matmul(ps[:, b, :], q2[:, i * P:(i + 1) * P], k_lo[:, 512 * b:512 * b + 512],
                      start=False, stop=True).then_inc(s_ps, 1)

    def transpose_unit(pe, hp, h2, i):
        un = unit(hp, h2, i)
        for b in range(NKB):
            pe.wait_ge(exp_sb, un * NKB + b + 1)
            pe.wait_ge(p_lo_sb, un * NKB + b)
            for k in range(4):
                last = pe.transpose(ps[:, 4 + b % 2, k * P:(k + 1) * P],
                                    pr[i % 2][:, (4 * b + k) * P:(4 * b + k + 1) * P], ident[:])
            last.then_inc(pT_ps, 1)

    def group(hp, h2, q):
        return hp * (NU // QG) + (h2 * (NT // QG) + q)

    def attend_group(pe, hp, h2, q):
        gn = group(hp, h2, q)
        pe.wait_ge(c_sb, 1 + gn)
        for b in range(NKB):
            pe.wait_ge(p_lo_sb, 1 + unit(hp, h2, QG * q + QG - 1) * NKB + b + 1)
            for k in range(4):
                t = 4 * b + k
                for part in (p_hi, p_lo):
                    last = pe.matmul(ps[:, 6, :], v2[:, t, h2].rearrange("p r c -> p (r c)"),
                                     part[:, t].rearrange("p a b -> p (a b)"),
                                     start=(t == 0 and part is p_hi), stop=(t == NT - 1 and part is p_lo))
            last.then_inc(pv_kt, 1)
        pe.wait_ge(c_sb, 1 + gn + 1)
        pe.wait_ge(y_sb, 1 + unit(hp, h2, QG * q))
        settle(pe)
        for r in range(QG):
            last = pe.matmul(ps[:, 7, r * P:(r + 1) * P], cT[:, r * P:(r + 1) * P],
                             wo[:, bass.ds(2 * hp + h2, 1), :].rearrange("p a n -> p (a n)"),
                             start=True, stop=True)
        last.then_inc(o_ps, 1)

    def scalar(act):
        for s in (qkv_sb, c_sb):
            act.sem_inc(s, 1)
        act.wait_ge(consts, 16 * N_CONSTS)
        for b in range(4):
            act.wait_ge(xT_ps, b + 1)
            act.activation(xT[:, 512 * b:512 * b + 512], ps[:, b, :], ACT.Identity, scale=lnv[:, 0:1],
                           bias=lnv[:, 1:2]).then_inc(xT_sb, 1)
        act.wait_ge(gam_set, 1)
        with act.Fori(0, HP) as hp:
            for t in range(NT):
                act.wait_ge(qkv_ps, hp * NT + t + 1)
                act.activation(qkv[:, t, :], ps[:, t % 4, 0:3 * P], ACT.Copy).then_inc(qkv_sb, 1)
            act.wait_ge(qkv_sb, 1 + hp * NT + NT)
            act.wait_ge(ss_sb, 1 + hp)
            act.wait_ge(dup_ps, 1 + hp * 16)
            act.activation(square, qkv[:, :, 0:2 * P], ACT.Square).then_inc(squared, 1)
            act.activation(v2[:, :, :, 0, :], qkv[:, :, 2 * P:].rearrange("p t (h c) -> p t h c", c=DH),
                           ACT.Copy).then_inc(v_hi, 1)
            for h2 in range(2):
                for u in range(2):
                    dst = q2 if u == 0 else k_hi
                    for b in range(4):
                        act.wait_ge(dup_ps, 1 + hp * 16 + 8 * h2 + 4 * u + b + 1)
                        settle(act)
                        act.activation(dst[:, 512 * b:512 * b + 512], ps[:, b, :], ACT.Copy,
                                       scale=gain(u, hp, h2)).then_inc(hi_sb, 1)
                for i in range(NT + 1):
                    if i:
                        high_parts(act, hp, h2, i - 1, (0, 1))
                    if i < NT:
                        un = unit(hp, h2, i)
                        act.wait_ge(neg_max, un + 1)
                        if i >= 2:
                            act.wait_ge(pT_ps, (un - 1) * NKB)
                    for b in range(NKB):
                        if i < NT:
                            act.activation(pr[i % 2][:, 512 * b:512 * b + 512], ps[:, b, :], ACT.Exp,
                                           bias=nm[:, i % 2:i % 2 + 1],
                                           accum_out=rs[:, i // QG % 2, i % QG, b:b + 1]).then_inc(exp_sb, 1)
                        if i and b in (1, 2):
                            high_parts(act, hp, h2, i - 1, (b + 1,))
                    if i and i % QG == 0:
                        gn = group(hp, h2, i // QG - 1)
                        act.wait_ge(pv_kt, 1 + (gn + 2) * NKB)
                        act.activation(cT[:], ps[:, 6, :], ACT.Copy).then_inc(c_sb, 1)

    def high_parts(act, hp, h2, i, banks):
        un = unit(hp, h2, i)
        for b in banks:
            act.wait_ge(pT_ps, un * NKB + b + 1)
            act.wait_ge(pv_kt, 1 + group(hp, h2, i // QG) * NKB + b + 1)
            act.activation(p_hi[:, 4 * b:4 * b + 4, i % QG, :],
                           ps[:, 4 + b % 2, :].rearrange("p (a c) -> p a c", c=P), ACT.Copy) \
                .then_inc(p_hi_sb, 1)

    def gain(u, hp, h2, rows=slice(0, P)):
        return gam[rows, u, bass.ds(2 * hp + h2, 1)]

    def vector(v):
        for s in (ss_sb, y_sb, qk_sb, p_lo_sb):
            v.sem_inc(s, 1)
        v.wait_ge(x_ready, 1)
        layernorm_vector(v, chain, var1, rstd1, xtok[:], lnx, lnsq, small)
        layernorm_vector(v, chain, var2, rstd2, lnx, lnx, lnsq, small)
        v.sem_inc(normed, 1)
        v.memset(y[:], 0.0).then_inc(y_zero, 1)
        v.memset(half[:], -0.5).then_inc(half_set, 1)
        v.wait_ge(consts, 16 * N_CONSTS)
        v.tensor_scalar(gam[:], gam[:], 8.0, None, ALU.mult).then_inc(gam_set, 1)
        v.wait_ge(gam_set, 1)
        with v.Fori(0, HP) as hp:
            v.wait_ge(squared, hp + 1)
            chain_ss = v.tensor_reduce(ssq[:], square.rearrange("p t (h c) -> p (t h) c", c=DH),
                                       axis=AX.X, op=ALU.add)
            chain_ss.then_inc(rsum, 1)
            v.wait_ge(rsum, hp * (NU // QG + 1) + 1)
            v.tensor_scalar(ssq[:], ssq[:], 1.0 / DH, 1e-8, ALU.mult, ALU.add).then_inc(ss_sb, 1)
            v.wait_ge(v_hi, hp + 1)
            v.tensor_tensor(v2[:, :, :, 1, :], qkv[:, :, 2 * P:].rearrange("p t (h c) -> p t h c", c=DH),
                            v2[:, :, :, 0, :].bitcast(F32), ALU.subtract).then_inc(v_lo, 1)
            v.wait_ge(rinv_sb, hp + 1)
            for h2 in range(2):
                for u in range(2):
                    v.wait_ge(dup_ps, 1 + hp * 16 + max(8 * (h2 - 1) + 4 * u + 4, 0))
                    at = u * P + DH * h2
                    v.tensor_tensor(
                        twice[u].rearrange("p t (r c) -> p t r c", c=DH),
                        qkv[:, :, at:at + DH].unsqueeze(2).broadcast_to([P, NT, 2, DH]),
                        rinv[:].rearrange("p (t s) -> p t s", s=4)[:, :, 2 * u + h2:2 * u + h2 + 1]
                        .unsqueeze(3).broadcast_to([P, NT, 2, DH]), ALU.mult).then_inc(qk_sb, 1)
                for u in range(2):
                    for b in range(4):
                        v.wait_ge(hi_sb, hp * 16 + 8 * h2 + 4 * u + b + 1)
                        rows = slice(DH, P) if u == 0 else slice(0, P)
                        hi, lo = (q2, q2) if u == 0 else (k_hi, k_lo)
                        cols = slice(512 * b, 512 * b + 512)
                        v.scalar_tensor_tensor(lo[rows, cols], ps[rows, b, :], gain(u, hp, h2, rows),
                                               hi[rows, cols].bitcast(F32), ALU.mult, ALU.subtract) \
                            .then_inc(lo_sb, 1)
                for i in range(NT + 1):
                    if i < NT:
                        un = unit(hp, h2, i)
                        for b in range(NKB):
                            v.wait_ge(s_ps, un * NKB + b + 1)
                            v.tensor_reduce(mx[:, i % 2, b:b + 1], ps[:, b, :], axis=AX.X, op=ALU.max) \
                                .then_inc(bank_max, 1)
                        v.wait_ge(bank_max, un * NKB + NKB)
                        if i >= 2:
                            v.wait_ge(exp_sb, (un - 1) * NKB)
                        v.tensor_reduce(nm[:, i % 2:i % 2 + 1], mx[:, i % 2, :], axis=AX.X, op=ALU.max,
                                        negate=True).then_inc(neg_max, 1)
                    if i:
                        un = unit(hp, h2, i - 1)
                        for b in range(NKB):
                            v.wait_ge(p_hi_sb, un * NKB + b + 1)
                            at = (slice(None), slice(4 * b, 4 * b + 4), (i - 1) % QG)
                            v.tensor_tensor(p_lo[at], ps[:, 4 + b % 2, :].rearrange("p (a c) -> p a c", c=P),
                                            p_hi[at].bitcast(F32), ALU.subtract).then_inc(p_lo_sb, 1)
                    if i and i % QG == 0:
                        q = i // QG - 1
                        gn = group(hp, h2, q)
                        sums, inverse = ri[:, q % 2, 0, :], ri[:, q % 2, 1, :]
                        v.tensor_reduce(sums, rs[:, q % 2], axis=AX.X, op=ALU.add).then_inc(rsum, 1)
                        v.wait_ge(rsum, hp * (NU // QG + 1) + (h2 * (NT // QG) + q + 2))
                        v.reciprocal(inverse, sums).then_inc(rrec, 1)
                        v.wait_ge(rrec, gn + 1)
                        v.wait_ge(o_ps, 1 + gn + 1)
                        for r in range(QG):
                            t = QG * q + r
                            v.scalar_tensor_tensor(y[:, t, :], ps[:, 7, r * P:(r + 1) * P], inverse[:, r:r + 1],
                                                   y[:, t, :], ALU.mult, ALU.add).then_inc(y_sb, 1)
        v.wait_ge(y_sb, 1 + HP * NU)
        chain.add(v.tensor_tensor(xtok[:], xtok[:], y[:], ALU.add))
        chain.wait(v)
        v.sem_inc(x_next, 1)

    def gpsimd(pool):
        layernorm_gpsimd(pool, var1, rstd1, small, minus_half)
        layernorm_gpsimd(pool, var2, rstd2, small, minus_half)
        pool.wait_ge(half_set, 1)
        with pool.Fori(0, HP) as hp:
            pool.wait_ge(ss_sb, 1 + hp + 1)
            pool.wait_ge(qk_sb, 1 + hp * 4)
            pool.tensor_tensor(rinv[:], ssq[:], half[:], ALU.pow).then_inc(rinv_sb, 1)

    add_phase(sync=sync, tensor=tensor, scalar=scalar, vector=vector, gpsimd=gpsimd)


def shape_constants():
    half = np.arange(0, DH, 2, dtype=np.float32)
    inv_freq = (1.0 / np.float32(10000.0) ** (half / np.float32(DH))).astype(np.float32)
    t = np.arange(T, dtype=np.float32)
    freqs = (t[:, None] * inv_freq[None, :]).astype(np.float32)
    cos, sin = np.cos(freqs.astype(np.float64)), np.sin(freqs.astype(np.float64))
    base = ((half + np.float32(0.4 * DH)) / np.float32(1.4 * DH)).astype(np.float64)
    power = (np.arange(T) % P - P // 2) / (WIN // 2)
    scale = base[None, :] ** power[:, None]
    tabs = np.zeros((T, 2, 2, DH))
    for u, s in enumerate((8.0 * scale, 1.0 / scale)):
        tabs[:, u, 0, :] = np.concatenate([cos * s, cos * s], -1)
        tabs[:, u, 1, :] = np.concatenate([sin * s, -sin * s], -1)
    tabs = tabs.reshape(NT, P, 2, 2, DH).transpose(1, 0, 2, 3, 4).astype(np.float32)
    i = np.arange(P) % WIN
    key = np.arange(2 * WIN)[None, :] - WIN
    masked = (key > i[:, None]) | (key < i[:, None] - WIN)
    general = np.where(masked, NEG, 0.0)
    first = np.where(masked | ((np.arange(P)[:, None] < WIN) & (key < 0)), NEG, 0.0)
    masks = np.stack([first, general], 1)
    decay = np.tile(np.concatenate([base, base]) ** (P / (WIN // 2)), 2)[:, None]
    return {
        "tabs": tabs, "masks": masks.astype(np.float32), "decay": decay.astype(np.float32),
        "ident": np.eye(P, dtype=np.float32),
    }


def kernel(**inputs):
    import concourse.bacc as bacc
    from concourse.bass_utils import run_bass_kernel_spmd as run

    a = {k.removeprefix("L0_"): np.asarray(v) for k, v in inputs.items()}
    arrays = {
        "x": a["attn_a_x"].reshape(T, P),
        "hawk_gamma": a["attn_a_hawk_norm_gamma"], "gmlp_gamma": a["attn_a_gmlp_norm_gamma"],
        "input_wT": a["attn_a_input_w"].T, "gates_wT": a["attn_a_gates_w"].T,
        "output_wT": a["attn_a_output_w"].T, "grow_wT": a["attn_a_grow_w"].T,
        "shrink_wT": a["attn_a_shrink_w"].T,
        "conv_w": a["attn_a_conv_w"].reshape(P, 4), "conv_b": a["attn_a_conv_b"],
        "gates_b": a["attn_a_gates_b"], "forget_base": a["attn_a_forget_base"],
        "b_ln_w": a["attn_b_ln_w"], "b_ln_b": a["attn_b_ln_b"], "b_Wq": a["attn_b_Wq"],
        "b_Wkv": a["attn_b_Wkv"], "b_q_gamma": a["attn_b_q_gamma"].reshape(H, DH),
        "b_k_gamma": a["attn_b_k_gamma"].reshape(H, DH), "b_Wo": a["attn_b_Wo"],
        "Wqkv": a["ffn_Wqkv"], "q_scale": a["ffn_q_scale"], "k_scale": a["ffn_k_scale"],
        "Wo": a["ffn_Wo"], "ln_g": a["ffn_ln_g"], "ln_b": a["ffn_ln_b"], "W1": a["ffn_W1"],
        "b1": a["ffn_b1"], "W2": a["ffn_W2"], "b2": a["ffn_b2"],
    }
    arrays.update(shape_constants())
    arrays = {k: np.ascontiguousarray(v) for k, v in arrays.items()}
    nc = bacc.Bacc("TRN2", target_bir_lowering=False, num_devices=1)
    d = {k: nc.dram_tensor("in_" + k, v.shape, mybir.dt.from_np(v.dtype), kind="ExternalInput").ap()
         for k, v in arrays.items()}
    out = nc.dram_tensor("out", (T, P), F32, kind="ExternalOutput").ap()
    build_program(nc, d, out)
    r = run(nc, [{"in_" + k: v for k, v in arrays.items()}], core_ids=[0])
    return r.results[0]["out"].reshape(1, T, P)
```

```python
from contextlib import ExitStack

import numpy as np
import concourse.bass as bass
from concourse import mybir

ALU = mybir.AluOpType
ACT = mybir.ActivationFunctionType
AX = mybir.AxisListType
F32 = mybir.dt.float32
F32R = mybir.dt.float32r
BF16 = mybir.dt.bfloat16

P = 128
T = 2048
NT = T // P
H = 16
DH = 64
HP = H // 2
INNER = H * DH
WIN = 32
NW = P // WIN
DEPTH = 6
GT = 4
GW = GT * P
NG = T // GW
FF = 341
FCH = [(0, 128), (128, 128), (256, 85)]
NEG = -1e30


class Signal:

    def __init__(self, sem, per_group, early=0):
        self.sem, self.per_group, self.early = sem, per_group, early

    def start(self, eng, nth):
        n = self.per_group - (self.early if nth else 0)
        if n:
            eng.sem_inc(self.sem, n)

    def wait(self, eng, turn, n):
        count = turn * self.per_group + (self.per_group + n + 1)
        if not isinstance(count, int) or count > 0:
            eng.wait_ge(self.sem, count)


class Settle:

    def __init__(self, sem):
        self.sem = sem

    def __call__(self, eng):
        eng.sem_inc(self.sem, 1)


class Chain:

    def __init__(self, sem):
        self.sem, self.n = sem, 0

    def add(self, ins):
        self.n += 1
        ins.then_inc(self.sem, 1)

    def wait(self, eng):
        eng.wait_ge(self.sem, self.n)


def build_program(nc, d, out):
    ctx = ExitStack()
    with ctx:
        semaphores = {}

        def sem(name):
            if name not in semaphores:
                semaphores[name] = ctx.enter_context(nc.semaphore(name))
            return semaphores[name]

        stack_chain = Chain(sem("f_dve"))
        half_set = sem("half_set")
        settle = Settle(sem("settled"))

        def keep(name, shape, dt=F32):
            return ctx.enter_context(nc.sbuf_tensor(name, shape, dt))

        ps = ctx.enter_context(nc.psum_tensor("ps", [P, 8, 512], F32))
        xtok = keep("xtok", [P, NT, P])
        ident = keep("ident", [P, P])
        identb = keep("identb", [P, P], BF16)
        minus_half = keep("minus_half", [P, 64])
        small = keep("small", [P, 8, 64])

        loads_done = sem("loads_done")
        n_loads = 2
        engines = {"sync": [], "scalar": [], "vector": [], "gpsimd": [], "tensor": []}
        x_ready = [sem(f"x_ready{i}") for i in range(5)]

        def load_common(sp):
            sp.dma_start(xtok[:], d["x"].rearrange("(t p) c -> p t c", p=P)).then_inc(loads_done, 16)
            sp.dma_start(ident[:], d["ident"]).then_inc(loads_done, 16)
        engines["sync"].append(load_common)

        def set_half(pool):
            pool.memset(minus_half[:], -0.5).then_inc(half_set, 1)
        engines["gpsimd"].append(set_half)

        def add_phase(**programs):
            for name, program in programs.items():
                engines[name].append(program)

        build_recurrent_block(nc, ps, xtok, ident, minus_half, small, d, sem, add_phase,
                              (loads_done, 16 * n_loads), half_set, x_ready[1])
        build_window_stack(nc, 0, stack_chain, settle, ps, xtok, ident, identb, minus_half, small, d, sem, add_phase,
                           x_ready[1], x_ready[2])
        build_full_attention(nc, settle, ps, xtok, ident, minus_half, small, d, sem, add_phase,
                             x_ready[2], x_ready[3])
        build_window_stack(nc, 1, stack_chain, settle, ps, xtok, ident, identb, minus_half, small, d, sem, add_phase,
                           x_ready[3], x_ready[4])

        out_stored = sem("out_stored")

        def store(sp):
            sp.wait_ge(x_ready[4], 1)
            sp.dma_start(out.rearrange("(t p) c -> p t c", p=P), xtok[:]).then_inc(out_stored, 16)
            sp.wait_ge(out_stored, 16)
        engines["sync"].append(store)

        block = ctx.enter_context(nc.Block())

        @block.sync
        def _(eng):
            for program in engines["sync"]:
                program(eng)

        @block.scalar
        def _(eng):
            for program in engines["scalar"]:
                program(eng)

        @block.vector
        def _(eng):
            for program in engines["vector"]:
                program(eng)

        @block.gpsimd
        def _(eng):
            for program in engines["gpsimd"]:
                program(eng)

        @block.tensor
        def _(eng):
            for program in engines["tensor"]:
                program(eng)


def per_token(ap, n=P):
    return ap.unsqueeze(2).broadcast_to([P, NT, n])


def layernorm_vector(v, chain, variance_ready, rstd_ready, src, dst, square, small, nth=1, eps=1e-5):
    mean, var, rstd = small[:, 0, 0:NT], small[:, 1, 0:NT], small[:, 2, 0:NT]
    chain.add(v.tensor_reduce(mean, src, axis=AX.X, op=ALU.add))
    chain.wait(v)
    chain.add(v.tensor_scalar(mean, mean, 1.0 / P, None, ALU.mult))
    chain.wait(v)
    chain.add(v.tensor_tensor(dst, src, per_token(mean), ALU.subtract))
    chain.wait(v)
    chain.add(v.tensor_tensor(square, dst, dst, ALU.mult))
    chain.wait(v)
    chain.add(v.tensor_reduce(var, square, axis=AX.X, op=ALU.add))
    chain.wait(v)
    v.tensor_scalar(var, var, 1.0 / P, eps, ALU.mult, ALU.add).then_inc(variance_ready, 1)
    v.wait_ge(rstd_ready, nth)
    chain.add(v.tensor_tensor(dst, dst, per_token(rstd), ALU.mult))
    chain.wait(v)


def layernorm_gpsimd(pool, variance_ready, rstd_ready, small, minus_half, nth=1):
    pool.wait_ge(variance_ready, nth)
    pool.tensor_tensor(small[:, 2, 0:NT], small[:, 1, 0:NT], minus_half[:, 0:NT], ALU.pow) \
        .then_inc(rstd_ready, 1)


def transpose_tiles(pe, ps, src, ident, banks, ready):
    for b, bank in enumerate(banks):
        for k in range(4):
            last = pe.transpose(ps[:, bank, k * P:(k + 1) * P], src(4 * b + k), ident[:])
        last.then_inc(ready, 1)


def build_recurrent_block(nc, ps, xtok, ident, minus_half, small, d, sem, add_phase, loaded, half_set,
                          x_next):
    with ExitStack() as mem:
        def sb(name, shape, dt=F32):
            return mem.enter_context(nc.sbuf_tensor("a_" + name, shape, dt))

        atok = sb("atok", [P, NT, P])
        ntok = sb("ntok", [P, NT, P])
        nT = sb("nT", [P, T])
        square = sb("square", [P, NT, P])
        gate = sb("gate", [P, T])
        z = sb("z", [P, 3 + T])
        zc = sb("zc", [P, T])
        forget = sb("forget", [P, T])
        insig = sb("insig", [P, T])
        beta = sb("beta", [P, T])
        hid = sb("hid", [P, T])
        yT = sb("yT", [P, T])
        w_in = sb("w_in", [P, 256])
        w_gates = sb("w_gates", [P, 256])
        w_out = sb("w_out", [P, P])
        w_grow = sb("w_grow", [P, 512])
        w_shrink = sb("w_shrink", [P, 2, P])
        cols = sb("cols", [P, 16])
        cw = sb("cw", [P, 4])
        tiny = sb("tiny", [P, 12])
        G1, G2, CB, FB, BF, BI = (cols[:, i:i + 1] for i in range(6))

    w_loaded = sem("a_w_loaded")
    chain = Chain(sem("a_dve"))
    var1, rstd1, var2, rstd2, var3, rstd3 = (sem(f"a_norm{i}") for i in range(6))
    norm_ready = [sem(f"a_norm_ready{i}") for i in range(2)]
    tr = [sem(f"a_transposed{i}") for i in range(4)]
    nT_ready = [sem(f"a_nT_ready{i}") for i in range(2)]
    cols_scaled = sem("a_cols_scaled")
    u_ps, gate_sb, z_sb = sem("a_u_ps"), sem("a_gate_sb"), sem("a_z_sb")
    conv_done, fg_ps, sig_sb = sem("a_conv_done"), sem("a_fg_ps"), sem("a_sig_sb")
    softplus_done, alpha_sb, one_minus, beta_sb = (sem(f"a_{n}") for n in
                                                   ("softplus", "alpha", "one_minus", "beta_sb"))
    zpad, h_done, y_ps, y_sb, back_used = (sem(f"a_{n}") for n in ("zpad", "h", "y_ps", "y_sb", "back"))
    absx, expx = sem("a_absx"), sem("a_expx")
    m_ps, m_gelu, m_u, m_out, m_sb, m_used = (sem(f"a_m_{n}") for n in
                                              ("ps", "gelu", "u", "out", "sb", "used"))

    def sync(sp):
        n = lambda ap: ap.rearrange("(p a) -> p a", a=1)
        for dst, src in ((w_in[:], d["input_wT"]), (w_gates[:], d["gates_wT"]), (w_out[:], d["output_wT"]),
                         (w_grow[:], d["grow_wT"]),
                         (w_shrink[:], d["shrink_wT"].rearrange("(c p) n -> p c n", p=P)),
                         (cw[:], d["conv_w"]), (G1, n(d["hawk_gamma"])), (G2, n(d["gmlp_gamma"])),
                         (CB, n(d["conv_b"])), (FB, n(d["forget_base"])),
                         (BF, n(d["gates_b"][0:P])), (BI, n(d["gates_b"][P:2 * P]))):
            sp.dma_start(dst, src).then_inc(w_loaded, 16)
    n_w = 12

    def rms_vector(v, ss_ready, rinv_ready, norm_done):
        chain.add(v.tensor_tensor(square[:], atok[:], atok[:], ALU.mult))
        chain.wait(v)
        v.tensor_reduce(small[:, 1, 0:NT], square[:], axis=AX.X, op=ALU.add).then_inc(ss_ready, 1)
        v.wait_ge(rinv_ready, 1)
        v.tensor_tensor(ntok[:], atok[:], per_token(small[:, 2, 0:NT]), ALU.mult).then_inc(norm_done, 1)

    def vector(v):
        v.wait_ge(loaded[0], loaded[1])
        layernorm_vector(v, chain, var1, rstd1, xtok[:], atok[:], square[:], small)
        rms_vector(v, var2, rstd2, norm_ready[0])
        v.wait_ge(w_loaded, 16 * n_w)
        v.tensor_scalar(cols[:, 0:2], cols[:, 0:2], float(np.sqrt(P)), None, ALU.mult).then_inc(cols_scaled, 1)
        v.memset(z[:, 0:3], 0.0).then_inc(zpad, 1)
        c = lambda i: tiny[:, i:i + 1]
        chain.add(v.tensor_scalar(c(0), FB, -1.0, None, ALU.mult))
        chain.wait(v)
        v.tensor_tensor(c(1), c(0), FB, ALU.min).then_inc(absx, 1)
        v.wait_ge(expx, 1)
        chain.add(v.tensor_scalar(c(3), c(2), 2.0, None, ALU.add))
        chain.wait(v)
        chain.add(v.reciprocal(c(4), c(3)))
        chain.wait(v)
        chain.add(v.tensor_tensor(c(5), c(2), c(4), ALU.mult))
        chain.wait(v)
        chain.add(v.tensor_tensor(c(6), c(5), c(5), ALU.mult))
        chain.add(v.memset(c(7), 1.0 / 17))
        chain.wait(v)
        for k in range(15, 0, -2):
            chain.add(v.tensor_scalar(c(7), c(7), c(6), 1.0 / k, ALU.mult, ALU.add))
            chain.wait(v)
        chain.add(v.scalar_tensor_tensor(c(8), c(7), 2.0, c(5), ALU.mult, ALU.mult))
        chain.add(v.tensor_scalar(c(9), FB, 0.0, None, ALU.max))
        chain.wait(v)
        chain.add(v.tensor_tensor(c(10), c(8), c(9), ALU.add))
        chain.wait(v)
        v.tensor_scalar(c(11), c(10), -8.0, None, ALU.mult).then_inc(softplus_done, 1)
        v.wait_ge(z_sb, 4)
        chain.add(v.tensor_scalar(zc[:], z[:, 0:T], cw[:, 0:1], CB, ALU.mult, ALU.add))
        chain.wait(v)
        for k in range(1, 4):
            ins = v.scalar_tensor_tensor(zc[:], z[:, k:k + T], cw[:, k:k + 1], zc[:], ALU.mult, ALU.add)
            if k < 3:
                chain.add(ins)
                chain.wait(v)
            else:
                ins.then_inc(conv_done, 1)
        v.wait_ge(alpha_sb, 1)
        chain.add(v.tensor_tensor(beta[:], forget[:], forget[:], ALU.mult))
        chain.wait(v)
        v.tensor_scalar(beta[:], beta[:], -1.0, 1.0, ALU.mult, ALU.add).then_inc(one_minus, 1)
        v.wait_ge(beta_sb, 1)
        chain.add(v.tensor_tensor(beta[:], beta[:], insig[:], ALU.mult))
        chain.wait(v)
        chain.add(v.tensor_tensor(beta[:], beta[:], zc[:], ALU.mult))
        chain.wait(v)
        chain.add(v.tensor_tensor_scan(hid[:], forget[:], beta[:], 0.0, ALU.mult, ALU.add))
        chain.wait(v)
        v.wait_ge(gate_sb, 4)
        v.tensor_tensor(hid[:], hid[:], gate[:], ALU.mult).then_inc(h_done, 1)
        for b in range(4):
            v.wait_ge(tr[1], b + 1)
            ins = v.tensor_tensor(atok[:, 4 * b:4 * b + 4, :].rearrange("p a c -> p (a c)"),
                                  atok[:, 4 * b:4 * b + 4, :].rearrange("p a c -> p (a c)"),
                                  ps[:, 4 + b, :], ALU.add)
            chain.add(ins)
        chain.wait(v)
        rms_vector(v, var3, rstd3, norm_ready[1])
        for q in range(4):
            for c_ in range(2):
                v.wait_ge(m_gelu, 2 * q + c_ + 1)
                v.tensor_tensor(forget[:, 1024 * (q % 2) + 512 * c_:1024 * (q % 2) + 512 * c_ + 512],
                                beta[:, 512 * c_:512 * c_ + 512], ps[:, 2 * c_ + 1, :], ALU.mult) \
                    .then_inc(m_u, 1)
        for b in range(4):
            v.wait_ge(tr[3], b + 1)
            a4 = atok[:, 4 * b:4 * b + 4, :].rearrange("p a c -> p (a c)")
            x4 = xtok[:, 4 * b:4 * b + 4, :].rearrange("p a c -> p (a c)")
            chain.add(v.tensor_tensor(a4, a4, ps[:, 4 + b, :], ALU.add))
            chain.wait(v)
            chain.add(v.tensor_tensor(x4, x4, a4, ALU.add))
        chain.wait(v)
        v.sem_inc(x_next, 1)

    def gpsimd(pool):
        pool.wait_ge(half_set, 1)
        layernorm_gpsimd(pool, var1, rstd1, small, minus_half)
        layernorm_gpsimd(pool, var2, rstd2, small, minus_half)
        layernorm_gpsimd(pool, var3, rstd3, small, minus_half)

    def tensor(pe):
        pe.wait_ge(norm_ready[0], 1)
        transpose_tiles(pe, ps, lambda t: ntok[:, t, :], ident, range(4), tr[0])
        pe.wait_ge(w_loaded, 16 * n_w)
        pe.wait_ge(nT_ready[0], 4)
        for m in range(2):
            for q in range(4):
                pe.matmul(ps[:, 4 * m + q, :], w_in[:, m * P:(m + 1) * P], nT[:, 512 * q:512 * q + 512],
                          start=True, stop=True).then_inc(u_ps, 1)
        pe.wait_ge(conv_done, 1)
        pe.wait_ge(gate_sb, 4)
        for m in range(2):
            for q in range(4):
                pe.matmul(ps[:, 4 * m + q, :], w_gates[:, m * P:(m + 1) * P], zc[:, 512 * q:512 * q + 512],
                          start=True, stop=True).then_inc(fg_ps, 1)
        pe.wait_ge(h_done, 1)
        for q in range(4):
            pe.matmul(ps[:, q, :], w_out[:], hid[:, 512 * q:512 * q + 512], start=True, stop=True) \
                .then_inc(y_ps, 1)
        pe.wait_ge(y_sb, 4)
        transpose_tiles(pe, ps, lambda t: yT[:, t * P:(t + 1) * P], ident, range(4, 8), tr[1])
        pe.wait_ge(norm_ready[1], 1)
        transpose_tiles(pe, ps, lambda t: ntok[:, t, :], ident, range(4), tr[2])
        pe.wait_ge(nT_ready[1], 4)
        for q in range(4):
            for c in range(2):
                if q:
                    pe.wait_ge(m_u, 2 * (q - 1) + c + 1)
                pe.matmul(ps[:, 2 * c, :], w_grow[:, c * P:(c + 1) * P], nT[:, 512 * q:512 * q + 512],
                          start=True, stop=True)
                pe.matmul(ps[:, 2 * c + 1, :], w_grow[:, 256 + c * P:256 + (c + 1) * P],
                          nT[:, 512 * q:512 * q + 512], start=True, stop=True).then_inc(m_ps, 1)
            for c in range(2):
                pe.wait_ge(m_u, 2 * q + c + 1)
                last = pe.matmul(ps[:, 4 + q, :], w_shrink[:, c, :],
                                 forget[:, 1024 * (q % 2) + 512 * c:1024 * (q % 2) + 512 * c + 512],
                                 start=(c == 0), stop=(c == 1))
            last.then_inc(m_out, 1)
        pe.wait_ge(m_sb, 4)
        transpose_tiles(pe, ps, lambda t: yT[:, t * P:(t + 1) * P], ident, range(4, 8), tr[3])

    def scalar(act):
        act.wait_ge(cols_scaled, 1)
        for b in range(4):
            act.wait_ge(tr[0], b + 1)
            act.activation(nT[:, 512 * b:512 * b + 512], ps[:, b, :], ACT.Copy, scale=G1).then_inc(nT_ready[0], 1)
        act.wait_ge(absx, 1)
        act.activation(tiny[:, 2:3], tiny[:, 1:2], ACT.Exp).then_inc(expx, 1)
        for q in range(4):
            act.wait_ge(u_ps, 4 + q + 1)
            act.activation(z[:, 3 + 512 * q:3 + 512 * q + 512], ps[:, 4 + q, :], ACT.Copy).then_inc(z_sb, 1)
        for q in range(4):
            act.activation(gate[:, 512 * q:512 * q + 512], ps[:, q, :], ACT.Gelu).then_inc(gate_sb, 1)
        for m, dst, bias in ((0, forget, BF), (1, insig, BI)):
            for q in range(4):
                act.wait_ge(fg_ps, 4 * m + q + 1)
                act.activation(dst[:, 512 * q:512 * q + 512], ps[:, 4 * m + q, :], ACT.Sigmoid, bias=bias) \
                    .then_inc(sig_sb, 1)
        act.wait_ge(sig_sb, 8)
        act.wait_ge(softplus_done, 1)
        act.activation(forget[:], forget[:], ACT.Exp, scale=tiny[:, 11:12]).then_inc(alpha_sb, 1)
        act.wait_ge(one_minus, 1)
        act.activation(beta[:], beta[:], ACT.Sqrt, bias=eps6[:]).then_inc(beta_sb, 1)
        for q in range(4):
            act.wait_ge(y_ps, q + 1)
            act.activation(yT[:, 512 * q:512 * q + 512], ps[:, q, :], ACT.Copy).then_inc(y_sb, 1)
        for b in range(4):
            act.wait_ge(tr[2], b + 1)
            act.activation(nT[:, 512 * b:512 * b + 512], ps[:, b, :], ACT.Copy, scale=G2).then_inc(nT_ready[1], 1)
        for q in range(4):
            for c in range(2):
                act.wait_ge(m_ps, 2 * q + c + 1)
                if q:
                    act.wait_ge(m_u, 2 * (q - 1) + c + 1)
                act.activation(beta[:, 512 * c:512 * c + 512], ps[:, 2 * c, :], ACT.Gelu).then_inc(m_gelu, 1)
            act.wait_ge(m_out, q + 1)
            act.activation(yT[:, 512 * q:512 * q + 512], ps[:, 4 + q, :], ACT.Copy).then_inc(m_sb, 1)

    eps6 = small[:, 7, 0:1]
    eps_set = sem("a_eps_set")

    def gpsimd_eps(pool):
        pool.memset(small[:, 7, 0:1], 1e-6).then_inc(eps_set, 1)

    def scalar_all(act):
        act.wait_ge(eps_set, 1)
        scalar(act)

    add_phase(gpsimd=gpsimd_eps)
    add_phase(sync=sync, vector=vector, gpsimd=gpsimd, tensor=tensor, scalar=scalar_all)


WIDE_SLOTS = 3
NARROW_BANK = 6


def psum_orders():
    def halves(what, j, ahead=0):
        return [(what, 2 * j, ahead), (what, 2 * j + 1, ahead)]

    wide, narrow = [], []
    for j in range(1, GT):
        n, ahead = (j + 1) % GT, (j + 1) // GT
        if j > 1:
            wide += [("q", n, ahead)]
            narrow += halves("qT", j)
        wide += [("k", n, ahead), ("ctx", j - 1, 0), ("v", n, ahead), ("s", j, 0)]
        narrow += halves("pT", j - 1) + halves("kT", j) + halves("cT", j - 1) + [("o", j - 1, 0)]
    wide += [("q", 1, 1), ("ctx", GT - 1, 0), ("k", 1, 1), ("v", 1, 1), ("s", 0, 1)]
    wide += [("ff", 0, 0), ("ff", 1, 0), ("ff", 2, 0), ("q", 2, 1), ("y", 0, 0)]
    narrow += halves("qT", 0, 1) + halves("pT", GT - 1) + halves("kT", 0, 1) + halves("cT", GT - 1)
    narrow += [("o", GT - 1, 0), ("ln", 0, 0), ("xn", 0, 0)] + halves("qT", 1, 1)
    assert len(wide) % WIDE_SLOTS == 0 and len(narrow) % 2 == 0
    return wide, narrow


def at(index):
    return slice(index, index + 1) if isinstance(index, int) else bass.ds(index, 1)


def build_window_stack(nc, nth, chain, settle, ps, xtok, ident, identb, minus_half, small, d, sem, add_phase,
                       x_ready, x_next):
    wide, narrow = psum_orders()
    wide_uses, narrow_uses = [u[:2] for u in wide], [u[:2] for u in narrow]
    with ExitStack() as mem:
        def sb(name, shape, dt=F32):
            return mem.enter_context(nc.sbuf_tensor(f"f{nth}_" + name, shape, dt))

        hT = sb("hT", [P, T])
        wqkv = sb("wqkv", [P, 3 * INNER])
        wo = sb("wo", [P, HP, P])
        w1 = sb("w1", [P, 2 * FF])
        w2 = sb("w2", [P, 3, P])
        tabs = sb("tabs", [P, NT, 2, 2, DH])
        masks = sb("masks", [P, 2, 512], BF16)
        mask32 = sb("mask32", [P, 2, 2 * WIN])
        decay = sb("decay", [P, 1])
        gains = sb("gains", [P, DEPTH + 1, 2, DH])
        vecs = sb("vecs", [P, DEPTH, 9])
        xs = sb("xs", [P, GW + 1])
        xf = sb("xf", [P, GW + 1])
        tab = [sb(f"tab{i}", [P, 2, 2, DH]) for i in range(2)]
        prod = [sb(f"prod{i}", [P, H, 2, DH]) for i in range(2)]
        sq = [sb(f"sq{i}", [P, H, DH]) for i in range(2)]
        stat = sb("stat", [P, 2, 2, H])
        qk = [[sb(f"qk{i}{u}", [P, H, DH]) for u in range(2)] for i in range(2)]
        qT = sb("qT", [P, HP, P])
        kT = [sb(f"kT{i}", [P, HP, 2, WIN + P]) for i in range(2)]
        vtok = [sb(f"vtok{i}", [P, 2, 512]) for i in range(2)]
        vbd = [sb(f"vbd{i}", [P, NW, 2, 512]) for i in range(2)]
        pr = [sb(f"pr{i}", [P, H, 2 * WIN]) for i in range(2)]
        mx = sb("mx", [P, H])
        rs = [sb(f"rs{i}", [P, H]) for i in range(2)]
        pT = sb("pT", [P, HP, P])
        cn = sb("cn", [P, INNER])
        cT = sb("cT", [P, HP, P])
        bn = sb("bn", [P, GT, 6])
        mv = sb("mv", [P, GT, 2])
        rstd = sb("rstd", [P, GT])
        xn = sb("xn", [P, GT, P])
        xnT = sb("xnT", [P, GW])
        carried = sb("carried", [P, NG])
        gl = sb("gl", [P, 2, GW])
        uT = sb("uT", [P, 3, GW])
        ntok = qk[0][0][:].rearrange("p a b -> p (a b)")
        lnsq = prod[0][:].rearrange("p a b c -> p (a b c)").rearrange("p (t c) -> p t c", c=P)
        lnx = prod[1][:].rearrange("p a b c -> p (a b c)").rearrange("p (t c) -> p t c", c=P)

    def signal(name, per_group, early=0):
        return Signal(sem(f"f_{name}"), per_group, early)

    proj = signal("proj", 3 * GT, 7)
    qkT_ps = signal("qkT_ps", 4 * GT, 6)
    s_ps = signal("s_ps", GT, 1)
    pT_ps = signal("pT_ps", 2 * GT)
    ctx_ps = signal("ctx_ps", GT)
    cT_ps = signal("cT_ps", 2 * GT)
    o_ps = signal("o_ps", GT)
    ln_ps, xn_ps, ff_ps, y_ps = signal("ln_ps", 1), signal("xn_ps", 1), signal("ff_ps", 3), signal("y_ps", 1)
    squared = signal("squared", 2 * GT, 5)
    v_sb = signal("v_sb", GT, 2)
    qkT_sb = signal("qkT_sb", 4 * GT, 6)
    exp_sb = signal("exp_sb", GT, 1)
    pT_sb = signal("pT_sb", 2 * GT)
    cT_sb = signal("cT_sb", 2 * GT)
    xnT_sb, gelu_sb = signal("xnT_sb", 1), signal("gelu_sb", 3)
    xs_sb, xf_sb = signal("xs_sb", 1, 1), signal("xf_sb", 1)
    xs_moved, xf_moved = signal("xs_moved", 1, 1), signal("xf_moved", 1)
    prod_sb = signal("prod_sb", 2 * GT, 5)
    sums = signal("sums", 2 * GT, 5)
    normed = signal("normed", 2 * GT, 4)
    maxed = signal("maxed", GT, 1)
    shifted = signal("shifted", GT, 1)
    summed = signal("summed", GT, 1)
    inverted = signal("inverted", GT, 1)
    ctx_sb = signal("ctx_sb", GT)
    x1 = signal("x1", GT)
    bn_done, mv_done, xn_sb = signal("bn_done", 1), signal("mv_done", 1), signal("xn_sb", 1)
    u_sb, x2 = signal("u_sb", 3), signal("x2", 1)
    tab_sb = signal("tab_sb", GT, 3)
    clamped, rinv = signal("clamped", 2 * GT, 5), signal("rinv", 2 * GT, 5)
    rotated = signal("rotated", 2 * GT, 5)
    k_prev = signal("k_prev", GT, 2)
    rstd_a, rstd_sb = signal("rstd_a", 1), signal("rstd_sb", 1)
    consts = sem(f"f_consts")
    wqkv_ld, wo_ld, w1_ld, w2_ld = (sem(f"f_{n}") for n in ("wqkv_ld", "wo_ld", "w1_ld", "w2_ld"))
    v_keys = [sem(f"f_v_keys{i}") for i in range(2)]
    zeroed, var0, rstd0, n0, t0, h0, back_ps = (sem(f"f_{n}") for n in
                                               ("zeroed", "var0", "rstd0", "n0", "t0", "h0", "back"))
    V_DMAS = 10
    V_TURN = 16 * V_DMAS * GT // 2
    base = nth * (DEPTH * NG + 1)
    end = base + DEPTH * NG

    released = {
        "q": lambda e, t, j: prod_sb.wait(e, t, 2 * j),
        "k": lambda e, t, j: prod_sb.wait(e, t, 2 * j + 1),
        "v": lambda e, t, j: v_sb.wait(e, t, j),
        "s": lambda e, t, j: shifted.wait(e, t, j),
        "ctx": lambda e, t, j: ctx_sb.wait(e, t, j),
        "ff": lambda e, t, j: u_sb.wait(e, t, j),
        "y": lambda e, t, j: x2.wait(e, t, j),
        "qT": lambda e, t, j: qkT_sb.wait(e, t, 2 * (j // 2) * 2 + j % 2),
        "kT": lambda e, t, j: qkT_sb.wait(e, t, 2 * (j // 2) * 2 + 2 + j % 2),
        "pT": lambda e, t, j: pT_sb.wait(e, t, j),
        "cT": lambda e, t, j: cT_sb.wait(e, t, j),
        "o": lambda e, t, j: x1.wait(e, t, j),
        "ln": lambda e, t, j: xn_sb.wait(e, t, j),
        "xn": lambda e, t, j: xnT_sb.wait(e, t, j),
    }
    def wide_slot(use):
        i = wide_uses.index(use)
        b = 2 * (i % WIDE_SLOTS)
        return ps[:, b:b + 2, :].rearrange("p b n -> p (b n)")

    def narrow_bank(use):
        return ps[:, NARROW_BANK + narrow_uses.index(use) % 2, :]

    def wait_room(pe, turn, use):
        order, uses, step = (wide, wide_uses, WIDE_SLOTS) if use in wide_uses else (narrow, narrow_uses, 2)
        i = uses.index(use)
        what, j, ahead = order[i - step]
        released[what](pe, turn + (ahead - order[i][2] - (1 if i < step else 0)), j)

    def sync(sp):
        for s in v_keys:
            sp.sem_inc(s, V_TURN // 2 if nth else 1)
        sp.wait_ge(x_ready, 1)
        n = 0
        for dst, src in ((tabs[:], d["tabs"]), (mask32[:], d["masks"]), (decay[:], d["decay"])):
            sp.dma_start(dst, src).then_inc(consts, 16)
            n += 1
        for u, name in enumerate(("q_scale", "k_scale")):
            sp.dma_start(gains[:, 0:DEPTH, u, :], d[name].unsqueeze(0).broadcast_to([P, DEPTH, DH])) \
                .then_inc(consts, 16)
            n += 1
        for c, name in enumerate(("ln_g", "ln_b", "b2")):
            sp.dma_start(vecs[:, :, c], d[name].rearrange("l p -> p l"),
                         allow_slow_non_contiguous=True).then_inc(consts, 16)
            n += 1
        for half in range(2):
            for c, (o, m) in enumerate(FCH):
                sp.dma_start(vecs[0:m, :, 3 + 3 * half + c],
                             d["b1"][:, half * FF + o:half * FF + o + m].rearrange("l p -> p l"),
                             allow_slow_non_contiguous=True) \
                    .then_inc(consts, 16)
                n += 1
        assert n == N_CONSTS
        sp.dma_start(wqkv[:], d["Wqkv"][0]).then_inc(wqkv_ld, 16)
        with sp.Fori(0, DEPTH) as layer:
            first = base + layer * NG
            for j in range(2):
                copy_values(sp, first, j)
            o_ps.wait(sp, first, -1)
            settle(sp)
            sp.dma_start(wo[:], d["Wo"][layer].rearrange("(c p) n -> p c n", p=P)).then_inc(wo_ld, 16)
            ff_ps.wait(sp, first, -1)
            settle(sp)
            sp.dma_start(w1[:], d["W1"][layer]).then_inc(w1_ld, 16)
            y_ps.wait(sp, first, -1)
            settle(sp)
            for c, (o, m) in enumerate(FCH):
                sp.dma_start(w2[0:m, c, :], d["W2"][layer][o:o + m, :]).then_inc(w2_ld, 16)
            with sp.Fori(0, NG - 1) as g:
                for j in range(2, GT + 2):
                    copy_values(sp, first + g + j // GT, j % GT)
            copy_values(sp, first + (NG - 1), 2)
            proj.wait(sp, first + NG, -1)
            settle(sp)
            sp.dma_start(wqkv[:], d["Wqkv"][(layer + 1) % DEPTH]).then_inc(wqkv_ld, 16)
            copy_values(sp, first + (NG - 1), 3)
        for j in range(2):
            copy_values(sp, end, j)

    def copy_values(sp, turn, j):
        a, b = j % 2, 1 - j % 2
        v_sb.wait(sp, turn, j)
        settle(sp)
        ctx_ps.wait(sp, turn, j - 2)
        settle(sp)
        for h2 in range(2):
            lo = DH * h2
            sp.dma_start(vbd[a][lo:lo + WIN, 0, h2, :], vtok[b][P - WIN:P, h2, :]).then_inc(v_keys[a], 16)
            sp.dma_start(vbd[a][lo + WIN:lo + DH, 0, h2, :], vtok[a][0:WIN, h2, :]).then_inc(v_keys[a], 16)
            for w in range(1, NW):
                sp.dma_start(vbd[a][lo:lo + DH, w, h2, :], vtok[a][WIN * (w - 1):WIN * (w + 1), h2, :]) \
                    .then_inc(v_keys[a], 16)

    def v_keys_wait(eng, turn, j):
        eng.wait_ge(v_keys[j % 2], turn * V_TURN + (16 * V_DMAS * (j // 2 + 1) + 1))

    def tensor(pe):
        for s in (proj, qkT_ps, s_ps, pT_ps, ctx_ps, cT_ps, o_ps, ln_ps, xn_ps, ff_ps, y_ps):
            s.start(pe, nth)
        pe.wait_ge(n0, nth + 1)
        transpose_tiles(pe, ps, lambda t: lnx[:, t, :], ident, range(4), t0)
        pe.wait_ge(consts, 16 * N_CONSTS * (nth + 1))
        pe.wait_ge(h0, 4 * nth + 4)
        pe.wait_ge(zeroed, nth + 1)
        pe.wait_ge(wqkv_ld, (nth * (DEPTH + 1) + 1) * 16)
        xs_sb.wait(pe, base, 0)

        def room():
            shifted.wait(pe, base, scored - 1)
            prod_sb.wait(pe, base, 2 * (done // 3) + min(done % 3, 2) - 1)
            v_sb.wait(pe, base, done // 3 - 1)
            qkT_sb.wait(pe, base, transposed - 1)

        done, scored, transposed = 0, 0, 0
        for piece in ("q0", "k0", "v0", "qT", "q1", "kT", "k1", "v1", "s", "qT1", "q2"):
            room()
            if piece == "qT":
                transpose_qk(pe, base, 0, 0)
                transposed = 2
            elif piece == "kT":
                transpose_qk(pe, base, 0, 1)
                transposed = 4
            elif piece == "qT1":
                transpose_qk(pe, base, 1, 0)
                transposed = 6
            elif piece == "s":
                scores(pe, base, 0, masks[:, 0, :])
                scored = 1
            else:
                project(pe, base, int(piece[1]), piece[0])
                done += 1
        room()
        with pe.Fori(0, DEPTH) as layer:
            with pe.Fori(0, NG) as g:
                tensor_turn(pe, base + layer * NG + g, layer, g)
        x2.wait(pe, end - 1, 0)
        prod_sb.wait(pe, end, 4)
        v_sb.wait(pe, end, 1)
        qkT_sb.wait(pe, end, 5)
        shifted.wait(pe, end, 0)
        transpose_tiles(pe, ps, lambda t: hT[:, t * P:(t + 1) * P], ident, range(4), back_ps)

    def project(pe, turn, j, what):
        wait_room(pe, turn, (what, j))
        dst = wide_slot((what, j))
        for half in range(2):
            if what == "v":
                w = wqkv[:, 2 * INNER:].rearrange("p (a h c) -> p h a c", h=2, c=DH)[:, half]
            else:
                u = "qk".index(what)
                w = wqkv[:, u * INNER + 512 * half:u * INNER + 512 * half + 512]
            last = pe.matmul(dst[:, 512 * half:512 * half + 512], xs[:, j * P:(j + 1) * P], w,
                             start=True, stop=True)
        last.then_inc(proj.sem, 1)

    def transpose_qk(pe, turn, j, u):
        normed.wait(pe, turn, 2 * j + u)
        for half in range(2):
            use = (("qT", "kT")[u], 2 * j + half)
            wait_room(pe, turn, use)
            for c in range(4):
                hp = 4 * half + c
                src = qk[j % 2][u][:, 2 * hp:2 * hp + 2, :].rearrange("p a b -> p (a b)")
                last = pe.transpose(narrow_bank(use)[:, c * P:(c + 1) * P], src, ident[:])
            last.then_inc(qkT_ps.sem, 1)

    def scores(pe, turn, j, first_mask=None):
        wait_room(pe, turn, ("s", j))
        dst = wide_slot(("s", j))
        qkT_sb.wait(pe, turn, 4 * j + 3)
        k_prev.wait(pe, turn, j)
        for half in range(2):
            bank = dst[:, 512 * half:512 * half + 512]
            mask = first_mask if j == 0 else masks[:, 1, :]
            pe.matmul(bank, identb[:], mask, start=True, stop=False, skip_group_check=True)
            for c in range(4):
                hp = 4 * half + c
                for w in range(NW):
                    last = pe.matmul(bank[WIN * w:WIN * (w + 1), c * P:(c + 1) * P],
                                     qT[:, hp, WIN * w:WIN * (w + 1)],
                                     kT[j % 2][:, hp, :, WIN * w:WIN * (w + 2)],
                                     start=False, stop=True, skip_group_check=True)
        last.then_inc(s_ps.sem, 1)

    def transpose_probabilities(pe, turn, j):
        exp_sb.wait(pe, turn, j)
        for half in range(2):
            use = ("pT", 2 * j + half)
            wait_room(pe, turn, use)
            for c in range(4):
                hp = 4 * half + c
                src = pr[j % 2][:, 2 * hp:2 * hp + 2, :].rearrange("p a b -> p (a b)")
                last = pe.transpose(narrow_bank(use)[:, c * P:(c + 1) * P], src, ident[:])
            last.then_inc(pT_ps.sem, 1)

    def attend(pe, turn, j):
        wait_room(pe, turn, ("ctx", j))
        dst = wide_slot(("ctx", j))
        v_keys_wait(pe, turn, j)
        for hp in range(HP):
            if hp % 4 == 0:
                pT_sb.wait(pe, turn, 2 * j + hp // 4)
            for w in range(NW):
                last = pe.matmul(dst[WIN * w:WIN * (w + 1), hp * P:(hp + 1) * P],
                                 pT[:, hp, WIN * w:WIN * (w + 1)],
                                 vbd[j % 2][:, w, :, hp * DH:(hp + 1) * DH],
                                 start=True, stop=True)
        last.then_inc(ctx_ps.sem, 1)

    def transpose_context(pe, turn, j):
        ctx_sb.wait(pe, turn, j)
        for half in range(2):
            use = ("cT", 2 * j + half)
            wait_room(pe, turn, use)
            for c in range(4):
                hp = 4 * half + c
                last = pe.transpose(narrow_bank(use)[:, c * P:(c + 1) * P], cn[:, hp * P:(hp + 1) * P], ident[:])
            last.then_inc(cT_ps.sem, 1)

    def project_out(pe, turn, j):
        wait_room(pe, turn, ("o", j))
        for hp in range(HP):
            if hp % 4 == 0:
                cT_sb.wait(pe, turn, 2 * j + hp // 4)
            last = pe.matmul(narrow_bank(("o", j))[:, 0:P], wo[:, hp, :], cT[:, hp, :],
                             start=(hp == 0), stop=(hp == HP - 1))
        last.then_inc(o_ps.sem, 1)

    def tensor_turn(pe, turn, layer, g):
        following = (g + 1) % NG
        loaded = layer + (nth * DEPTH + 1)
        pe.wait_ge(wo_ld, loaded * 16)
        settle(pe)
        for j in range(1, GT):
            n, projected = (j + 1) % GT, turn + (j + 1) // GT
            if j > 1:
                transpose_qk(pe, turn, j, 0)
                if j == GT - 1:
                    pe.wait_ge(wqkv_ld, (layer + (g + 1) // NG) * 16 + (nth * (DEPTH + 1) + 1) * 16)
                    settle(pe)
                    xs_sb.wait(pe, projected, 0)
                project(pe, projected, n, "q")
            transpose_probabilities(pe, turn, j - 1)
            project(pe, projected, n, "k")
            transpose_qk(pe, turn, j, 1)
            attend(pe, turn, j - 1)
            project(pe, projected, n, "v")
            transpose_context(pe, turn, j - 1)
            scores(pe, turn, j)
            project_out(pe, turn, j - 1)
        transpose_qk(pe, turn + 1, 0, 0)
        project(pe, turn + 1, 1, "q")
        transpose_probabilities(pe, turn, GT - 1)
        transpose_qk(pe, turn + 1, 0, 1)
        attend(pe, turn, GT - 1)
        project(pe, turn + 1, 1, "k")
        transpose_context(pe, turn, GT - 1)
        project_out(pe, turn, GT - 1)
        project(pe, turn + 1, 1, "v")
        xf_sb.wait(pe, turn, 0)
        wait_room(pe, turn, ("ln", 0))
        for j in range(GT):
            last = pe.transpose(narrow_bank(("ln", 0))[:, j * P:(j + 1) * P], xf[:, j * P:(j + 1) * P], ident[:])
        last.then_inc(ln_ps.sem, 1)
        scores(pe, turn + 1, 0, masks[:, at((following + (NG - 1)) // NG), :].rearrange("p a n -> p (a n)"))
        xn_sb.wait(pe, turn, 0)
        wait_room(pe, turn, ("xn", 0))
        for j in range(GT):
            last = pe.transpose(narrow_bank(("xn", 0))[:, j * P:(j + 1) * P], xn[:, j, :], ident[:])
        last.then_inc(xn_ps.sem, 1)
        xnT_sb.wait(pe, turn, 0)
        pe.wait_ge(w1_ld, loaded * 16)
        pe.wait_ge(w2_ld, loaded * 48)
        settle(pe)
        for c, (o, m) in enumerate(FCH):
            wait_room(pe, turn, ("ff", c))
            dst = wide_slot(("ff", c))
            pe.matmul(dst[0:m, 0:GW], w1[:, FF + o:FF + o + m], xnT[:], start=True, stop=True)
            pe.matmul(dst[0:m, GW:2 * GW], w1[:, o:o + m], xnT[:], start=True, stop=True) \
                .then_inc(ff_ps.sem, 1)
        transpose_qk(pe, turn + 1, 1, 0)
        project(pe, turn + 1, 2, "q")
        wait_room(pe, turn, ("y", 0))
        for c, (o, m) in enumerate(FCH):
            u_sb.wait(pe, turn, c)
            last = pe.matmul(wide_slot(("y", 0))[:, 0:GW], w2[0:m, c, :], uT[0:m, c, :],
                             start=(c == 0), stop=(c == 2))
        last.then_inc(y_ps.sem, 1)

    def scalar(act):
        for s in (xs_sb, xf_sb, xs_moved, xf_moved, squared, v_sb, qkT_sb, exp_sb, pT_sb, cT_sb, xnT_sb, gelu_sb):
            s.start(act, nth)
        for b in range(4):
            act.wait_ge(t0, 4 * nth + b + 1)
            act.activation(hT[:, 512 * b:512 * b + 512], ps[:, b, :], ACT.Copy).then_inc(h0, 1)
        act.wait_ge(zeroed, nth + 1)
        act.wait_ge(consts, 16 * N_CONSTS * (nth + 1))
        begin, square_of, store_v, store_q, store_k, _, _, exponentials, _ = scalar_steps(act)
        begin(base, 0)
        square_of(base, 0, 0)
        square_of(base, 0, 1)
        store_v(base, 0)
        store_q(base, 0)
        square_of(base, 1, 0)
        store_k(base, 0)
        square_of(base, 1, 1)
        store_v(base, 1)
        exponentials(base, 0)
        store_q(base, 1)
        square_of(base, 2, 0)
        with act.Fori(0, DEPTH) as layer:
            with act.Fori(0, NG) as g:
                scalar_turn(act, base + layer * NG + g, layer, g)

    def scalar_steps(act):
        def shift(turn, group, dst, moved, ready):
            if isinstance(group, int):
                factor, cols = carried[DH:P, group:group + 1], slice(group * GW, (group + 1) * GW)
            else:
                factor, cols = carried[DH:P, bass.ds(group, 1)], bass.ds(group * GW, GW)
            act.activation(dst[DH:P, 0:1], dst[DH:P, GW:GW + 1], ACT.Copy, scale=factor).then_inc(moved.sem, 1)
            moved.wait(act, turn, 0)
            settle(act)
            act.activation(dst[0:DH, 0:GW], hT[0:DH, cols], ACT.Copy)
            act.activation(dst[DH:P, 1:GW + 1], hT[DH:P, cols], ACT.Copy).then_inc(ready.sem, 1)

        def square_of(turn, j, u):
            proj.wait(act, turn, 3 * j + u)
            sums.wait(act, turn, 2 * j + u - 2)
            act.activation(sq[u][:].rearrange("p a b -> p (a b)"), wide_slot(("qk"[u], j)), ACT.Square) \
                .then_inc(squared.sem, 1)

        def store_v(turn, j):
            proj.wait(act, turn, 3 * j + 2)
            v_copied(act, turn, j)
            act.activation(vtok[j % 2][:].rearrange("p a b -> p (a b)"), wide_slot(("v", j)), ACT.Copy) \
                .then_inc(v_sb.sem, 1)

        def store_q(turn, j):
            s_ps.wait(act, turn, j - 1)
            for half in range(2):
                qkT_ps.wait(act, turn, 4 * j + half)
                act.activation(qT[:, 4 * half:4 * half + 4, :].rearrange("p a b -> p (a b)"),
                               narrow_bank(("qT", 2 * j + half)), ACT.Copy).then_inc(qkT_sb.sem, 1)

        def store_k(turn, j):
            s_ps.wait(act, turn, j - 2)
            k_prev.wait(act, turn, j - 1)
            for half in range(2):
                qkT_ps.wait(act, turn, 4 * j + 2 + half)
                for h2 in range(2):
                    rows = slice(DH * h2, DH * h2 + DH)
                    last = act.activation(
                        kT[j % 2][rows, 4 * half:4 * half + 4, h2, WIN:],
                        narrow_bank(("kT", 2 * j + half)).rearrange("p (a b) -> p a b", b=P)[rows], ACT.Copy)
                last.then_inc(qkT_sb.sem, 1)

        def exponentials(turn, j):
            shifted.wait(act, turn, j)
            act.activation(pr[j % 2][:], pr[j % 2][:], ACT.Exp).then_inc(exp_sb.sem, 1)

        def store_probabilities(turn, j):
            ctx_ps.wait(act, turn, j - 1)
            for half in range(2):
                pT_ps.wait(act, turn, 2 * j + half)
                act.activation(pT[:, 4 * half:4 * half + 4, :].rearrange("p a b -> p (a b)"),
                               narrow_bank(("pT", 2 * j + half)), ACT.Copy).then_inc(pT_sb.sem, 1)

        def store_context(turn, j):
            o_ps.wait(act, turn, j - 1)
            for half in range(2):
                cT_ps.wait(act, turn, 2 * j + half)
                act.activation(cT[:, 4 * half:4 * half + 4, :].rearrange("p a b -> p (a b)"),
                               narrow_bank(("cT", 2 * j + half)), ACT.Copy).then_inc(cT_sb.sem, 1)

        def begin(turn, group):
            proj.wait(act, turn, -1)
            x2.wait(act, turn, -2)
            settle(act)
            shift(turn, group, xs, xs_moved, xs_sb)

        def feed_forward_input(turn, group):
            ln_ps.wait(act, turn, -1)
            x1.wait(act, turn, GT - 1)
            settle(act)
            shift(turn, group, xf, xf_moved, xf_sb)

        return (begin, square_of, store_v, store_q, store_k, store_probabilities, store_context,
                exponentials, feed_forward_input)

    def scalar_turn(act, turn, layer, g):
        following = (g + 1) % NG
        (begin, square_of, store_v, store_q, store_k, store_probabilities, store_context,
         exponentials, feed_forward_input) = scalar_steps(act)
        for j in range(1, GT):
            n, projected = (j + 1) % GT, turn + (j + 1) // GT
            if j > 1:
                if j == GT - 1:
                    begin(projected, following)
                store_q(turn, j)
                square_of(projected, n, 0)
            store_probabilities(turn, j - 1)
            square_of(projected, n, 1)
            store_k(turn, j)
            store_v(projected, n)
            store_context(turn, j - 1)
            exponentials(turn, j)
        store_q(turn + 1, 0)
        square_of(turn + 1, 1, 0)
        store_probabilities(turn, GT - 1)
        store_k(turn + 1, 0)
        square_of(turn + 1, 1, 1)
        store_context(turn, GT - 1)
        feed_forward_input(turn, g)
        store_v(turn + 1, 1)
        vec = lambda c, m=P: vecs[0:m, bass.ds(layer, 1), c]
        xn_ps.wait(act, turn, 0)
        ff_ps.wait(act, turn, -1)
        settle(act)
        act.activation(xnT[:], narrow_bank(("xn", 0)), ACT.Identity, scale=vec(0), bias=vec(1)) \
            .then_inc(xnT_sb.sem, 1)
        exponentials(turn + 1, 0)
        for c, (o, m) in enumerate(FCH):
            ff_ps.wait(act, turn, c)
            u_sb.wait(act, turn, (-1, -2, 0)[c])
            settle(act)
            act.activation(gl[0:m, c % 2, :], wide_slot(("ff", c))[0:m, 0:GW], ACT.Gelu, bias=vec(6 + c, m)) \
                .then_inc(gelu_sb.sem, 1)
        store_q(turn + 1, 1)
        square_of(turn + 1, 2, 0)

    def v_copied(eng, turn, j):
        if j >= 1:
            v_keys_wait(eng, turn, j - 1)
        if j == 0:
            for a in range(2):
                eng.wait_ge(v_keys[a], turn * V_TURN + 1)
        if j == 1:
            eng.wait_ge(v_keys[1], turn * V_TURN + 1)

    def vector(v):
        for s in (prod_sb, sums, normed, maxed, shifted, summed, inverted, ctx_sb, x1, bn_done, mv_done,
                  xn_sb, u_sb, x2):
            s.start(v, nth)
        v.wait_ge(x_ready, 1)
        layernorm_vector(v, chain, var0, rstd0, xtok[:], lnx, lnsq, small, nth=nth + 1)
        v.sem_inc(n0, 1)
        v.wait_ge(t0, 4 * nth + 4)
        chain.add(v.memset(carried[:], 1.0))
        chain.wait(v)
        v.memset(carried[:, 0:1], 0.0)
        v.memset(xs[:], 0.0)
        v.memset(xf[:], 0.0)
        v.memset(gains[:, DEPTH], 1.0)
        v.wait_ge(consts, 16 * N_CONSTS * (nth + 1))
        v.tensor_copy(identb[:], ident[:])
        for i in range(2):
            v.tensor_copy(masks[:, i, :].rearrange("p (a c) -> p a c", c=2 * WIN),
                          mask32[:, i:i + 1, :].broadcast_to([P, 8, 2 * WIN]))
        for buf in (vtok[0], vtok[1], vbd[0], vbd[1], kT[0], kT[1]):
            last = v.memset(buf[:], 0.0)
        last.then_inc(zeroed, 1)
        v.wait_ge(h0, 4 * nth + 4)
        v.wait_ge(consts, 16 * N_CONSTS * (nth + 1))
        vector_first_tiles(v)
        with v.Fori(0, DEPTH) as layer:
            with v.Fori(0, NG) as g:
                vector_turn(v, base + layer * NG + g, layer, g)
        exp_sb.wait(v, end, 0)
        k_prev.wait(v, end, 1)
        rotated.wait(v, end, 4)
        rinv.wait(v, end, 4)
        qkT_sb.wait(v, end, 5)
        for a in range(2):
            v_keys_wait(v, end, a)
        for b in range(4):
            v.wait_ge(back_ps, 4 * nth + b + 1)
            x4 = xtok[:, 4 * b:4 * b + 4, :].rearrange("p a c -> p (a c)")
            chain.add(v.tensor_tensor(x4, x4, ps[:, b, :], ALU.add))
        chain.wait(v)
        v.sem_inc(x_next, 1)

    def vector_steps(v):
        def products(turn, j, u):
            tab_sb.wait(v, turn, j)
            proj.wait(v, turn, 3 * j + u)
            rotated.wait(v, turn, 2 * j + u - 2)
            squared.wait(v, turn, 2 * j + u)
            src = wide_slot(("qk"[u], j)).rearrange("p (h c) -> p h c", c=DH)
            v.tensor_tensor(prod[u][:], src.unsqueeze(2).broadcast_to([P, H, 2, DH]),
                            tab[j % 2][:, u].unsqueeze(1).broadcast_to([P, H, 2, DH]), ALU.mult) \
                .then_inc(prod_sb.sem, 1)

        def norms(turn, j, u):
            rinv.wait(v, turn, 2 * j + u - 4)
            v.tensor_reduce(stat[:, j % 2, u, :], sq[u][:], axis=AX.X, op=ALU.add).then_inc(sums.sem, 1)

        def normalise(turn, j, u):
            rotated.wait(v, turn, 2 * j + u)
            rinv.wait(v, turn, 2 * j + u)
            buf = qk[j % 2][u]
            v.tensor_tensor(buf[:], buf[:], stat[:, j % 2, u, :].unsqueeze(2).broadcast_to([P, H, DH]),
                            ALU.mult).then_inc(normed.sem, 1)

        def softmax(turn, j):
            src = wide_slot(("s", j)).rearrange("p (h c) -> p h c", c=2 * WIN)
            s_ps.wait(v, turn, j)
            v.tensor_reduce(mx[:], src, axis=AX.X, op=ALU.max).then_inc(maxed.sem, 1)
            maxed.wait(v, turn, j)
            pT_ps.wait(v, turn, 2 * j - 3)
            v.tensor_tensor(pr[j % 2][:], src, mx[:].unsqueeze(2).broadcast_to([P, H, 2 * WIN]),
                            ALU.subtract).then_inc(shifted.sem, 1)

        def sum_up(turn, j):
            exp_sb.wait(v, turn, j)
            v.tensor_reduce(rs[j % 2][:], pr[j % 2][:], axis=AX.X, op=ALU.add).then_inc(summed.sem, 1)
            summed.wait(v, turn, j)
            v.reciprocal(rs[j % 2][:], rs[j % 2][:]).then_inc(inverted.sem, 1)

        def divide(turn, j):
            ctx_ps.wait(v, turn, j)
            cT_ps.wait(v, turn, 2 * j - 1)
            inverted.wait(v, turn, j)
            v.tensor_tensor(cn[:].rearrange("p (h c) -> p h c", c=DH),
                            wide_slot(("ctx", j)).rearrange("p (h c) -> p h c", c=DH),
                            rs[j % 2][:].unsqueeze(2).broadcast_to([P, H, DH]), ALU.mult) \
                .then_inc(ctx_sb.sem, 1)

        return products, norms, normalise, softmax, sum_up, divide

    def vector_first_tiles(v):
        products, norms, normalise, softmax, sum_up, _ = vector_steps(v)
        for j in range(2):
            for u in range(2):
                products(base, j, u)
                norms(base, j, u)
            for u in range(2):
                normalise(base, j, u)
        softmax(base, 0)
        sum_up(base, 0)
        products(base, 2, 0)
        norms(base, 2, 0)

    def vector_turn(v, turn, layer, g):
        vec = lambda c, m=P: vecs[0:m, bass.ds(layer, 1), c]
        products, norms, normalise, softmax, sum_up, divide = vector_steps(v)

        def add_attention(j):
            o_ps.wait(v, turn, j)
            if j == 0:
                xs_sb.wait(v, turn, 0)
            at = hT[:, bass.ds(g * GW + j * P, P)]
            v.tensor_tensor(at, at, narrow_bank(("o", j))[:, 0:P], ALU.add).then_inc(x1.sem, 1)

        for j in range(1, GT):
            n, projected = (j + 1) % GT, turn + (j + 1) // GT
            if j > 1:
                products(projected, n, 0)
                norms(projected, n, 0)
            products(projected, n, 1)
            divide(turn, j - 1)
            norms(projected, n, 1)
            normalise(projected, n, 0)
            softmax(turn, j)
            add_attention(j - 1)
            normalise(projected, n, 1)
            sum_up(turn, j)
        products(turn + 1, 1, 0)
        norms(turn + 1, 1, 0)
        divide(turn, GT - 1)
        products(turn + 1, 1, 1)
        add_attention(GT - 1)
        norms(turn + 1, 1, 1)
        ln_ps.wait(v, turn, 0)
        bank = narrow_bank(("ln", 0)).rearrange("p (t c) -> p t c", c=P)
        for j in range(GT):
            last = v.bn_stats(bn[:, j, :], bank[:, j, :])
        last.then_inc(bn_done.sem, 1)
        bn_done.wait(v, turn, 0)
        settle(v)
        for j in range(GT):
            last = v.bn_aggr(mv[:, j, :], bn[:, j, :])
        last.then_inc(mv_done.sem, 1)
        rstd_sb.wait(v, turn, 0)
        mv_done.wait(v, turn, 0)
        for j in range(GT):
            last = v.tensor_scalar(xn[:, j, :], bank[:, j, :], mv[:, j, 0:1], rstd[:, j:j + 1],
                                   ALU.subtract, ALU.mult)
        last.then_inc(xn_sb.sem, 1)
        softmax(turn + 1, 0)
        normalise(turn + 1, 1, 0)
        normalise(turn + 1, 1, 1)
        sum_up(turn + 1, 0)
        for c, (o, m) in enumerate(FCH):
            gelu_sb.wait(v, turn, c)
            y_ps.wait(v, turn, -1)
            v.scalar_tensor_tensor(uT[0:m, c, :], wide_slot(("ff", c))[0:m, GW:2 * GW], vec(3 + c, m),
                                   gl[0:m, c % 2, :], ALU.add, ALU.mult).then_inc(u_sb.sem, 1)
        products(turn + 1, 2, 0)
        norms(turn + 1, 2, 0)
        y_ps.wait(v, turn, 0)
        xf_sb.wait(v, turn, 0)
        at = hT[:, bass.ds(g * GW, GW)]
        v.scalar_tensor_tensor(at, wide_slot(("y", 0))[:, 0:GW], vec(2), at, ALU.add, ALU.add) \
            .then_inc(x2.sem, 1)

    def gpsimd(pool):
        for s in (tab_sb, clamped, rinv, rotated, k_prev, rstd_a, rstd_sb):
            s.start(pool, nth)
        layernorm_gpsimd(pool, var0, rstd0, small, minus_half, nth + 1)
        pool.wait_ge(zeroed, nth + 1)
        pool.wait_ge(consts, 16 * N_CONSTS * (nth + 1))
        pool.wait_ge(h0, 4 * nth + 4)
        tables(pool, base, 0, 0, 0)
        for u in range(2):
            rotate(pool, base, 0, u)
        tables(pool, base, 0, 0, 1)
        previous_keys(pool, base, 0)
        for u in range(2):
            rotate(pool, base, 1, u)
        tables(pool, base, 0, 0, 2)
        previous_keys(pool, base, 1)
        rotate(pool, base, 2, 0)
        with pool.Fori(0, DEPTH) as layer:
            with pool.Fori(0, NG) as g:
                gpsimd_turn(pool, base + layer * NG + g, layer, g)

    def tables(pool, turn, layer, group, j):
        prod_sb.wait(pool, turn, 2 * j - 3)
        settle(pool)
        pool.tensor_tensor(tab[j % 2][:].rearrange("p u s c -> p (u s) c"),
                           tabs[:, at(group * GT + j), :, :, :].rearrange("p t u s c -> p (t u s) c"),
                           gains[:, at(layer), :, :].rearrange("p l u c -> p (l u) c")
                           .unsqueeze(2).broadcast_to([P, 2, 2, DH]), ALU.mult).then_inc(tab_sb.sem, 1)

    def rotate(pool, turn, j, u):
        half = DH // 2
        dst, src = qk[j % 2][u], prod[u]
        prod_sb.wait(pool, turn, 2 * j + u)
        qkT_ps.wait(pool, turn, 4 * (j - 2) + 2 * u + 1)
        pool.tensor_tensor(dst[:, :, 0:half], src[:, :, 0, 0:half], src[:, :, 1, half:], ALU.add)
        pool.tensor_tensor(dst[:, :, half:], src[:, :, 0, half:], src[:, :, 1, 0:half], ALU.add) \
            .then_inc(rotated.sem, 1)
        st = stat[:, j % 2, u, :]
        sums.wait(pool, turn, 2 * j + u)
        settle(pool)
        pool.tensor_scalar(st, st, 1e-24, None, ALU.max).then_inc(clamped.sem, 1)
        clamped.wait(pool, turn, 2 * j + u)
        pool.tensor_tensor(st, st, minus_half[:, 0:H], ALU.pow).then_inc(rinv.sem, 1)

    def previous_keys(pool, turn, j):
        qkT_sb.wait(pool, turn, 4 * j - 1)
        s_ps.wait(pool, turn, j - 2)
        settle(pool)
        pool.tensor_scalar(kT[j % 2][:, :, :, 0:WIN], kT[1 - j % 2][:, :, :, P:P + WIN], decay[:, 0:1],
                           None, ALU.mult).then_inc(k_prev.sem, 1)

    def gpsimd_turn(pool, turn, layer, g):
        following, following_layer = (g + 1) % NG, layer + ((g + 1) // NG)
        for j in range(1, GT):
            if j == GT - 1:
                tables(pool, turn + 1, following_layer, following, 0)
            elif j > 1:
                tables(pool, turn, layer, g, j + 1)
            projected = turn + (j + 1) // GT
            if j > 1:
                previous_keys(pool, turn, j)
                rotate(pool, projected, (j + 1) % GT, 0)
            rotate(pool, projected, (j + 1) % GT, 1)
        tables(pool, turn + 1, following_layer, following, 1)
        previous_keys(pool, turn + 1, 0)
        rotate(pool, turn + 1, 1, 0)
        mv_done.wait(pool, turn, 0)
        settle(pool)
        pool.tensor_scalar(rstd[:], mv[:, :, 1], 1e-5, None, ALU.add).then_inc(rstd_a.sem, 1)
        rstd_a.wait(pool, turn, 0)
        pool.tensor_tensor(rstd[:], rstd[:], minus_half[:, 0:GT], ALU.pow).then_inc(rstd_sb.sem, 1)
        rotate(pool, turn + 1, 1, 1)
        tables(pool, turn + 1, following_layer, following, 2)
        previous_keys(pool, turn + 1, 1)
        rotate(pool, turn + 1, 2, 0)

    N_CONSTS = 3 + 2 + 3 + 6
    add_phase(sync=sync, tensor=tensor, scalar=scalar, vector=vector, gpsimd=gpsimd)


def build_full_attention(nc, settle, ps, xtok, ident, minus_half, small, d, sem, add_phase, x_ready, x_next):
    NS, NU = NT, 2 * NT
    NKB = T // 512
    QG = 4
    with ExitStack() as mem:
        def sb(name, shape, dt=F32):
            return mem.enter_context(nc.sbuf_tensor("b_" + name, shape, dt))

        xT = sb("xT", [P, T])
        w = [sb(f"w{i}", [P, 3, P]) for i in range(2)]
        wo = sb("wo", [P, H, P])
        qkv = sb("qkv", [P, NT, 3 * P])
        q2 = sb("q2", [P, T], F32R)
        k_hi = sb("k_hi", [P, T], F32R)
        k_lo = sb("k_lo", [P, T], F32R)
        both = sb("both", [P, 2, NT, P])
        twice = [both[:, i] for i in range(2)]
        square = both[:].rearrange("p u t c -> p (u t c)").rearrange("p (t c) -> p t c", c=2 * P)
        gam = sb("gam", [P, 2, H])
        lnv = sb("lnv", [P, 2])
        pr = [sb(f"pr{i}", [P, T]) for i in range(2)]
        v2 = sb("v2", [P, NT, 2, 2, DH], F32R)
        p_hi = sb("p_hi", [P, NT, QG, P], F32R)
        p_lo = sb("p_lo", [P, NT, QG, P], F32R)
        mx = sb("mx", [P, 2, NKB])
        nm = sb("nm", [P, 2])
        rs = sb("rs", [P, 2, QG, NKB])
        ri = sb("ri", [P, 2, 2, QG])
        cT = sb("cT", [P, QG * P])
        y = sb("y", [P, NT, P])
        ssq = sb("ssq", [P, 4 * NT])
        rinv = sb("rinv", [P, 4 * NT])
        half = sb("half", [P, 4 * NT])
        lnx = qkv[:].rearrange("p t c -> p (t c)")[:, 0:T].rearrange("p (t c) -> p t c", c=P)
        lnsq = twice[0]

    chain = Chain(sem("b_dve"))
    var1, rstd1, var2, rstd2 = (sem(f"b_norm{i}") for i in range(4))
    normed, xT_ps, xT_sb = sem("b_normed"), sem("b_xT_ps"), sem("b_xT_sb")
    consts, half_set, gam_set = sem("b_consts"), sem("b_half"), sem("b_gam")
    w_ld = [sem(f"b_w_ld{i}") for i in range(2)]
    qkv_ps, qkv_sb = sem("b_qkv_ps"), sem("b_qkv_sb")
    squared, ss_sb, rinv_sb, qk_sb = (sem(f"b_{n}") for n in ("squared", "ss", "rinv", "qk"))
    dup_ps, hi_sb, lo_sb = sem("b_dup_ps"), sem("b_hi_sb"), sem("b_lo_sb")
    s_ps, bank_max, neg_max, exp_sb = (sem(f"b_{n}") for n in ("s_ps", "bank_max", "neg_max", "exp"))
    pT_ps, p_hi_sb, p_lo_sb, c_sb, o_ps, y_sb = (sem(f"b_{n}") for n in
                                                      ("pT_ps", "p_hi", "p_lo", "c_sb", "o_ps", "y"))
    v_hi, v_lo, pv_kt = sem("b_v_hi"), sem("b_v_lo"), sem("b_pv")
    rsum, rrec, y_zero = sem("b_rsum"), sem("b_rrec"), sem("b_y_zero")
    N_CONSTS = 8

    def sync(sp):
        sp.wait_ge(x_ready, 1)
        for h2 in range(2):
            sp.dma_start(wo[DH * h2:DH * h2 + DH, :, :], d["b_Wo"].rearrange("(h c) n -> c h n", c=DH)) \
                .then_inc(consts, 16)
        for u, name in enumerate(("b_q_gamma", "b_k_gamma")):
            for h2 in range(2):
                sp.dma_start(gam[DH * h2:DH * h2 + DH, u, :], d[name].rearrange("h c -> c h"),
                             allow_slow_non_contiguous=True).then_inc(consts, 16)
        for c, name in enumerate(("b_ln_w", "b_ln_b")):
            sp.dma_start(lnv[:, c:c + 1], d[name].rearrange("(p a) -> p a", a=1)).then_inc(consts, 16)
        for hp in range(HP):
            if hp >= 2:
                sp.wait_ge(qkv_ps, NT * (hp - 1))
            for u in range(3):
                src = d["b_Wq"][:, hp * P:(hp + 1) * P] if u == 0 else \
                    d["b_Wkv"][:, (u - 1) * INNER + hp * P:(u - 1) * INNER + (hp + 1) * P]
                sp.dma_start(w[hp % 2][:, u, :], src).then_inc(w_ld[hp % 2], 16)

    def tensor(pe):
        for s in (dup_ps, o_ps):
            pe.sem_inc(s, 1)
        pe.sem_inc(pv_kt, 1 + NKB)
        pe.wait_ge(normed, 1)
        transpose_tiles(pe, ps, lambda t: lnx[:, t, :], ident, range(4), xT_ps)
        pe.wait_ge(xT_sb, 4)
        pe.wait_ge(consts, 16 * N_CONSTS)
        with pe.Fori(0, HP // 2) as hq:
            for e in range(2):
                pe.wait_ge(w_ld[e], hq * 48 + 48)
                tensor_pair(pe, 2 * hq + e, e)

    def tensor_pair(pe, hp, parity):
        pe.wait_ge(y_sb, 1 + hp * NU)
        for t in range(NT):
            if t >= 4:
                pe.wait_ge(qkv_sb, 1 + hp * NT + (t - 3))
            pe.matmul(ps[:, t % 4, 0:3 * P], xT[:, t * P:(t + 1) * P],
                      w[parity][:].rearrange("p u c -> p (u c)"), start=True, stop=True).then_inc(qkv_ps, 1)
        for h2 in range(2):
            n = 0
            if h2:
                pe.wait_ge(y_sb, 1 + hp * NU + NT)
            for u in range(2):
                pe.wait_ge(qk_sb, 1 + hp * 4 + 2 * h2 + u + 1)
                for b in range(4):
                    if u:
                        pe.wait_ge(lo_sb, hp * 16 + 8 * h2 + b + 1)
                    for k in range(4):
                        t = 4 * b + k
                        last = pe.transpose(ps[:, b, k * P:(k + 1) * P], twice[u][:, t, :], ident[:])
                    last.then_inc(dup_ps, 1)
            pe.wait_ge(lo_sb, hp * 16 + 8 * h2 + 8)
            pe.wait_ge(v_lo, hp + 1)
            for i in range(NT + 1):
                if i < NT:
                    score_unit(pe, hp, h2, i)
                if i:
                    transpose_unit(pe, hp, h2, i - 1)
                if i and i % QG == 0:
                    attend_group(pe, hp, h2, i // QG - 1)

    def unit(hp, h2, i):
        return hp * NU + (h2 * NT + i)

    def score_unit(pe, hp, h2, i):
        un = unit(hp, h2, i)
        for b in range(NKB):
            if i:
                pe.wait_ge(exp_sb, (un - 1) * NKB + b + 1)
            pe.matmul(ps[:, b, :], q2[:, i * P:(i + 1) * P], k_hi[:, 512 * b:512 * b + 512],
                      start=True, stop=False)
            pe.matmul(ps[:, b, :], q2[:, i * P:(i + 1) * P], k_lo[:, 512 * b:512 * b + 512],
                      start=False, stop=True).then_inc(s_ps, 1)

    def transpose_unit(pe, hp, h2, i):
        un = unit(hp, h2, i)
        for b in range(NKB):
            pe.wait_ge(exp_sb, un * NKB + b + 1)
            pe.wait_ge(p_lo_sb, un * NKB + b)
            for k in range(4):
                last = pe.transpose(ps[:, 4 + b % 2, k * P:(k + 1) * P],
                                    pr[i % 2][:, (4 * b + k) * P:(4 * b + k + 1) * P], ident[:])
            last.then_inc(pT_ps, 1)

    def group(hp, h2, q):
        return hp * (NU // QG) + (h2 * (NT // QG) + q)

    def attend_group(pe, hp, h2, q):
        gn = group(hp, h2, q)
        pe.wait_ge(c_sb, 1 + gn)
        for b in range(NKB):
            pe.wait_ge(p_lo_sb, 1 + unit(hp, h2, QG * q + QG - 1) * NKB + b + 1)
            for k in range(4):
                t = 4 * b + k
                for part in (p_hi, p_lo):
                    last = pe.matmul(ps[:, 6, :], v2[:, t, h2].rearrange("p r c -> p (r c)"),
                                     part[:, t].rearrange("p a b -> p (a b)"),
                                     start=(t == 0 and part is p_hi), stop=(t == NT - 1 and part is p_lo))
            last.then_inc(pv_kt, 1)
        pe.wait_ge(c_sb, 1 + gn + 1)
        pe.wait_ge(y_sb, 1 + unit(hp, h2, QG * q))
        settle(pe)
        for r in range(QG):
            last = pe.matmul(ps[:, 7, r * P:(r + 1) * P], cT[:, r * P:(r + 1) * P],
                             wo[:, bass.ds(2 * hp + h2, 1), :].rearrange("p a n -> p (a n)"),
                             start=True, stop=True)
        last.then_inc(o_ps, 1)

    def scalar(act):
        for s in (qkv_sb, c_sb):
            act.sem_inc(s, 1)
        act.wait_ge(consts, 16 * N_CONSTS)
        for b in range(4):
            act.wait_ge(xT_ps, b + 1)
            act.activation(xT[:, 512 * b:512 * b + 512], ps[:, b, :], ACT.Identity, scale=lnv[:, 0:1],
                           bias=lnv[:, 1:2]).then_inc(xT_sb, 1)
        act.wait_ge(gam_set, 1)
        with act.Fori(0, HP) as hp:
            for t in range(NT):
                act.wait_ge(qkv_ps, hp * NT + t + 1)
                act.activation(qkv[:, t, :], ps[:, t % 4, 0:3 * P], ACT.Copy).then_inc(qkv_sb, 1)
            act.wait_ge(qkv_sb, 1 + hp * NT + NT)
            act.wait_ge(ss_sb, 1 + hp)
            act.wait_ge(dup_ps, 1 + hp * 16)
            act.activation(square, qkv[:, :, 0:2 * P], ACT.Square).then_inc(squared, 1)
            act.activation(v2[:, :, :, 0, :], qkv[:, :, 2 * P:].rearrange("p t (h c) -> p t h c", c=DH),
                           ACT.Copy).then_inc(v_hi, 1)
            for h2 in range(2):
                for u in range(2):
                    dst = q2 if u == 0 else k_hi
                    for b in range(4):
                        act.wait_ge(dup_ps, 1 + hp * 16 + 8 * h2 + 4 * u + b + 1)
                        settle(act)
                        act.activation(dst[:, 512 * b:512 * b + 512], ps[:, b, :], ACT.Copy,
                                       scale=gain(u, hp, h2)).then_inc(hi_sb, 1)
                for i in range(NT + 1):
                    if i:
                        high_parts(act, hp, h2, i - 1, (0, 1))
                    if i < NT:
                        un = unit(hp, h2, i)
                        act.wait_ge(neg_max, un + 1)
                        if i >= 2:
                            act.wait_ge(pT_ps, (un - 1) * NKB)
                    for b in range(NKB):
                        if i < NT:
                            act.activation(pr[i % 2][:, 512 * b:512 * b + 512], ps[:, b, :], ACT.Exp,
                                           bias=nm[:, i % 2:i % 2 + 1],
                                           accum_out=rs[:, i // QG % 2, i % QG, b:b + 1]).then_inc(exp_sb, 1)
                        if i and b in (1, 2):
                            high_parts(act, hp, h2, i - 1, (b + 1,))
                    if i and i % QG == 0:
                        gn = group(hp, h2, i // QG - 1)
                        act.wait_ge(pv_kt, 1 + (gn + 2) * NKB)
                        act.activation(cT[:], ps[:, 6, :], ACT.Copy).then_inc(c_sb, 1)

    def high_parts(act, hp, h2, i, banks):
        un = unit(hp, h2, i)
        for b in banks:
            act.wait_ge(pT_ps, un * NKB + b + 1)
            act.wait_ge(pv_kt, 1 + group(hp, h2, i // QG) * NKB + b + 1)
            act.activation(p_hi[:, 4 * b:4 * b + 4, i % QG, :],
                           ps[:, 4 + b % 2, :].rearrange("p (a c) -> p a c", c=P), ACT.Copy) \
                .then_inc(p_hi_sb, 1)

    def gain(u, hp, h2, rows=slice(0, P)):
        return gam[rows, u, bass.ds(2 * hp + h2, 1)]

    def vector(v):
        for s in (ss_sb, y_sb, qk_sb, p_lo_sb):
            v.sem_inc(s, 1)
        v.wait_ge(x_ready, 1)
        layernorm_vector(v, chain, var1, rstd1, xtok[:], lnx, lnsq, small)
        layernorm_vector(v, chain, var2, rstd2, lnx, lnx, lnsq, small)
        v.sem_inc(normed, 1)
        v.memset(y[:], 0.0).then_inc(y_zero, 1)
        v.memset(half[:], -0.5).then_inc(half_set, 1)
        v.wait_ge(consts, 16 * N_CONSTS)
        v.tensor_scalar(gam[:], gam[:], 8.0, None, ALU.mult).then_inc(gam_set, 1)
        v.wait_ge(gam_set, 1)
        with v.Fori(0, HP) as hp:
            v.wait_ge(squared, hp + 1)
            chain_ss = v.tensor_reduce(ssq[:], square.rearrange("p t (h c) -> p (t h) c", c=DH),
                                       axis=AX.X, op=ALU.add)
            chain_ss.then_inc(rsum, 1)
            v.wait_ge(rsum, hp * (NU // QG + 1) + 1)
            v.tensor_scalar(ssq[:], ssq[:], 1.0 / DH, 1e-8, ALU.mult, ALU.add).then_inc(ss_sb, 1)
            v.wait_ge(v_hi, hp + 1)
            v.tensor_tensor(v2[:, :, :, 1, :], qkv[:, :, 2 * P:].rearrange("p t (h c) -> p t h c", c=DH),
                            v2[:, :, :, 0, :].bitcast(F32), ALU.subtract).then_inc(v_lo, 1)
            v.wait_ge(rinv_sb, hp + 1)
            for h2 in range(2):
                for u in range(2):
                    v.wait_ge(dup_ps, 1 + hp * 16 + max(8 * (h2 - 1) + 4 * u + 4, 0))
                    at = u * P + DH * h2
                    v.tensor_tensor(
                        twice[u].rearrange("p t (r c) -> p t r c", c=DH),
                        qkv[:, :, at:at + DH].unsqueeze(2).broadcast_to([P, NT, 2, DH]),
                        rinv[:].rearrange("p (t s) -> p t s", s=4)[:, :, 2 * u + h2:2 * u + h2 + 1]
                        .unsqueeze(3).broadcast_to([P, NT, 2, DH]), ALU.mult).then_inc(qk_sb, 1)
                for u in range(2):
                    for b in range(4):
                        v.wait_ge(hi_sb, hp * 16 + 8 * h2 + 4 * u + b + 1)
                        rows = slice(DH, P) if u == 0 else slice(0, P)
                        hi, lo = (q2, q2) if u == 0 else (k_hi, k_lo)
                        cols = slice(512 * b, 512 * b + 512)
                        v.scalar_tensor_tensor(lo[rows, cols], ps[rows, b, :], gain(u, hp, h2, rows),
                                               hi[rows, cols].bitcast(F32), ALU.mult, ALU.subtract) \
                            .then_inc(lo_sb, 1)
                for i in range(NT + 1):
                    if i < NT:
                        un = unit(hp, h2, i)
                        for b in range(NKB):
                            v.wait_ge(s_ps, un * NKB + b + 1)
                            v.tensor_reduce(mx[:, i % 2, b:b + 1], ps[:, b, :], axis=AX.X, op=ALU.max) \
                                .then_inc(bank_max, 1)
                        v.wait_ge(bank_max, un * NKB + NKB)
                        if i >= 2:
                            v.wait_ge(exp_sb, (un - 1) * NKB)
                        v.tensor_reduce(nm[:, i % 2:i % 2 + 1], mx[:, i % 2, :], axis=AX.X, op=ALU.max,
                                        negate=True).then_inc(neg_max, 1)
                    if i:
                        un = unit(hp, h2, i - 1)
                        for b in range(NKB):
                            v.wait_ge(p_hi_sb, un * NKB + b + 1)
                            at = (slice(None), slice(4 * b, 4 * b + 4), (i - 1) % QG)
                            v.tensor_tensor(p_lo[at], ps[:, 4 + b % 2, :].rearrange("p (a c) -> p a c", c=P),
                                            p_hi[at].bitcast(F32), ALU.subtract).then_inc(p_lo_sb, 1)
                    if i and i % QG == 0:
                        q = i // QG - 1
                        gn = group(hp, h2, q)
                        sums, inverse = ri[:, q % 2, 0, :], ri[:, q % 2, 1, :]
                        v.tensor_reduce(sums, rs[:, q % 2], axis=AX.X, op=ALU.add).then_inc(rsum, 1)
                        v.wait_ge(rsum, hp * (NU // QG + 1) + (h2 * (NT // QG) + q + 2))
                        v.reciprocal(inverse, sums).then_inc(rrec, 1)
                        v.wait_ge(rrec, gn + 1)
                        v.wait_ge(o_ps, 1 + gn + 1)
                        for r in range(QG):
                            t = QG * q + r
                            v.scalar_tensor_tensor(y[:, t, :], ps[:, 7, r * P:(r + 1) * P], inverse[:, r:r + 1],
                                                   y[:, t, :], ALU.mult, ALU.add).then_inc(y_sb, 1)
        v.wait_ge(y_sb, 1 + HP * NU)
        chain.add(v.tensor_tensor(xtok[:], xtok[:], y[:], ALU.add))
        chain.wait(v)
        v.sem_inc(x_next, 1)

    def gpsimd(pool):
        layernorm_gpsimd(pool, var1, rstd1, small, minus_half)
        layernorm_gpsimd(pool, var2, rstd2, small, minus_half)
        pool.wait_ge(half_set, 1)
        with pool.Fori(0, HP) as hp:
            pool.wait_ge(ss_sb, 1 + hp + 1)
            pool.wait_ge(qk_sb, 1 + hp * 4)
            pool.tensor_tensor(rinv[:], ssq[:], half[:], ALU.pow).then_inc(rinv_sb, 1)

    add_phase(sync=sync, tensor=tensor, scalar=scalar, vector=vector, gpsimd=gpsimd)


def shape_constants():
    half = np.arange(0, DH, 2, dtype=np.float32)
    inv_freq = (1.0 / np.float32(10000.0) ** (half / np.float32(DH))).astype(np.float32)
    t = np.arange(T, dtype=np.float32)
    freqs = (t[:, None] * inv_freq[None, :]).astype(np.float32)
    cos, sin = np.cos(freqs.astype(np.float64)), np.sin(freqs.astype(np.float64))
    base = ((half + np.float32(0.4 * DH)) / np.float32(1.4 * DH)).astype(np.float64)
    power = (np.arange(T) % P - P // 2) / (WIN // 2)
    scale = base[None, :] ** power[:, None]
    tabs = np.zeros((T, 2, 2, DH))
    for u, s in enumerate((8.0 * scale, 1.0 / scale)):
        tabs[:, u, 0, :] = np.concatenate([cos * s, cos * s], -1)
        tabs[:, u, 1, :] = np.concatenate([sin * s, -sin * s], -1)
    tabs = tabs.reshape(NT, P, 2, 2, DH).transpose(1, 0, 2, 3, 4).astype(np.float32)
    i = np.arange(P) % WIN
    key = np.arange(2 * WIN)[None, :] - WIN
    masked = (key > i[:, None]) | (key < i[:, None] - WIN)
    general = np.where(masked, NEG, 0.0)
    first = np.where(masked | ((np.arange(P)[:, None] < WIN) & (key < 0)), NEG, 0.0)
    masks = np.stack([first, general], 1)
    decay = np.tile(np.concatenate([base, base]) ** (P / (WIN // 2)), 2)[:, None]
    return {
        "tabs": tabs, "masks": masks.astype(np.float32), "decay": decay.astype(np.float32),
        "ident": np.eye(P, dtype=np.float32),
    }


def kernel(**inputs):
    import concourse.bacc as bacc
    from concourse.bass_utils import run_bass_kernel_spmd as run

    a = {k.removeprefix("L0_"): np.asarray(v) for k, v in inputs.items()}
    arrays = {
        "x": a["attn_a_x"].reshape(T, P),
        "hawk_gamma": a["attn_a_hawk_norm_gamma"], "gmlp_gamma": a["attn_a_gmlp_norm_gamma"],
        "input_wT": a["attn_a_input_w"].T, "gates_wT": a["attn_a_gates_w"].T,
        "output_wT": a["attn_a_output_w"].T, "grow_wT": a["attn_a_grow_w"].T,
        "shrink_wT": a["attn_a_shrink_w"].T,
        "conv_w": a["attn_a_conv_w"].reshape(P, 4), "conv_b": a["attn_a_conv_b"],
        "gates_b": a["attn_a_gates_b"], "forget_base": a["attn_a_forget_base"],
        "b_ln_w": a["attn_b_ln_w"], "b_ln_b": a["attn_b_ln_b"], "b_Wq": a["attn_b_Wq"],
        "b_Wkv": a["attn_b_Wkv"], "b_q_gamma": a["attn_b_q_gamma"].reshape(H, DH),
        "b_k_gamma": a["attn_b_k_gamma"].reshape(H, DH), "b_Wo": a["attn_b_Wo"],
        "Wqkv": a["ffn_Wqkv"], "q_scale": a["ffn_q_scale"], "k_scale": a["ffn_k_scale"],
        "Wo": a["ffn_Wo"], "ln_g": a["ffn_ln_g"], "ln_b": a["ffn_ln_b"], "W1": a["ffn_W1"],
        "b1": a["ffn_b1"], "W2": a["ffn_W2"], "b2": a["ffn_b2"],
    }
    arrays.update(shape_constants())
    arrays = {k: np.ascontiguousarray(v) for k, v in arrays.items()}
    nc = bacc.Bacc("TRN2", target_bir_lowering=False, num_devices=1)
    d = {k: nc.dram_tensor("in_" + k, v.shape, mybir.dt.from_np(v.dtype), kind="ExternalInput").ap()
         for k, v in arrays.items()}
    out = nc.dram_tensor("out", (T, P), F32, kind="ExternalOutput").ap()
    build_program(nc, d, out)
    r = run(nc, [{"in_" + k: v for k, v in arrays.items()}], core_ids=[0])
    return r.results[0]["out"].reshape(1, T, P)
```

```python
from contextlib import ExitStack

import numpy as np
import concourse.bass as bass
from concourse import mybir

ALU = mybir.AluOpType
ACT = mybir.ActivationFunctionType
AX = mybir.AxisListType
F32 = mybir.dt.float32
F32R = mybir.dt.float32r
BF16 = mybir.dt.bfloat16

P = 128
T = 2048
NT = T // P
H = 16
DH = 64
HP = H // 2
INNER = H * DH
WIN = 32
NW = P // WIN
DEPTH = 6
GT = 4
GW = GT * P
NG = T // GW
FF = 341
FCH = [(0, 128), (128, 128), (256, 85)]
NEG = -1e30


class Signal:

    def __init__(self, sem, per_group, early=0):
        self.sem, self.per_group, self.early = sem, per_group, early

    def start(self, eng, nth):
        n = self.per_group - (self.early if nth else 0)
        if n:
            eng.sem_inc(self.sem, n)

    def wait(self, eng, turn, n):
        count = turn * self.per_group + (self.per_group + n + 1)
        if not isinstance(count, int) or count > 0:
            eng.wait_ge(self.sem, count)


class Settle:

    def __init__(self, sem):
        self.sem = sem

    def __call__(self, eng):
        eng.sem_inc(self.sem, 1)


class Chain:

    def __init__(self, sem):
        self.sem, self.n = sem, 0

    def add(self, ins):
        self.n += 1
        ins.then_inc(self.sem, 1)

    def wait(self, eng):
        eng.wait_ge(self.sem, self.n)


def build_program(nc, d, out):
    ctx = ExitStack()
    with ctx:
        semaphores = {}

        def sem(name):
            if name not in semaphores:
                semaphores[name] = ctx.enter_context(nc.semaphore(name))
            return semaphores[name]

        stack_chain = Chain(sem("f_dve"))
        half_set = sem("half_set")
        settle = Settle(sem("settled"))

        def keep(name, shape, dt=F32):
            return ctx.enter_context(nc.sbuf_tensor(name, shape, dt))

        ps = ctx.enter_context(nc.psum_tensor("ps", [P, 8, 512], F32))
        xtok = keep("xtok", [P, NT, P])
        ident = keep("ident", [P, P])
        identb = keep("identb", [P, P], BF16)
        minus_half = keep("minus_half", [P, 64])
        small = keep("small", [P, 8, 64])

        loads_done = sem("loads_done")
        n_loads = 2
        engines = {"sync": [], "scalar": [], "vector": [], "gpsimd": [], "tensor": []}
        x_ready = [sem(f"x_ready{i}") for i in range(5)]

        def load_common(sp):
            sp.dma_start(xtok[:], d["x"].rearrange("(t p) c -> p t c", p=P)).then_inc(loads_done, 16)
            sp.dma_start(ident[:], d["ident"]).then_inc(loads_done, 16)
        engines["sync"].append(load_common)

        def set_half(pool):
            pool.memset(minus_half[:], -0.5).then_inc(half_set, 1)
        engines["gpsimd"].append(set_half)

        def add_phase(**programs):
            for name, program in programs.items():
                engines[name].append(program)

        build_recurrent_block(nc, ps, xtok, ident, minus_half, small, d, sem, add_phase,
                              (loads_done, 16 * n_loads), half_set, x_ready[1])
        build_window_stack(nc, 0, stack_chain, settle, ps, xtok, ident, identb, minus_half, small, d, sem, add_phase,
                           x_ready[1], x_ready[2])
        build_full_attention(nc, settle, ps, xtok, ident, minus_half, small, d, sem, add_phase,
                             x_ready[2], x_ready[3])
        build_window_stack(nc, 1, stack_chain, settle, ps, xtok, ident, identb, minus_half, small, d, sem, add_phase,
                           x_ready[3], x_ready[4])

        out_stored = sem("out_stored")

        def store(sp):
            sp.wait_ge(x_ready[4], 1)
            sp.dma_start(out.rearrange("(t p) c -> p t c", p=P), xtok[:]).then_inc(out_stored, 16)
            sp.wait_ge(out_stored, 16)
        engines["sync"].append(store)

        block = ctx.enter_context(nc.Block())

        @block.sync
        def _(eng):
            for program in engines["sync"]:
                program(eng)

        @block.scalar
        def _(eng):
            for program in engines["scalar"]:
                program(eng)

        @block.vector
        def _(eng):
            for program in engines["vector"]:
                program(eng)

        @block.gpsimd
        def _(eng):
            for program in engines["gpsimd"]:
                program(eng)

        @block.tensor
        def _(eng):
            for program in engines["tensor"]:
                program(eng)


def per_token(ap, n=P):
    return ap.unsqueeze(2).broadcast_to([P, NT, n])


def layernorm_vector(v, chain, variance_ready, rstd_ready, src, dst, square, small, nth=1, eps=1e-5):
    mean, var, rstd = small[:, 0, 0:NT], small[:, 1, 0:NT], small[:, 2, 0:NT]
    chain.add(v.tensor_reduce(mean, src, axis=AX.X, op=ALU.add))
    chain.wait(v)
    chain.add(v.tensor_scalar(mean, mean, 1.0 / P, None, ALU.mult))
    chain.wait(v)
    chain.add(v.tensor_tensor(dst, src, per_token(mean), ALU.subtract))
    chain.wait(v)
    chain.add(v.tensor_tensor(square, dst, dst, ALU.mult))
    chain.wait(v)
    chain.add(v.tensor_reduce(var, square, axis=AX.X, op=ALU.add))
    chain.wait(v)
    v.tensor_scalar(var, var, 1.0 / P, eps, ALU.mult, ALU.add).then_inc(variance_ready, 1)
    v.wait_ge(rstd_ready, nth)
    chain.add(v.tensor_tensor(dst, dst, per_token(rstd), ALU.mult))
    chain.wait(v)


def layernorm_gpsimd(pool, variance_ready, rstd_ready, small, minus_half, nth=1):
    pool.wait_ge(variance_ready, nth)
    pool.tensor_tensor(small[:, 2, 0:NT], small[:, 1, 0:NT], minus_half[:, 0:NT], ALU.pow) \
        .then_inc(rstd_ready, 1)


def transpose_tiles(pe, ps, src, ident, banks, ready):
    for b, bank in enumerate(banks):
        for k in range(4):
            last = pe.transpose(ps[:, bank, k * P:(k + 1) * P], src(4 * b + k), ident[:])
        last.then_inc(ready, 1)


def build_recurrent_block(nc, ps, xtok, ident, minus_half, small, d, sem, add_phase, loaded, half_set,
                          x_next):
    with ExitStack() as mem:
        def sb(name, shape, dt=F32):
            return mem.enter_context(nc.sbuf_tensor("a_" + name, shape, dt))

        atok = sb("atok", [P, NT, P])
        ntok = sb("ntok", [P, NT, P])
        nT = sb("nT", [P, T])
        square = sb("square", [P, NT, P])
        gate = sb("gate", [P, T])
        z = sb("z", [P, 3 + T])
        zc = sb("zc", [P, T])
        forget = sb("forget", [P, T])
        insig = sb("insig", [P, T])
        beta = sb("beta", [P, T])
        hid = sb("hid", [P, T])
        yT = sb("yT", [P, T])
        w_in = sb("w_in", [P, 256])
        w_gates = sb("w_gates", [P, 256])
        w_out = sb("w_out", [P, P])
        w_grow = sb("w_grow", [P, 512])
        w_shrink = sb("w_shrink", [P, 2, P])
        cols = sb("cols", [P, 16])
        cw = sb("cw", [P, 4])
        tiny = sb("tiny", [P, 12])
        G1, G2, CB, FB, BF, BI = (cols[:, i:i + 1] for i in range(6))

    w_loaded = sem("a_w_loaded")
    chain = Chain(sem("a_dve"))
    var1, rstd1, var2, rstd2, var3, rstd3 = (sem(f"a_norm{i}") for i in range(6))
    norm_ready = [sem(f"a_norm_ready{i}") for i in range(2)]
    tr = [sem(f"a_transposed{i}") for i in range(4)]
    nT_ready = [sem(f"a_nT_ready{i}") for i in range(2)]
    cols_scaled = sem("a_cols_scaled")
    u_ps, gate_sb, z_sb = sem("a_u_ps"), sem("a_gate_sb"), sem("a_z_sb")
    conv_done, fg_ps, sig_sb = sem("a_conv_done"), sem("a_fg_ps"), sem("a_sig_sb")
    softplus_done, alpha_sb, one_minus, beta_sb = (sem(f"a_{n}") for n in
                                                   ("softplus", "alpha", "one_minus", "beta_sb"))
    zpad, h_done, y_ps, y_sb, back_used = (sem(f"a_{n}") for n in ("zpad", "h", "y_ps", "y_sb", "back"))
    absx, expx = sem("a_absx"), sem("a_expx")
    m_ps, m_gelu, m_u, m_out, m_sb, m_used = (sem(f"a_m_{n}") for n in
                                              ("ps", "gelu", "u", "out", "sb", "used"))

    def sync(sp):
        n = lambda ap: ap.rearrange("(p a) -> p a", a=1)
        for dst, src in ((w_in[:], d["input_wT"]), (w_gates[:], d["gates_wT"]), (w_out[:], d["output_wT"]),
                         (w_grow[:], d["grow_wT"]),
                         (w_shrink[:], d["shrink_wT"].rearrange("(c p) n -> p c n", p=P)),
                         (cw[:], d["conv_w"]), (G1, n(d["hawk_gamma"])), (G2, n(d["gmlp_gamma"])),
                         (CB, n(d["conv_b"])), (FB, n(d["forget_base"])),
                         (BF, n(d["gates_b"][0:P])), (BI, n(d["gates_b"][P:2 * P]))):
            sp.dma_start(dst, src).then_inc(w_loaded, 16)
    n_w = 12

    def rms_vector(v, ss_ready, rinv_ready, norm_done):
        chain.add(v.tensor_tensor(square[:], atok[:], atok[:], ALU.mult))
        chain.wait(v)
        v.tensor_reduce(small[:, 1, 0:NT], square[:], axis=AX.X, op=ALU.add).then_inc(ss_ready, 1)
        v.wait_ge(rinv_ready, 1)
        v.tensor_tensor(ntok[:], atok[:], per_token(small[:, 2, 0:NT]), ALU.mult).then_inc(norm_done, 1)

    def vector(v):
        v.wait_ge(loaded[0], loaded[1])
        layernorm_vector(v, chain, var1, rstd1, xtok[:], atok[:], square[:], small)
        rms_vector(v, var2, rstd2, norm_ready[0])
        v.wait_ge(w_loaded, 16 * n_w)
        v.tensor_scalar(cols[:, 0:2], cols[:, 0:2], float(np.sqrt(P)), None, ALU.mult).then_inc(cols_scaled, 1)
        v.memset(z[:, 0:3], 0.0).then_inc(zpad, 1)
        c = lambda i: tiny[:, i:i + 1]
        chain.add(v.tensor_scalar(c(0), FB, -1.0, None, ALU.mult))
        chain.wait(v)
        v.tensor_tensor(c(1), c(0), FB, ALU.min).then_inc(absx, 1)
        v.wait_ge(expx, 1)
        chain.add(v.tensor_scalar(c(3), c(2), 2.0, None, ALU.add))
        chain.wait(v)
        chain.add(v.reciprocal(c(4), c(3)))
        chain.wait(v)
        chain.add(v.tensor_tensor(c(5), c(2), c(4), ALU.mult))
        chain.wait(v)
        chain.add(v.tensor_tensor(c(6), c(5), c(5), ALU.mult))
        chain.add(v.memset(c(7), 1.0 / 17))
        chain.wait(v)
        for k in range(15, 0, -2):
            chain.add(v.tensor_scalar(c(7), c(7), c(6), 1.0 / k, ALU.mult, ALU.add))
            chain.wait(v)
        chain.add(v.scalar_tensor_tensor(c(8), c(7), 2.0, c(5), ALU.mult, ALU.mult))
        chain.add(v.tensor_scalar(c(9), FB, 0.0, None, ALU.max))
        chain.wait(v)
        chain.add(v.tensor_tensor(c(10), c(8), c(9), ALU.add))
        chain.wait(v)
        v.tensor_scalar(c(11), c(10), -8.0, None, ALU.mult).then_inc(softplus_done, 1)
        v.wait_ge(z_sb, 4)
        chain.add(v.tensor_scalar(zc[:], z[:, 0:T], cw[:, 0:1], CB, ALU.mult, ALU.add))
        chain.wait(v)
        for k in range(1, 4):
            ins = v.scalar_tensor_tensor(zc[:], z[:, k:k + T], cw[:, k:k + 1], zc[:], ALU.mult, ALU.add)
            if k < 3:
                chain.add(ins)
                chain.wait(v)
            else:
                ins.then_inc(conv_done, 1)
        v.wait_ge(alpha_sb, 1)
        chain.add(v.tensor_tensor(beta[:], forget[:], forget[:], ALU.mult))
        chain.wait(v)
        v.tensor_scalar(beta[:], beta[:], -1.0, 1.0, ALU.mult, ALU.add).then_inc(one_minus, 1)
        v.wait_ge(beta_sb, 1)
        chain.add(v.tensor_tensor(beta[:], beta[:], insig[:], ALU.mult))
        chain.wait(v)
        chain.add(v.tensor_tensor(beta[:], beta[:], zc[:], ALU.mult))
        chain.wait(v)
        chain.add(v.tensor_tensor_scan(hid[:], forget[:], beta[:], 0.0, ALU.mult, ALU.add))
        chain.wait(v)
        v.wait_ge(gate_sb, 4)
        v.tensor_tensor(hid[:], hid[:], gate[:], ALU.mult).then_inc(h_done, 1)
        for b in range(4):
            v.wait_ge(tr[1], b + 1)
            ins = v.tensor_tensor(atok[:, 4 * b:4 * b + 4, :].rearrange("p a c -> p (a c)"),
                                  atok[:, 4 * b:4 * b + 4, :].rearrange("p a c -> p (a c)"),
                                  ps[:, 4 + b, :], ALU.add)
            chain.add(ins)
        chain.wait(v)
        rms_vector(v, var3, rstd3, norm_ready[1])
        for q in range(4):
            for c_ in range(2):
                v.wait_ge(m_gelu, 2 * q + c_ + 1)
                v.tensor_tensor(forget[:, 1024 * (q % 2) + 512 * c_:1024 * (q % 2) + 512 * c_ + 512],
                                beta[:, 512 * c_:512 * c_ + 512], ps[:, 2 * c_ + 1, :], ALU.mult) \
                    .then_inc(m_u, 1)
        for b in range(4):
            v.wait_ge(tr[3], b + 1)
            a4 = atok[:, 4 * b:4 * b + 4, :].rearrange("p a c -> p (a c)")
            x4 = xtok[:, 4 * b:4 * b + 4, :].rearrange("p a c -> p (a c)")
            chain.add(v.tensor_tensor(a4, a4, ps[:, 4 + b, :], ALU.add))
            chain.wait(v)
            chain.add(v.tensor_tensor(x4, x4, a4, ALU.add))
        chain.wait(v)
        v.sem_inc(x_next, 1)

    def gpsimd(pool):
        pool.wait_ge(half_set, 1)
        layernorm_gpsimd(pool, var1, rstd1, small, minus_half)
        layernorm_gpsimd(pool, var2, rstd2, small, minus_half)
        layernorm_gpsimd(pool, var3, rstd3, small, minus_half)

    def tensor(pe):
        pe.wait_ge(norm_ready[0], 1)
        transpose_tiles(pe, ps, lambda t: ntok[:, t, :], ident, range(4), tr[0])
        pe.wait_ge(w_loaded, 16 * n_w)
        pe.wait_ge(nT_ready[0], 4)
        for m in range(2):
            for q in range(4):
                pe.matmul(ps[:, 4 * m + q, :], w_in[:, m * P:(m + 1) * P], nT[:, 512 * q:512 * q + 512],
                          start=True, stop=True).then_inc(u_ps, 1)
        pe.wait_ge(conv_done, 1)
        pe.wait_ge(gate_sb, 4)
        for m in range(2):
            for q in range(4):
                pe.matmul(ps[:, 4 * m + q, :], w_gates[:, m * P:(m + 1) * P], zc[:, 512 * q:512 * q + 512],
                          start=True, stop=True).then_inc(fg_ps, 1)
        pe.wait_ge(h_done, 1)
        for q in range(4):
            pe.matmul(ps[:, q, :], w_out[:], hid[:, 512 * q:512 * q + 512], start=True, stop=True) \
                .then_inc(y_ps, 1)
        pe.wait_ge(y_sb, 4)
        transpose_tiles(pe, ps, lambda t: yT[:, t * P:(t + 1) * P], ident, range(4, 8), tr[1])
        pe.wait_ge(norm_ready[1], 1)
        transpose_tiles(pe, ps, lambda t: ntok[:, t, :], ident, range(4), tr[2])
        pe.wait_ge(nT_ready[1], 4)
        for q in range(4):
            for c in range(2):
                if q:
                    pe.wait_ge(m_u, 2 * (q - 1) + c + 1)
                pe.matmul(ps[:, 2 * c, :], w_grow[:, c * P:(c + 1) * P], nT[:, 512 * q:512 * q + 512],
                          start=True, stop=True)
                pe.matmul(ps[:, 2 * c + 1, :], w_grow[:, 256 + c * P:256 + (c + 1) * P],
                          nT[:, 512 * q:512 * q + 512], start=True, stop=True).then_inc(m_ps, 1)
            for c in range(2):
                pe.wait_ge(m_u, 2 * q + c + 1)
                last = pe.matmul(ps[:, 4 + q, :], w_shrink[:, c, :],
                                 forget[:, 1024 * (q % 2) + 512 * c:1024 * (q % 2) + 512 * c + 512],
                                 start=(c == 0), stop=(c == 1))
            last.then_inc(m_out, 1)
        pe.wait_ge(m_sb, 4)
        transpose_tiles(pe, ps, lambda t: yT[:, t * P:(t + 1) * P], ident, range(4, 8), tr[3])

    def scalar(act):
        act.wait_ge(cols_scaled, 1)
        for b in range(4):
            act.wait_ge(tr[0], b + 1)
            act.activation(nT[:, 512 * b:512 * b + 512], ps[:, b, :], ACT.Copy, scale=G1).then_inc(nT_ready[0], 1)
        act.wait_ge(absx, 1)
        act.activation(tiny[:, 2:3], tiny[:, 1:2], ACT.Exp).then_inc(expx, 1)
        for q in range(4):
            act.wait_ge(u_ps, 4 + q + 1)
            act.activation(z[:, 3 + 512 * q:3 + 512 * q + 512], ps[:, 4 + q, :], ACT.Copy).then_inc(z_sb, 1)
        for q in range(4):
            act.activation(gate[:, 512 * q:512 * q + 512], ps[:, q, :], ACT.Gelu).then_inc(gate_sb, 1)
        for m, dst, bias in ((0, forget, BF), (1, insig, BI)):
            for q in range(4):
                act.wait_ge(fg_ps, 4 * m + q + 1)
                act.activation(dst[:, 512 * q:512 * q + 512], ps[:, 4 * m + q, :], ACT.Sigmoid, bias=bias) \
                    .then_inc(sig_sb, 1)
        act.wait_ge(sig_sb, 8)
        act.wait_ge(softplus_done, 1)
        act.activation(forget[:], forget[:], ACT.Exp, scale=tiny[:, 11:12]).then_inc(alpha_sb, 1)
        act.wait_ge(one_minus, 1)
        act.activation(beta[:], beta[:], ACT.Sqrt, bias=eps6[:]).then_inc(beta_sb, 1)
        for q in range(4):
            act.wait_ge(y_ps, q + 1)
            act.activation(yT[:, 512 * q:512 * q + 512], ps[:, q, :], ACT.Copy).then_inc(y_sb, 1)
        for b in range(4):
            act.wait_ge(tr[2], b + 1)
            act.activation(nT[:, 512 * b:512 * b + 512], ps[:, b, :], ACT.Copy, scale=G2).then_inc(nT_ready[1], 1)
        for q in range(4):
            for c in range(2):
                act.wait_ge(m_ps, 2 * q + c + 1)
                if q:
                    act.wait_ge(m_u, 2 * (q - 1) + c + 1)
                act.activation(beta[:, 512 * c:512 * c + 512], ps[:, 2 * c, :], ACT.Gelu).then_inc(m_gelu, 1)
            act.wait_ge(m_out, q + 1)
            act.activation(yT[:, 512 * q:512 * q + 512], ps[:, 4 + q, :], ACT.Copy).then_inc(m_sb, 1)

    eps6 = small[:, 7, 0:1]
    eps_set = sem("a_eps_set")

    def gpsimd_eps(pool):
        pool.memset(small[:, 7, 0:1], 1e-6).then_inc(eps_set, 1)

    def scalar_all(act):
        act.wait_ge(eps_set, 1)
        scalar(act)

    add_phase(gpsimd=gpsimd_eps)
    add_phase(sync=sync, vector=vector, gpsimd=gpsimd, tensor=tensor, scalar=scalar_all)


WIDE_SLOTS = 3
NARROW_BANK = 6


def psum_orders():
    def halves(what, j, ahead=0):
        return [(what, 2 * j, ahead), (what, 2 * j + 1, ahead)]

    wide, narrow = [], []
    for j in range(1, GT):
        n, ahead = (j + 1) % GT, (j + 1) // GT
        if j > 1:
            wide += [("q", n, ahead)]
            narrow += halves("qT", j)
        wide += [("k", n, ahead), ("ctx", j - 1, 0), ("v", n, ahead), ("s", j, 0)]
        narrow += halves("pT", j - 1) + halves("kT", j) + halves("cT", j - 1) + [("o", j - 1, 0)]
    wide += [("q", 1, 1), ("ctx", GT - 1, 0), ("k", 1, 1), ("v", 1, 1), ("s", 0, 1), ("q", 2, 1)]
    wide += [("ff", 0, 0), ("ff", 1, 0), ("ff", 2, 0), ("y", 0, 0)]
    narrow += halves("qT", 0, 1) + halves("pT", GT - 1) + halves("kT", 0, 1) + halves("cT", GT - 1)
    narrow += [("o", GT - 1, 0), ("ln", 0, 0), ("xn", 0, 0)] + halves("qT", 1, 1)
    assert len(wide) % WIDE_SLOTS == 0 and len(narrow) % 2 == 0
    return wide, narrow


def at(index):
    return slice(index, index + 1) if isinstance(index, int) else bass.ds(index, 1)


def build_window_stack(nc, nth, chain, settle, ps, xtok, ident, identb, minus_half, small, d, sem, add_phase,
                       x_ready, x_next):
    wide, narrow = psum_orders()
    wide_uses, narrow_uses = [u[:2] for u in wide], [u[:2] for u in narrow]
    with ExitStack() as mem:
        def sb(name, shape, dt=F32):
            return mem.enter_context(nc.sbuf_tensor(f"f{nth}_" + name, shape, dt))

        hT = sb("hT", [P, T])
        wqkv = sb("wqkv", [P, 3 * INNER])
        wo = sb("wo", [P, HP, P])
        w1 = sb("w1", [P, 2 * FF])
        w2 = sb("w2", [P, 3, P])
        tabs = sb("tabs", [P, NT, 2, 2, DH])
        masks = sb("masks", [P, 2, 512], BF16)
        mask32 = sb("mask32", [P, 2, 2 * WIN])
        decay = sb("decay", [P, 1])
        gains = sb("gains", [P, DEPTH + 1, 2, DH])
        vecs = sb("vecs", [P, DEPTH, 9])
        xs = sb("xs", [P, GW + 1])
        xf = sb("xf", [P, GW + 1])
        tab = [sb(f"tab{i}", [P, 2, 2, DH]) for i in range(2)]
        prod = [sb(f"prod{i}", [P, H, 2, DH]) for i in range(2)]
        sq = [sb(f"sq{i}", [P, H, DH]) for i in range(2)]
        stat = sb("stat", [P, 2, 2, H])
        qk = [[sb(f"qk{i}{u}", [P, H, DH]) for u in range(2)] for i in range(2)]
        qT = sb("qT", [P, HP, P])
        kT = [sb(f"kT{i}", [P, HP, 2, WIN + P]) for i in range(2)]
        vtok = [sb(f"vtok{i}", [P, 2, 512]) for i in range(2)]
        vbd = [sb(f"vbd{i}", [P, NW, 2, 512]) for i in range(2)]
        pr = [sb(f"pr{i}", [P, H, 2 * WIN]) for i in range(2)]
        mx = sb("mx", [P, H])
        rs = [sb(f"rs{i}", [P, H]) for i in range(2)]
        pT = sb("pT", [P, HP, P])
        cn = sb("cn", [P, INNER])
        cT = sb("cT", [P, HP, P])
        bn = sb("bn", [P, GT, 6])
        mv = sb("mv", [P, GT, 2])
        rstd = sb("rstd", [P, GT])
        xn = sb("xn", [P, GT, P])
        xnT = sb("xnT", [P, GW])
        carried = sb("carried", [P, NG])
        gl = sb("gl", [P, 2, GW])
        uT = sb("uT", [P, 3, GW])
        ntok = qk[0][0][:].rearrange("p a b -> p (a b)")
        lnsq = prod[0][:].rearrange("p a b c -> p (a b c)").rearrange("p (t c) -> p t c", c=P)
        lnx = prod[1][:].rearrange("p a b c -> p (a b c)").rearrange("p (t c) -> p t c", c=P)

    def signal(name, per_group, early=0):
        return Signal(sem(f"f_{name}"), per_group, early)

    proj = signal("proj", 3 * GT, 7)
    qkT_ps = signal("qkT_ps", 4 * GT, 6)
    s_ps = signal("s_ps", GT, 1)
    pT_ps = signal("pT_ps", 2 * GT)
    ctx_ps = signal("ctx_ps", GT)
    cT_ps = signal("cT_ps", 2 * GT)
    o_ps = signal("o_ps", GT)
    ln_ps, xn_ps, ff_ps, y_ps = signal("ln_ps", 1), signal("xn_ps", 1), signal("ff_ps", 3), signal("y_ps", 1)
    squared = signal("squared", 2 * GT, 5)
    v_sb = signal("v_sb", GT, 2)
    qkT_sb = signal("qkT_sb", 4 * GT, 6)
    exp_sb = signal("exp_sb", GT, 1)
    pT_sb = signal("pT_sb", 2 * GT)
    cT_sb = signal("cT_sb", 2 * GT)
    xnT_sb, gelu_sb = signal("xnT_sb", 1), signal("gelu_sb", 3)
    xs_sb, xf_sb = signal("xs_sb", 1, 1), signal("xf_sb", 1)
    xs_moved, xf_moved = signal("xs_moved", 1, 1), signal("xf_moved", 1)
    prod_sb = signal("prod_sb", 2 * GT, 5)
    sums = signal("sums", 2 * GT, 5)
    normed = signal("normed", 2 * GT, 4)
    maxed = signal("maxed", GT, 1)
    shifted = signal("shifted", GT, 1)
    summed = signal("summed", GT, 1)
    inverted = signal("inverted", GT, 1)
    ctx_sb = signal("ctx_sb", GT)
    x1 = signal("x1", GT)
    bn_done, mv_done, xn_sb = signal("bn_done", 1), signal("mv_done", 1), signal("xn_sb", 1)
    u_sb, x2 = signal("u_sb", 3), signal("x2", 1)
    tab_sb = signal("tab_sb", GT, 3)
    clamped, rinv = signal("clamped", 2 * GT, 5), signal("rinv", 2 * GT, 5)
    rotated = signal("rotated", 2 * GT, 5)
    k_prev = signal("k_prev", GT, 2)
    rstd_a, rstd_sb = signal("rstd_a", 1), signal("rstd_sb", 1)
    consts = sem(f"f_consts")
    wqkv_ld, wo_ld, w1_ld, w2_ld = (sem(f"f_{n}") for n in ("wqkv_ld", "wo_ld", "w1_ld", "w2_ld"))
    v_keys = [sem(f"f_v_keys{i}") for i in range(2)]
    zeroed, var0, rstd0, n0, t0, h0, back_ps = (sem(f"f_{n}") for n in
                                               ("zeroed", "var0", "rstd0", "n0", "t0", "h0", "back"))
    V_DMAS = 10
    V_TURN = 16 * V_DMAS * GT // 2
    base = nth * (DEPTH * NG + 1)
    end = base + DEPTH * NG

    released = {
        "q": lambda e, t, j: prod_sb.wait(e, t, 2 * j),
        "k": lambda e, t, j: prod_sb.wait(e, t, 2 * j + 1),
        "v": lambda e, t, j: v_sb.wait(e, t, j),
        "s": lambda e, t, j: shifted.wait(e, t, j),
        "ctx": lambda e, t, j: ctx_sb.wait(e, t, j),
        "ff": lambda e, t, j: u_sb.wait(e, t, j),
        "y": lambda e, t, j: x2.wait(e, t, j),
        "qT": lambda e, t, j: qkT_sb.wait(e, t, 2 * (j // 2) * 2 + j % 2),
        "kT": lambda e, t, j: qkT_sb.wait(e, t, 2 * (j // 2) * 2 + 2 + j % 2),
        "pT": lambda e, t, j: pT_sb.wait(e, t, j),
        "cT": lambda e, t, j: cT_sb.wait(e, t, j),
        "o": lambda e, t, j: x1.wait(e, t, j),
        "ln": lambda e, t, j: xn_sb.wait(e, t, j),
        "xn": lambda e, t, j: xnT_sb.wait(e, t, j),
    }
    def wide_slot(use):
        i = wide_uses.index(use)
        b = 2 * (i % WIDE_SLOTS)
        return ps[:, b:b + 2, :].rearrange("p b n -> p (b n)")

    def narrow_bank(use):
        return ps[:, NARROW_BANK + narrow_uses.index(use) % 2, :]

    def wait_room(pe, turn, use):
        order, uses, step = (wide, wide_uses, WIDE_SLOTS) if use in wide_uses else (narrow, narrow_uses, 2)
        i = uses.index(use)
        what, j, ahead = order[i - step]
        released[what](pe, turn + (ahead - order[i][2] - (1 if i < step else 0)), j)

    def sync(sp):
        for s in v_keys:
            sp.sem_inc(s, V_TURN // 2 if nth else 1)
        sp.wait_ge(x_ready, 1)
        n = 0
        for dst, src in ((tabs[:], d["tabs"]), (mask32[:], d["masks"]), (decay[:], d["decay"])):
            sp.dma_start(dst, src).then_inc(consts, 16)
            n += 1
        for u, name in enumerate(("q_scale", "k_scale")):
            sp.dma_start(gains[:, 0:DEPTH, u, :], d[name].unsqueeze(0).broadcast_to([P, DEPTH, DH])) \
                .then_inc(consts, 16)
            n += 1
        for c, name in enumerate(("ln_g", "ln_b", "b2")):
            sp.dma_start(vecs[:, :, c], d[name].rearrange("l p -> p l"),
                         allow_slow_non_contiguous=True).then_inc(consts, 16)
            n += 1
        for half in range(2):
            for c, (o, m) in enumerate(FCH):
                sp.dma_start(vecs[0:m, :, 3 + 3 * half + c],
                             d["b1"][:, half * FF + o:half * FF + o + m].rearrange("l p -> p l"),
                             allow_slow_non_contiguous=True) \
                    .then_inc(consts, 16)
                n += 1
        assert n == N_CONSTS
        sp.dma_start(wqkv[:], d["Wqkv"][0]).then_inc(wqkv_ld, 16)
        with sp.Fori(0, DEPTH) as layer:
            first = base + layer * NG
            for j in range(2):
                copy_values(sp, first, j)
            o_ps.wait(sp, first, -1)
            settle(sp)
            sp.dma_start(wo[:], d["Wo"][layer].rearrange("(c p) n -> p c n", p=P)).then_inc(wo_ld, 16)
            ff_ps.wait(sp, first, -1)
            settle(sp)
            sp.dma_start(w1[:], d["W1"][layer]).then_inc(w1_ld, 16)
            y_ps.wait(sp, first, -1)
            settle(sp)
            for c, (o, m) in enumerate(FCH):
                sp.dma_start(w2[0:m, c, :], d["W2"][layer][o:o + m, :]).then_inc(w2_ld, 16)
            with sp.Fori(0, NG - 1) as g:
                for j in range(2, GT + 2):
                    copy_values(sp, first + g + j // GT, j % GT)
            copy_values(sp, first + (NG - 1), 2)
            proj.wait(sp, first + NG, -1)
            settle(sp)
            sp.dma_start(wqkv[:], d["Wqkv"][(layer + 1) % DEPTH]).then_inc(wqkv_ld, 16)
            copy_values(sp, first + (NG - 1), 3)
        for j in range(2):
            copy_values(sp, end, j)

    def copy_values(sp, turn, j):
        a, b = j % 2, 1 - j % 2
        v_sb.wait(sp, turn, j)
        settle(sp)
        ctx_ps.wait(sp, turn, j - 2)
        settle(sp)
        for h2 in range(2):
            lo = DH * h2
            sp.dma_start(vbd[a][lo:lo + WIN, 0, h2, :], vtok[b][P - WIN:P, h2, :]).then_inc(v_keys[a], 16)
            sp.dma_start(vbd[a][lo + WIN:lo + DH, 0, h2, :], vtok[a][0:WIN, h2, :]).then_inc(v_keys[a], 16)
            for w in range(1, NW):
                sp.dma_start(vbd[a][lo:lo + DH, w, h2, :], vtok[a][WIN * (w - 1):WIN * (w + 1), h2, :]) \
                    .then_inc(v_keys[a], 16)

    def v_keys_wait(eng, turn, j):
        eng.wait_ge(v_keys[j % 2], turn * V_TURN + (16 * V_DMAS * (j // 2 + 1) + 1))

    def tensor(pe):
        for s in (proj, qkT_ps, s_ps, pT_ps, ctx_ps, cT_ps, o_ps, ln_ps, xn_ps, ff_ps, y_ps):
            s.start(pe, nth)
        pe.wait_ge(n0, nth + 1)
        transpose_tiles(pe, ps, lambda t: lnx[:, t, :], ident, range(4), t0)
        pe.wait_ge(consts, 16 * N_CONSTS * (nth + 1))
        pe.wait_ge(h0, 4 * nth + 4)
        pe.wait_ge(zeroed, 2 * nth + 2)
        pe.wait_ge(wqkv_ld, (nth * (DEPTH + 1) + 1) * 16)
        xs_sb.wait(pe, base, 0)

        def room():
            shifted.wait(pe, base, scored - 1)
            prod_sb.wait(pe, base, 2 * (done // 3) + min(done % 3, 2) - 1)
            v_sb.wait(pe, base, done // 3 - 1)
            qkT_sb.wait(pe, base, transposed - 1)

        done, scored, transposed = 0, 0, 0
        for piece in ("q0", "k0", "v0", "qT", "q1", "kT", "k1", "v1", "s", "qT1", "q2"):
            room()
            if piece == "qT":
                transpose_qk(pe, base, 0, 0)
                transposed = 2
            elif piece == "kT":
                transpose_qk(pe, base, 0, 1)
                transposed = 4
            elif piece == "qT1":
                transpose_qk(pe, base, 1, 0)
                transposed = 6
            elif piece == "s":
                scores(pe, base, 0, masks[:, 0, :])
                scored = 1
            else:
                project(pe, base, int(piece[1]), piece[0])
                done += 1
        room()
        with pe.Fori(0, DEPTH) as layer:
            with pe.Fori(0, NG) as g:
                tensor_turn(pe, base + layer * NG + g, layer, g)
        x2.wait(pe, end - 1, 0)
        prod_sb.wait(pe, end, 4)
        v_sb.wait(pe, end, 1)
        qkT_sb.wait(pe, end, 5)
        shifted.wait(pe, end, 0)
        transpose_tiles(pe, ps, lambda t: hT[:, t * P:(t + 1) * P], ident, range(4), back_ps)

    def project(pe, turn, j, what):
        wait_room(pe, turn, (what, j))
        dst = wide_slot((what, j))
        for half in range(2):
            if what == "v":
                w = wqkv[:, 2 * INNER:].rearrange("p (a h c) -> p h a c", h=2, c=DH)[:, half]
            else:
                u = "qk".index(what)
                w = wqkv[:, u * INNER + 512 * half:u * INNER + 512 * half + 512]
            last = pe.matmul(dst[:, 512 * half:512 * half + 512], xs[:, j * P:(j + 1) * P], w,
                             start=True, stop=True)
        last.then_inc(proj.sem, 1)

    def transpose_qk(pe, turn, j, u):
        normed.wait(pe, turn, 2 * j + u)
        for half in range(2):
            use = (("qT", "kT")[u], 2 * j + half)
            wait_room(pe, turn, use)
            for c in range(4):
                hp = 4 * half + c
                src = qk[j % 2][u][:, 2 * hp:2 * hp + 2, :].rearrange("p a b -> p (a b)")
                last = pe.transpose(narrow_bank(use)[:, c * P:(c + 1) * P], src, ident[:])
            last.then_inc(qkT_ps.sem, 1)

    def scores(pe, turn, j, first_mask=None):
        wait_room(pe, turn, ("s", j))
        dst = wide_slot(("s", j))
        qkT_sb.wait(pe, turn, 4 * j + 3)
        k_prev.wait(pe, turn, j)
        for half in range(2):
            bank = dst[:, 512 * half:512 * half + 512]
            mask = first_mask if j == 0 else masks[:, 1, :]
            pe.matmul(bank, identb[:], mask, start=True, stop=False, skip_group_check=True)
            for c in range(4):
                hp = 4 * half + c
                for w in range(NW):
                    last = pe.matmul(bank[WIN * w:WIN * (w + 1), c * P:(c + 1) * P],
                                     qT[:, hp, WIN * w:WIN * (w + 1)],
                                     kT[j % 2][:, hp, :, WIN * w:WIN * (w + 2)],
                                     start=False, stop=True, skip_group_check=True)
        last.then_inc(s_ps.sem, 1)

    def transpose_probabilities(pe, turn, j):
        exp_sb.wait(pe, turn, j)
        for half in range(2):
            use = ("pT", 2 * j + half)
            wait_room(pe, turn, use)
            for c in range(4):
                hp = 4 * half + c
                src = pr[j % 2][:, 2 * hp:2 * hp + 2, :].rearrange("p a b -> p (a b)")
                last = pe.transpose(narrow_bank(use)[:, c * P:(c + 1) * P], src, ident[:])
            last.then_inc(pT_ps.sem, 1)

    def attend(pe, turn, j):
        wait_room(pe, turn, ("ctx", j))
        dst = wide_slot(("ctx", j))
        v_keys_wait(pe, turn, j)
        for hp in range(HP):
            if hp % 4 == 0:
                pT_sb.wait(pe, turn, 2 * j + hp // 4)
            for w in range(NW):
                last = pe.matmul(dst[WIN * w:WIN * (w + 1), hp * P:(hp + 1) * P],
                                 pT[:, hp, WIN * w:WIN * (w + 1)],
                                 vbd[j % 2][:, w, :, hp * DH:(hp + 1) * DH],
                                 start=True, stop=True)
        last.then_inc(ctx_ps.sem, 1)

    def transpose_context(pe, turn, j):
        ctx_sb.wait(pe, turn, j)
        for half in range(2):
            use = ("cT", 2 * j + half)
            wait_room(pe, turn, use)
            for c in range(4):
                hp = 4 * half + c
                last = pe.transpose(narrow_bank(use)[:, c * P:(c + 1) * P], cn[:, hp * P:(hp + 1) * P], ident[:])
            last.then_inc(cT_ps.sem, 1)

    def project_out(pe, turn, j):
        wait_room(pe, turn, ("o", j))
        for hp in range(HP):
            if hp % 4 == 0:
                cT_sb.wait(pe, turn, 2 * j + hp // 4)
            last = pe.matmul(narrow_bank(("o", j))[:, 0:P], wo[:, hp, :], cT[:, hp, :],
                             start=(hp == 0), stop=(hp == HP - 1))
        last.then_inc(o_ps.sem, 1)

    def tensor_turn(pe, turn, layer, g):
        following = (g + 1) % NG
        loaded = layer + (nth * DEPTH + 1)
        pe.wait_ge(wo_ld, loaded * 16)
        settle(pe)
        for j in range(1, GT):
            n, projected = (j + 1) % GT, turn + (j + 1) // GT
            if j > 1:
                transpose_qk(pe, turn, j, 0)
                if j == GT - 1:
                    pe.wait_ge(wqkv_ld, (layer + (g + 1) // NG) * 16 + (nth * (DEPTH + 1) + 1) * 16)
                    settle(pe)
                    xs_sb.wait(pe, projected, 0)
                project(pe, projected, n, "q")
            transpose_probabilities(pe, turn, j - 1)
            project(pe, projected, n, "k")
            transpose_qk(pe, turn, j, 1)
            attend(pe, turn, j - 1)
            project(pe, projected, n, "v")
            transpose_context(pe, turn, j - 1)
            scores(pe, turn, j)
            project_out(pe, turn, j - 1)
        transpose_qk(pe, turn + 1, 0, 0)
        project(pe, turn + 1, 1, "q")
        transpose_probabilities(pe, turn, GT - 1)
        transpose_qk(pe, turn + 1, 0, 1)
        attend(pe, turn, GT - 1)
        project(pe, turn + 1, 1, "k")
        transpose_context(pe, turn, GT - 1)
        project(pe, turn + 1, 1, "v")
        project_out(pe, turn, GT - 1)
        scores(pe, turn + 1, 0, masks[:, at((following + (NG - 1)) // NG), :].rearrange("p a n -> p (a n)"))
        xf_sb.wait(pe, turn, 0)
        wait_room(pe, turn, ("ln", 0))
        for j in range(GT):
            last = pe.transpose(narrow_bank(("ln", 0))[:, j * P:(j + 1) * P], xf[:, j * P:(j + 1) * P], ident[:])
        last.then_inc(ln_ps.sem, 1)
        project(pe, turn + 1, 2, "q")
        xn_sb.wait(pe, turn, 0)
        wait_room(pe, turn, ("xn", 0))
        for j in range(GT):
            last = pe.transpose(narrow_bank(("xn", 0))[:, j * P:(j + 1) * P], xn[:, j, :], ident[:])
        last.then_inc(xn_ps.sem, 1)
        xnT_sb.wait(pe, turn, 0)
        pe.wait_ge(w1_ld, loaded * 16)
        pe.wait_ge(w2_ld, loaded * 48)
        settle(pe)
        for c, (o, m) in enumerate(FCH):
            wait_room(pe, turn, ("ff", c))
            dst = wide_slot(("ff", c))
            pe.matmul(dst[0:m, 0:GW], w1[:, FF + o:FF + o + m], xnT[:], start=True, stop=True)
            pe.matmul(dst[0:m, GW:2 * GW], w1[:, o:o + m], xnT[:], start=True, stop=True) \
                .then_inc(ff_ps.sem, 1)
        transpose_qk(pe, turn + 1, 1, 0)
        wait_room(pe, turn, ("y", 0))
        for c, (o, m) in enumerate(FCH):
            u_sb.wait(pe, turn, c)
            last = pe.matmul(wide_slot(("y", 0))[:, 0:GW], w2[0:m, c, :], uT[0:m, c, :],
                             start=(c == 0), stop=(c == 2))
        last.then_inc(y_ps.sem, 1)

    def scalar(act):
        for s in (xs_sb, xf_sb, xs_moved, xf_moved, squared, v_sb, qkT_sb, exp_sb, pT_sb, cT_sb, xnT_sb, gelu_sb):
            s.start(act, nth)
        for b in range(4):
            act.wait_ge(t0, 4 * nth + b + 1)
            act.activation(hT[:, 512 * b:512 * b + 512], ps[:, b, :], ACT.Copy).then_inc(h0, 1)
        act.wait_ge(zeroed, 2 * nth + 2)
        act.wait_ge(consts, 16 * N_CONSTS * (nth + 1))
        begin, square_of, store_v, store_q, store_k, _, _, exponentials, _ = scalar_steps(act)
        begin(base, 0)
        square_of(base, 0, 0)
        square_of(base, 0, 1)
        store_v(base, 0)
        store_q(base, 0)
        square_of(base, 1, 0)
        store_k(base, 0)
        square_of(base, 1, 1)
        store_v(base, 1)
        exponentials(base, 0)
        store_q(base, 1)
        square_of(base, 2, 0)
        with act.Fori(0, DEPTH) as layer:
            with act.Fori(0, NG) as g:
                scalar_turn(act, base + layer * NG + g, layer, g)

    def scalar_steps(act):
        def shift(turn, group, dst, moved, ready):
            if isinstance(group, int):
                factor, cols = carried[DH:P, group:group + 1], slice(group * GW, (group + 1) * GW)
            else:
                factor, cols = carried[DH:P, bass.ds(group, 1)], bass.ds(group * GW, GW)
            act.activation(dst[DH:P, 0:1], dst[DH:P, GW:GW + 1], ACT.Copy, scale=factor).then_inc(moved.sem, 1)
            moved.wait(act, turn, 0)
            settle(act)
            act.activation(dst[0:DH, 0:GW], hT[0:DH, cols], ACT.Copy)
            act.activation(dst[DH:P, 1:GW + 1], hT[DH:P, cols], ACT.Copy).then_inc(ready.sem, 1)

        def square_of(turn, j, u):
            proj.wait(act, turn, 3 * j + u)
            sums.wait(act, turn, 2 * j + u - 2)
            act.activation(sq[u][:].rearrange("p a b -> p (a b)"), wide_slot(("qk"[u], j)), ACT.Square) \
                .then_inc(squared.sem, 1)

        def store_v(turn, j):
            proj.wait(act, turn, 3 * j + 2)
            v_copied(act, turn, j)
            act.activation(vtok[j % 2][:].rearrange("p a b -> p (a b)"), wide_slot(("v", j)), ACT.Copy) \
                .then_inc(v_sb.sem, 1)

        def store_q(turn, j):
            s_ps.wait(act, turn, j - 1)
            for half in range(2):
                qkT_ps.wait(act, turn, 4 * j + half)
                act.activation(qT[:, 4 * half:4 * half + 4, :].rearrange("p a b -> p (a b)"),
                               narrow_bank(("qT", 2 * j + half)), ACT.Copy).then_inc(qkT_sb.sem, 1)

        def store_k(turn, j):
            s_ps.wait(act, turn, j - 2)
            k_prev.wait(act, turn, j - 1)
            for half in range(2):
                qkT_ps.wait(act, turn, 4 * j + 2 + half)
                for h2 in range(2):
                    rows = slice(DH * h2, DH * h2 + DH)
                    last = act.activation(
                        kT[j % 2][rows, 4 * half:4 * half + 4, h2, WIN:],
                        narrow_bank(("kT", 2 * j + half)).rearrange("p (a b) -> p a b", b=P)[rows], ACT.Copy)
                last.then_inc(qkT_sb.sem, 1)

        def exponentials(turn, j):
            shifted.wait(act, turn, j)
            act.activation(pr[j % 2][:], pr[j % 2][:], ACT.Exp).then_inc(exp_sb.sem, 1)

        def store_probabilities(turn, j):
            ctx_ps.wait(act, turn, j - 1)
            for half in range(2):
                pT_ps.wait(act, turn, 2 * j + half)
                act.activation(pT[:, 4 * half:4 * half + 4, :].rearrange("p a b -> p (a b)"),
                               narrow_bank(("pT", 2 * j + half)), ACT.Copy).then_inc(pT_sb.sem, 1)

        def store_context(turn, j):
            o_ps.wait(act, turn, j - 1)
            for half in range(2):
                cT_ps.wait(act, turn, 2 * j + half)
                act.activation(cT[:, 4 * half:4 * half + 4, :].rearrange("p a b -> p (a b)"),
                               narrow_bank(("cT", 2 * j + half)), ACT.Copy).then_inc(cT_sb.sem, 1)

        def begin(turn, group):
            proj.wait(act, turn, -1)
            x2.wait(act, turn, -2)
            settle(act)
            shift(turn, group, xs, xs_moved, xs_sb)

        def feed_forward_input(turn, group):
            ln_ps.wait(act, turn, -1)
            x1.wait(act, turn, GT - 1)
            settle(act)
            shift(turn, group, xf, xf_moved, xf_sb)

        return (begin, square_of, store_v, store_q, store_k, store_probabilities, store_context,
                exponentials, feed_forward_input)

    def scalar_turn(act, turn, layer, g):
        following = (g + 1) % NG
        (begin, square_of, store_v, store_q, store_k, store_probabilities, store_context,
         exponentials, feed_forward_input) = scalar_steps(act)
        for j in range(1, GT):
            n, projected = (j + 1) % GT, turn + (j + 1) // GT
            if j > 1:
                store_q(turn, j)
                square_of(projected, n, 0)
            store_probabilities(turn, j - 1)
            square_of(projected, n, 1)
            store_k(turn, j)
            store_v(projected, n)
            store_context(turn, j - 1)
            if j == GT - 2:
                begin(turn + 1, following)
            exponentials(turn, j)
        store_q(turn + 1, 0)
        square_of(turn + 1, 1, 0)
        store_probabilities(turn, GT - 1)
        store_k(turn + 1, 0)
        square_of(turn + 1, 1, 1)
        store_context(turn, GT - 1)
        store_v(turn + 1, 1)
        feed_forward_input(turn, g)
        square_of(turn + 1, 2, 0)
        vec = lambda c, m=P: vecs[0:m, bass.ds(layer, 1), c]
        xn_ps.wait(act, turn, 0)
        ff_ps.wait(act, turn, -1)
        settle(act)
        act.activation(xnT[:], narrow_bank(("xn", 0)), ACT.Identity, scale=vec(0), bias=vec(1)) \
            .then_inc(xnT_sb.sem, 1)
        exponentials(turn + 1, 0)
        for c, (o, m) in enumerate(FCH):
            ff_ps.wait(act, turn, c)
            u_sb.wait(act, turn, (-1, -2, 0)[c])
            settle(act)
            act.activation(gl[0:m, c % 2, :], wide_slot(("ff", c))[0:m, 0:GW], ACT.Gelu, bias=vec(6 + c, m)) \
                .then_inc(gelu_sb.sem, 1)
        store_q(turn + 1, 1)

    def v_copied(eng, turn, j):
        if j >= 1:
            v_keys_wait(eng, turn, j - 1)
        if j == 0:
            for a in range(2):
                eng.wait_ge(v_keys[a], turn * V_TURN + 1)
        if j == 1:
            eng.wait_ge(v_keys[1], turn * V_TURN + 1)

    def vector(v):
        for s in (prod_sb, sums, normed, maxed, shifted, summed, inverted, ctx_sb, x1, bn_done, mv_done,
                  xn_sb, u_sb, x2):
            s.start(v, nth)
        v.wait_ge(x_ready, 1)
        layernorm_vector(v, chain, var0, rstd0, xtok[:], lnx, lnsq, small, nth=nth + 1)
        v.sem_inc(n0, 1)
        for buf in (vtok[0], vtok[1], kT[0], kT[1]):
            v.memset(buf[:], 0.0)
        chain.add(v.memset(carried[:], 1.0))
        chain.wait(v)
        v.memset(carried[:, 0:1], 0.0)
        v.memset(xs[:], 0.0)
        v.memset(xf[:], 0.0)
        v.memset(gains[:, DEPTH], 1.0)
        v.wait_ge(consts, 16 * N_CONSTS * (nth + 1))
        v.tensor_copy(identb[:], ident[:])
        for i in range(2):
            last = v.tensor_copy(masks[:, i, :].rearrange("p (a c) -> p a c", c=2 * WIN),
                          mask32[:, i:i + 1, :].broadcast_to([P, 8, 2 * WIN]))
        last.then_inc(zeroed, 1)
        v.wait_ge(h0, 4 * nth + 4)
        v.wait_ge(consts, 16 * N_CONSTS * (nth + 1))
        vector_first_tiles(v)
        with v.Fori(0, DEPTH) as layer:
            with v.Fori(0, NG) as g:
                vector_turn(v, base + layer * NG + g, layer, g)
        exp_sb.wait(v, end, 0)
        k_prev.wait(v, end, 1)
        rotated.wait(v, end, 4)
        rinv.wait(v, end, 4)
        qkT_sb.wait(v, end, 5)
        for a in range(2):
            v_keys_wait(v, end, a)
        for b in range(4):
            v.wait_ge(back_ps, 4 * nth + b + 1)
            x4 = xtok[:, 4 * b:4 * b + 4, :].rearrange("p a c -> p (a c)")
            chain.add(v.tensor_tensor(x4, x4, ps[:, b, :], ALU.add))
        chain.wait(v)
        v.sem_inc(x_next, 1)

    def vector_steps(v):
        def products(turn, j, u):
            tab_sb.wait(v, turn, j)
            proj.wait(v, turn, 3 * j + u)
            rotated.wait(v, turn, 2 * j + u - 2)
            squared.wait(v, turn, 2 * j + u)
            src = wide_slot(("qk"[u], j)).rearrange("p (h c) -> p h c", c=DH)
            v.tensor_tensor(prod[u][:], src.unsqueeze(2).broadcast_to([P, H, 2, DH]),
                            tab[j % 2][:, u].unsqueeze(1).broadcast_to([P, H, 2, DH]), ALU.mult) \
                .then_inc(prod_sb.sem, 1)

        def norms(turn, j, u):
            rinv.wait(v, turn, 2 * j + u - 4)
            v.tensor_reduce(stat[:, j % 2, u, :], sq[u][:], axis=AX.X, op=ALU.add).then_inc(sums.sem, 1)

        def normalise(turn, j, u):
            rotated.wait(v, turn, 2 * j + u)
            rinv.wait(v, turn, 2 * j + u)
            buf = qk[j % 2][u]
            v.tensor_tensor(buf[:], buf[:], stat[:, j % 2, u, :].unsqueeze(2).broadcast_to([P, H, DH]),
                            ALU.mult).then_inc(normed.sem, 1)

        def softmax(turn, j):
            src = wide_slot(("s", j)).rearrange("p (h c) -> p h c", c=2 * WIN)
            s_ps.wait(v, turn, j)
            v.tensor_reduce(mx[:], src, axis=AX.X, op=ALU.max).then_inc(maxed.sem, 1)
            maxed.wait(v, turn, j)
            pT_ps.wait(v, turn, 2 * j - 3)
            v.tensor_tensor(pr[j % 2][:], src, mx[:].unsqueeze(2).broadcast_to([P, H, 2 * WIN]),
                            ALU.subtract).then_inc(shifted.sem, 1)

        def sum_up(turn, j):
            exp_sb.wait(v, turn, j)
            v.tensor_reduce(rs[j % 2][:], pr[j % 2][:], axis=AX.X, op=ALU.add).then_inc(summed.sem, 1)
            summed.wait(v, turn, j)
            v.reciprocal(rs[j % 2][:], rs[j % 2][:]).then_inc(inverted.sem, 1)

        def divide(turn, j):
            ctx_ps.wait(v, turn, j)
            cT_ps.wait(v, turn, 2 * j - 1)
            inverted.wait(v, turn, j)
            v.tensor_tensor(cn[:].rearrange("p (h c) -> p h c", c=DH),
                            wide_slot(("ctx", j)).rearrange("p (h c) -> p h c", c=DH),
                            rs[j % 2][:].unsqueeze(2).broadcast_to([P, H, DH]), ALU.mult) \
                .then_inc(ctx_sb.sem, 1)

        return products, norms, normalise, softmax, sum_up, divide

    def vector_first_tiles(v):
        products, norms, normalise, softmax, sum_up, _ = vector_steps(v)
        for j in range(2):
            for u in range(2):
                products(base, j, u)
                norms(base, j, u)
            for u in range(2):
                normalise(base, j, u)
        softmax(base, 0)
        sum_up(base, 0)
        products(base, 2, 0)
        norms(base, 2, 0)

    def vector_turn(v, turn, layer, g):
        vec = lambda c, m=P: vecs[0:m, bass.ds(layer, 1), c]
        products, norms, normalise, softmax, sum_up, divide = vector_steps(v)

        def add_attention(j):
            o_ps.wait(v, turn, j)
            if j == 0:
                xs_sb.wait(v, turn, 0)
            at = hT[:, bass.ds(g * GW + j * P, P)]
            v.tensor_tensor(at, at, narrow_bank(("o", j))[:, 0:P], ALU.add).then_inc(x1.sem, 1)

        for j in range(1, GT):
            n, projected = (j + 1) % GT, turn + (j + 1) // GT
            if j > 1:
                products(projected, n, 0)
                norms(projected, n, 0)
            products(projected, n, 1)
            divide(turn, j - 1)
            norms(projected, n, 1)
            normalise(projected, n, 0)
            softmax(turn, j)
            add_attention(j - 1)
            normalise(projected, n, 1)
            sum_up(turn, j)
        products(turn + 1, 1, 0)
        norms(turn + 1, 1, 0)
        divide(turn, GT - 1)
        products(turn + 1, 1, 1)
        add_attention(GT - 1)
        norms(turn + 1, 1, 1)
        ln_ps.wait(v, turn, 0)
        bank = narrow_bank(("ln", 0)).rearrange("p (t c) -> p t c", c=P)
        for j in range(GT):
            last = v.bn_stats(bn[:, j, :], bank[:, j, :])
        last.then_inc(bn_done.sem, 1)
        bn_done.wait(v, turn, 0)
        settle(v)
        for j in range(GT):
            last = v.bn_aggr(mv[:, j, :], bn[:, j, :])
        last.then_inc(mv_done.sem, 1)
        rstd_sb.wait(v, turn, 0)
        mv_done.wait(v, turn, 0)
        for j in range(GT):
            last = v.tensor_scalar(xn[:, j, :], bank[:, j, :], mv[:, j, 0:1], rstd[:, j:j + 1],
                                   ALU.subtract, ALU.mult)
        last.then_inc(xn_sb.sem, 1)
        softmax(turn + 1, 0)
        products(turn + 1, 2, 0)
        normalise(turn + 1, 1, 0)
        normalise(turn + 1, 1, 1)
        sum_up(turn + 1, 0)
        for c, (o, m) in enumerate(FCH):
            gelu_sb.wait(v, turn, c)
            y_ps.wait(v, turn, -1)
            v.scalar_tensor_tensor(uT[0:m, c, :], wide_slot(("ff", c))[0:m, GW:2 * GW], vec(3 + c, m),
                                   gl[0:m, c % 2, :], ALU.add, ALU.mult).then_inc(u_sb.sem, 1)
        norms(turn + 1, 2, 0)
        y_ps.wait(v, turn, 0)
        xf_sb.wait(v, turn, 0)
        at = hT[:, bass.ds(g * GW, GW)]
        v.scalar_tensor_tensor(at, wide_slot(("y", 0))[:, 0:GW], vec(2), at, ALU.add, ALU.add) \
            .then_inc(x2.sem, 1)

    def gpsimd(pool):
        for s in (tab_sb, clamped, rinv, rotated, k_prev, rstd_a, rstd_sb):
            s.start(pool, nth)
        pool.wait_ge(x_ready, 1)
        pool.memset(vbd[0][:], 0.0)
        pool.memset(vbd[1][:], 0.0).then_inc(zeroed, 1)
        layernorm_gpsimd(pool, var0, rstd0, small, minus_half, nth + 1)
        pool.wait_ge(zeroed, 2 * nth + 2)
        pool.wait_ge(consts, 16 * N_CONSTS * (nth + 1))
        pool.wait_ge(h0, 4 * nth + 4)
        tables(pool, base, 0, 0, 0)
        for u in range(2):
            rotate(pool, base, 0, u)
        tables(pool, base, 0, 0, 1)
        previous_keys(pool, base, 0)
        for u in range(2):
            rotate(pool, base, 1, u)
        tables(pool, base, 0, 0, 2)
        previous_keys(pool, base, 1)
        rotate(pool, base, 2, 0)
        with pool.Fori(0, DEPTH) as layer:
            with pool.Fori(0, NG) as g:
                gpsimd_turn(pool, base + layer * NG + g, layer, g)

    def tables(pool, turn, layer, group, j):
        prod_sb.wait(pool, turn, 2 * j - 3)
        settle(pool)
        pool.tensor_tensor(tab[j % 2][:].rearrange("p u s c -> p (u s) c"),
                           tabs[:, at(group * GT + j), :, :, :].rearrange("p t u s c -> p (t u s) c"),
                           gains[:, at(layer), :, :].rearrange("p l u c -> p (l u) c")
                           .unsqueeze(2).broadcast_to([P, 2, 2, DH]), ALU.mult).then_inc(tab_sb.sem, 1)

    def rotate(pool, turn, j, u):
        half = DH // 2
        dst, src = qk[j % 2][u], prod[u]
        prod_sb.wait(pool, turn, 2 * j + u)
        qkT_ps.wait(pool, turn, 4 * (j - 2) + 2 * u + 1)
        pool.tensor_tensor(dst[:, :, 0:half], src[:, :, 0, 0:half], src[:, :, 1, half:], ALU.add)
        pool.tensor_tensor(dst[:, :, half:], src[:, :, 0, half:], src[:, :, 1, 0:half], ALU.add) \
            .then_inc(rotated.sem, 1)
        st = stat[:, j % 2, u, :]
        sums.wait(pool, turn, 2 * j + u)
        settle(pool)
        pool.tensor_scalar(st, st, 1e-24, None, ALU.max).then_inc(clamped.sem, 1)
        clamped.wait(pool, turn, 2 * j + u)
        pool.tensor_tensor(st, st, minus_half[:, 0:H], ALU.pow).then_inc(rinv.sem, 1)

    def previous_keys(pool, turn, j):
        qkT_sb.wait(pool, turn, 4 * j - 1)
        s_ps.wait(pool, turn, j - 2)
        settle(pool)
        pool.tensor_scalar(kT[j % 2][:, :, :, 0:WIN], kT[1 - j % 2][:, :, :, P:P + WIN], decay[:, 0:1],
                           None, ALU.mult).then_inc(k_prev.sem, 1)

    def gpsimd_turn(pool, turn, layer, g):
        following, following_layer = (g + 1) % NG, layer + ((g + 1) // NG)
        for j in range(1, GT):
            if j == GT - 1:
                tables(pool, turn + 1, following_layer, following, 0)
            elif j > 1:
                tables(pool, turn, layer, g, j + 1)
            projected = turn + (j + 1) // GT
            if j > 1:
                previous_keys(pool, turn, j)
                rotate(pool, projected, (j + 1) % GT, 0)
            rotate(pool, projected, (j + 1) % GT, 1)
        tables(pool, turn + 1, following_layer, following, 1)
        previous_keys(pool, turn + 1, 0)
        rotate(pool, turn + 1, 1, 0)
        tables(pool, turn + 1, following_layer, following, 2)
        mv_done.wait(pool, turn, 0)
        settle(pool)
        pool.tensor_scalar(rstd[:], mv[:, :, 1], 1e-5, None, ALU.add).then_inc(rstd_a.sem, 1)
        rstd_a.wait(pool, turn, 0)
        pool.tensor_tensor(rstd[:], rstd[:], minus_half[:, 0:GT], ALU.pow).then_inc(rstd_sb.sem, 1)
        rotate(pool, turn + 1, 1, 1)
        previous_keys(pool, turn + 1, 1)
        rotate(pool, turn + 1, 2, 0)

    N_CONSTS = 3 + 2 + 3 + 6
    add_phase(sync=sync, tensor=tensor, scalar=scalar, vector=vector, gpsimd=gpsimd)


def build_full_attention(nc, settle, ps, xtok, ident, minus_half, small, d, sem, add_phase, x_ready, x_next):
    NKB = T // 512
    QG = 2
    NGR = NT // QG
    KB = NT // NKB
    PT_BANK, C_BANK, O_BANK = 4, 6, 7
    with ExitStack() as mem:
        def sb(name, shape, dt=F32):
            return mem.enter_context(nc.sbuf_tensor("b_" + name, shape, dt))

        xT = sb("xT", [P, T])
        w = [sb(f"w{i}", [P, 3, P]) for i in range(2)]
        wo = sb("wo", [P, H, P])
        qkv = sb("qkv", [P, NT, 3 * P])
        q2 = sb("q2", [P, T], F32R)
        k_hi = sb("k_hi", [P, T], F32R)
        k_lo = sb("k_lo", [P, T], F32R)
        both = sb("both", [P, 2, NT, P])
        twice = [both[:, i] for i in range(2)]
        square = both[:].rearrange("p u t c -> p (u t c)").rearrange("p (t c) -> p t c", c=2 * P)
        gam = sb("gam", [P, 2, H + 1])
        lnv = sb("lnv", [P, 2])
        pr = [sb(f"pr{i}", [P, T]) for i in range(2)]
        v2 = sb("v2", [P, NT, 2, 2, DH], F32R)
        p_hi = [sb(f"p_hi{i}", [P, NT, QG, P], F32R) for i in range(2)]
        p_lo = [sb(f"p_lo{i}", [P, NT, QG, P], F32R) for i in range(2)]
        mx = sb("mx", [P, 2, NKB])
        nm = sb("nm", [P, 2])
        rs = sb("rs", [P, 4, QG, NKB])
        ri = sb("ri", [P, 2, 2, QG])
        cT = sb("cT", [P, 2, QG * P])
        y = sb("y", [P, NT, P])
        ssq = sb("ssq", [P, 4 * NT])
        rinv = sb("rinv", [P, 4 * NT])
        half = sb("half", [P, 4 * NT])
        lnx = qkv[:].rearrange("p t c -> p (t c)")[:, 0:T].rearrange("p (t c) -> p t c", c=P)
        lnsq = twice[0]

    chain = Chain(sem("b_dve"))
    var1, rstd1, var2, rstd2 = (sem(f"b_norm{i}") for i in range(4))
    normed, xT_ps, xT_sb = sem("b_normed"), sem("b_xT_ps"), sem("b_xT_sb")
    consts, half_set, gam_set, summed = sem("b_consts"), sem("b_half"), sem("b_gam"), sem("b_summed")
    w_ld = [sem(f"b_w_ld{i}") for i in range(2)]
    N_CONSTS = 8

    class Count:

        def __init__(self, name, ahead=0):
            self.sem, self.ahead = sem("b_" + name), ahead + 1

        def start(self, eng):
            eng.sem_inc(self.sem, self.ahead)

        def wait(self, eng, n):
            eng.wait_ge(self.sem, self.ahead + n)

    qkv_ps, dup_ps = Count("qkv_ps"), Count("dup_ps")
    s_ps, pT_ps, pv_kt, o_ps = Count("s_ps"), Count("pT_ps", 2 * NKB), Count("pv", 2 * NKB), Count("o_ps", 2)
    qkv_sb, v_hi, hi_sb = Count("qkv_sb"), Count("v_hi"), Count("hi_sb")
    exp_sb, p_hi_sb, c_sb = Count("exp", 2 * NKB), Count("p_hi"), Count("c_sb", 1)
    ss_sb, lo_sb, sq_sums = Count("ss"), Count("lo_sb"), Count("sq_sums")
    bank_max, neg_max, p_lo_sb = Count("bank_max"), Count("neg_max"), Count("p_lo", 2)
    rsum, rrec, y_sb = Count("rsum"), Count("rrec"), Count("y", QG)
    v_lo, squared, rinv_sb, qk_sb = Count("v_lo"), Count("squared"), Count("rinv"), Count("qk")

    def sync(sp):
        sp.wait_ge(x_ready, 1)
        for h2 in range(2):
            sp.dma_start(wo[DH * h2:DH * h2 + DH, :, :], d["b_Wo"].rearrange("(h c) n -> c h n", c=DH)) \
                .then_inc(consts, 16)
        for u, name in enumerate(("b_q_gamma", "b_k_gamma")):
            for h2 in range(2):
                sp.dma_start(gam[DH * h2:DH * h2 + DH, u, 0:H], d[name].rearrange("h c -> c h"),
                             allow_slow_non_contiguous=True).then_inc(consts, 16)
        for c, name in enumerate(("b_ln_w", "b_ln_b")):
            sp.dma_start(lnv[:, c:c + 1], d[name].rearrange("(p a) -> p a", a=1)).then_inc(consts, 16)
        for pair in range(HP + 1):
            if pair >= 2:
                qkv_ps.wait(sp, NT * (pair - 1))
            hp = pair % HP
            for u in range(3):
                src = d["b_Wq"][:, hp * P:(hp + 1) * P] if u == 0 else \
                    d["b_Wkv"][:, (u - 1) * INNER + hp * P:(u - 1) * INNER + (hp + 1) * P]
                sp.dma_start(w[pair % 2][:, u, :], src).then_inc(w_ld[pair % 2], 16)

    def unit(head, i):
        return head * NT + i

    def values_steps(i):
        if i == NT:
            return [(NGR - 2, (2, 3)), (NGR - 1, (0, 1, 2, 3))]
        if i < 3:
            return []
        g = (i - 3) // 2
        return [(g, (0, 1) if i % 2 else (2, 3))] if g < NGR - 1 else []

    def result_group(i):
        return (i - 5) // 2 if i >= 5 and i % 2 else None

    def projected(i):
        return (2 * i - 2, 2 * i - 1) if 1 <= i <= NT // 2 else ()

    def tensor(pe):
        for s in (qkv_ps, dup_ps, s_ps, pT_ps, pv_kt, o_ps):
            s.start(pe)
        pe.wait_ge(normed, 1)
        transpose_tiles(pe, ps, lambda t: lnx[:, t, :], ident, range(4), xT_ps)
        pe.wait_ge(xT_sb, 4)
        pe.wait_ge(consts, 16 * N_CONSTS)
        pe.wait_ge(w_ld[0], 48)
        for t in range(NT):
            project_tile(pe, 0, 0, t, 4)
        for u in range(2):
            for b in range(NKB):
                lay_out(pe, 0, u, b)
        for b in range(NKB):
            score(pe, 0, 0, b)
        with pe.Fori(0, HP // 2) as hq:
            for e in range(2):
                pair = 2 * hq + e
                for h2 in range(2):
                    tensor_head(pe, pair, 2 * pair + h2, h2, e, hq)

    def project_tile(pe, pair, parity, t, ring):
        bank = 8 - ring + t % ring
        qkv_sb.wait(pe, pair * NT + max(t - ring + 1, 0))
        pe.matmul(ps[:, bank, 0:3 * P], xT[:, t * P:(t + 1) * P], w[parity][:].rearrange("p u c -> p (u c)"),
                  start=True, stop=True).then_inc(qkv_ps.sem, 1)

    def lay_out(pe, head, u, b):
        qk_sb.wait(pe, head * 2 + u + 1)
        if u == 0:
            exp_sb.wait(pe, unit(head, -1) * NKB + b + 1)
        else:
            lo_sb.wait(pe, head * 8 + b + 1)
        for k in range(KB):
            last = pe.transpose(ps[:, b, k * P:(k + 1) * P], twice[u][:, KB * b + k, :], ident[:])
        last.then_inc(dup_ps.sem, 1)

    def score(pe, head, i, b):
        if i:
            exp_sb.wait(pe, unit(head, i - 1) * NKB + b + 1)
        else:
            lo_sb.wait(pe, head * 8 + 4 + b + 1)
        pe.matmul(ps[:, b, :], q2[:, i * P:(i + 1) * P], k_hi[:, 512 * b:512 * b + 512], start=True, stop=False)
        pe.matmul(ps[:, b, :], q2[:, i * P:(i + 1) * P], k_lo[:, 512 * b:512 * b + 512],
                  start=False, stop=True).then_inc(s_ps.sem, 1)

    def transpose_probabilities(pe, head, i, b):
        n = unit(head, i) * NKB + b
        exp_sb.wait(pe, n + 1)
        p_lo_sb.wait(pe, n - 1)
        for k in range(KB):
            last = pe.transpose(ps[:, PT_BANK + b % 2, k * P:(k + 1) * P],
                                pr[i % 2][:, (KB * b + k) * P:(KB * b + k + 1) * P], ident[:])
        last.then_inc(pT_ps.sem, 1)

    def times_values(pe, head, h2, g, b, part_of_bank):
        if b == 0:
            c_sb.wait(pe, head * NGR + g)
        p_lo_sb.wait(pe, unit(head, QG * g + QG - 1) * NKB + b + 1)
        for k in (0, 1) if part_of_bank == 0 else (2, 3):
            t = KB * b + k
            for part in (p_hi[g % 2], p_lo[g % 2]):
                last = pe.matmul(ps[:, C_BANK, 0:QG * P], v2[:, t, h2].rearrange("p r c -> p (r c)"),
                                 part[:, t].rearrange("p a b -> p (a b)"),
                                 start=(t == 0 and part is p_hi[g % 2]),
                                 stop=(t == NT - 1 and part is p_lo[g % 2]))
        if part_of_bank:
            last.then_inc(pv_kt.sem, 1)

    def project_out(pe, head, g, copied):
        c_sb.wait(pe, head * NGR + g + 1)
        y_sb.wait(pe, (head * NGR + g) * QG)
        qkv_sb.wait(pe, copied)
        settle(pe)
        for r in range(QG):
            last = pe.matmul(ps[:, O_BANK, r * P:(r + 1) * P], cT[:, g % 2, r * P:(r + 1) * P],
                             wo[:, at(head), :].rearrange("p a n -> p (a n)"), start=True, stop=True)
        last.then_inc(o_ps.sem, 1)

    def tensor_head(pe, pair, head, h2, e, hq):
        if h2:
            pe.wait_ge(w_ld[1 - e], (hq + e) * 48 + 48)
            settle(pe)
        for i in range(NT + 1):
            values = [(g, b, part) for g, banks in values_steps(i) for b in banks for part in range(2)]
            tiles = projected(i) if h2 else ()
            copied = (pair + 1) * NT + (min(2 * i, NT) if h2 else 0)

            def ahead(b):
                if i + 1 < NT:
                    score(pe, head, i + 1, b)
                elif i + 1 == NT:
                    lay_out(pe, head + 1, 0, b)
                else:
                    lay_out(pe, head + 1, 1, b)

            def values_piece():
                if values:
                    times_values(pe, head, h2, *values.pop(0))

            if h2 == 0 and i == 3:
                v_lo.wait(pe, pair + 1)
            def transpose_bank(i, b):
                if 0 <= i < NT:
                    transpose_probabilities(pe, head, i, b)

            if i < NT:
                transpose_bank(i - 1, 2)
                ahead(0)
                ahead(1)
                transpose_bank(i - 1, 3)
                if tiles:
                    y_sb.wait(pe, (head * NGR + max((i - 4) // 2, 0)) * QG)
                    project_tile(pe, pair + 1, 1 - e, tiles[0], 1)
                values_piece()
                ahead(2)
                transpose_bank(i, 0)
                ahead(3)
                if tiles:
                    project_tile(pe, pair + 1, 1 - e, tiles[1], 1)
                transpose_bank(i, 1)
                values_piece()
                if result_group(i) is not None:
                    project_out(pe, head, result_group(i), copied)
                values_piece()
                values_piece()
            else:
                transpose_bank(i - 1, 2)
                ahead(0)
                ahead(1)
                for _ in range(4):
                    values_piece()
                transpose_bank(i - 1, 3)
                ahead(2)
                ahead(3)
                for _ in range(4):
                    values_piece()
                for b in range(NKB):
                    score(pe, head + 1, 0, b)
                project_out(pe, head, NGR - 2, copied)
                for _ in range(4):
                    values_piece()
        project_out(pe, head, NGR - 1, copied)

    def scalar(act):
        for s in (qkv_sb, v_hi, hi_sb, exp_sb, p_hi_sb, c_sb):
            s.start(act)
        act.wait_ge(consts, 16 * N_CONSTS)
        for b in range(4):
            act.wait_ge(xT_ps, b + 1)
            act.activation(xT[:, 512 * b:512 * b + 512], ps[:, b, :], ACT.Identity, scale=lnv[:, 0:1],
                           bias=lnv[:, 1:2]).then_inc(xT_sb, 1)
        for t in range(NT):
            copy_tile(act, 0, t, 4)
        act.wait_ge(gam_set, 1)
        for u in range(2):
            for b in range(NKB):
                high_of(act, 0, u, b)
        with act.Fori(0, HP // 2) as hq:
            for e in range(2):
                for h2 in range(2):
                    scalar_head(act, 2 * hq + e, 2 * (2 * hq + e) + h2, h2)

    def copy_tile(act, pair, t, ring):
        if t == 0:
            qk_sb.wait(act, pair * 4)
            v_lo.wait(act, pair)
        qkv_ps.wait(act, pair * NT + t + 1)
        act.activation(qkv[:, t, :], ps[:, 8 - ring + t % ring, 0:3 * P], ACT.Copy).then_inc(qkv_sb.sem, 1)

    def gain(u, head, rows=slice(0, P)):
        return gam[rows, u, at(head)]

    def high_of(act, head, u, b):
        dup_ps.wait(act, head * 8 + 4 * u + b + 1)
        settle(act)
        act.activation((q2, k_hi)[u][:, 512 * b:512 * b + 512], ps[:, b, :], ACT.Copy,
                       scale=gain(u, head)).then_inc(hi_sb.sem, 1)

    def high_parts(act, head, i, b):
        g = i // QG
        pT_ps.wait(act, unit(head, i) * NKB + b + 1)
        pv_kt.wait(act, (head * NGR + g - 2) * NKB + b + 1)
        act.activation(p_hi[g % 2][:, KB * b:KB * b + KB, i % QG, :],
                       ps[:, PT_BANK + b % 2, :].rearrange("p (a c) -> p a c", c=P), ACT.Copy) \
            .then_inc(p_hi_sb.sem, 1)

    def store_result(act, head, g):
        pv_kt.wait(act, (head * NGR + g) * NKB + NKB)
        o_ps.wait(act, head * NGR + g - 1)
        act.activation(cT[:, g % 2, :], ps[:, C_BANK, 0:QG * P], ACT.Copy).then_inc(c_sb.sem, 1)

    def scalar_head(act, pair, head, h2):
        for i in range(NT + 1):
            tiles = projected(i) if h2 else ()
            g = result_group(i)

            def exponentials(b):
                neg_max.wait(act, unit(head, i) + 1)
                pT_ps.wait(act, unit(head, i - 1) * NKB)
                act.activation(pr[i % 2][:, 512 * b:512 * b + 512], ps[:, b, :], ACT.Exp,
                               bias=nm[:, i % 2:i % 2 + 1],
                               accum_out=rs[:, i // QG % 4, i % QG, b:b + 1]).then_inc(exp_sb.sem, 1)

            def high_before(b):
                if i:
                    high_parts(act, head, i - 1, b)

            if i == NT:
                high_before(2)
                high_of(act, head + 1, 1, 0)
                high_of(act, head + 1, 1, 1)
                high_before(3)
                store_result(act, head, NGR - 2)
                high_of(act, head + 1, 1, 2)
                high_of(act, head + 1, 1, 3)
                store_result(act, head, NGR - 1)
                continue
            exponentials(0)
            exponentials(1)
            high_before(2)
            if g is not None:
                store_result(act, head, g)
            exponentials(2)
            high_before(3)
            if tiles:
                copy_tile(act, pair + 1, tiles[0], 1)
            exponentials(3)
            if i == 0 and h2 == 0:
                pv_kt.wait(act, head * NGR * NKB)
                qkv_sb.wait(act, pair * NT + NT)
                act.activation(v2[:, :, :, 0, :], qkv[:, :, 2 * P:].rearrange("p t (h c) -> p t h c", c=DH),
                               ACT.Copy).then_inc(v_hi.sem, 1)
            high_parts(act, head, i, 0)
            if tiles:
                copy_tile(act, pair + 1, tiles[1], 1)
            high_parts(act, head, i, 1)
            if i == NT - 1:
                for b in range(NKB):
                    high_of(act, head + 1, 0, b)

    def vector(v):
        for s in (ss_sb, lo_sb, sq_sums, bank_max, neg_max, p_lo_sb, rsum, rrec, y_sb):
            s.start(v)
        v.wait_ge(x_ready, 1)
        layernorm_vector(v, chain, var1, rstd1, xtok[:], lnx, lnsq, small)
        layernorm_vector(v, chain, var2, rstd2, lnx, lnx, lnsq, small)
        v.sem_inc(normed, 1)
        v.memset(y[:], 0.0)
        v.memset(gam[:, :, H:], 0.0)
        v.memset(half[:], -0.5).then_inc(half_set, 1)
        v.wait_ge(consts, 16 * N_CONSTS)
        v.tensor_scalar(gam[:, :, 0:H], gam[:, :, 0:H], 8.0, None, ALU.mult).then_inc(gam_set, 1)
        v.wait_ge(gam_set, 1)
        for c in range(4):
            sum_squares(v, 0, c)
        mean_squares(v, 0)
        for u in range(2):
            for b in range(NKB):
                low_of(v, 0, u, b)
        for b in range(NKB):
            maximum(v, 0, 0, b)
        with v.Fori(0, HP // 2) as hq:
            for e in range(2):
                for h2 in range(2):
                    vector_head(v, 2 * hq + e, 2 * (2 * hq + e) + h2, h2)
        qk_sb.wait(v, 4 * HP + 2)
        y_sb.wait(v, H * NT)
        chain.add(v.tensor_tensor(xtok[:], xtok[:], y[:], ALU.add))
        chain.wait(v)
        v.sem_inc(x_next, 1)

    def sum_squares(v, pair, c):
        squared.wait(v, pair * 4 + c + 1)
        if c == 0:
            rinv_sb.wait(v, pair)
        v.tensor_reduce(ssq[:, 16 * c:16 * c + 16],
                        square[:, 4 * c:4 * c + 4, :].rearrange("p t (h c) -> p (t h) c", c=DH),
                        axis=AX.X, op=ALU.add).then_inc(sq_sums.sem, 1)

    def mean_squares(v, pair):
        sq_sums.wait(v, pair * 4 + 4)
        v.tensor_scalar(ssq[:], ssq[:], 1.0 / DH, 1e-8, ALU.mult, ALU.add).then_inc(ss_sb.sem, 1)

    def low_of(v, head, u, b):
        hi_sb.wait(v, head * 8 + 4 * u + b + 1)
        rows = slice(DH, P) if u == 0 else slice(0, P)
        hi, lo = (q2, q2) if u == 0 else (k_hi, k_lo)
        cols = slice(512 * b, 512 * b + 512)
        v.scalar_tensor_tensor(lo[rows, cols], ps[rows, b, :], gain(u, head, rows), hi[rows, cols].bitcast(F32),
                               ALU.mult, ALU.subtract).then_inc(lo_sb.sem, 1)

    def low_parts(v, head, i, b):
        p_hi_sb.wait(v, unit(head, i) * NKB + b + 1)
        where = (slice(None), slice(KB * b, KB * b + KB), i % QG)
        g = i // QG
        v.tensor_tensor(p_lo[g % 2][where], ps[:, PT_BANK + b % 2, :].rearrange("p (a c) -> p a c", c=P),
                        p_hi[g % 2][where].bitcast(F32), ALU.subtract).then_inc(p_lo_sb.sem, 1)

    def maximum(v, head, i, b):
        s_ps.wait(v, unit(head, i) * NKB + b + 1)
        v.tensor_reduce(mx[:, i % 2, b:b + 1], ps[:, b, :], axis=AX.X, op=ALU.max).then_inc(bank_max.sem, 1)
        if b == NKB - 1:
            bank_max.wait(v, unit(head, i) * NKB + NKB)
            exp_sb.wait(v, unit(head, i - 1) * NKB)
            v.tensor_reduce(nm[:, i % 2:i % 2 + 1], mx[:, i % 2, :], axis=AX.X, op=ALU.max,
                            negate=True).then_inc(neg_max.sem, 1)

    def add_result(v, head, g):
        gn = head * NGR + g
        sums, inverse = ri[:, g % 2, 0, :], ri[:, g % 2, 1, :]
        exp_sb.wait(v, unit(head, QG * g + QG) * NKB)
        v.tensor_reduce(sums, rs[:, g % 4], axis=AX.X, op=ALU.add).then_inc(rsum.sem, 1)
        rsum.wait(v, gn + 1)
        v.reciprocal(inverse, sums).then_inc(rrec.sem, 1)
        rrec.wait(v, gn + 1)
        y_sb.wait(v, gn * QG)
        o_ps.wait(v, gn + 1)
        for r in range(QG):
            t = QG * g + r
            v.scalar_tensor_tensor(y[:, t, :], ps[:, O_BANK, r * P:(r + 1) * P], inverse[:, r:r + 1],
                                   y[:, t, :], ALU.mult, ALU.add).then_inc(y_sb.sem, 1)

    def vector_head(v, pair, head, h2):
        for i in range(NT + 1):
            g = result_group(i)
            if i == NT:
                low_parts(v, head, i - 1, 2)
                low_of(v, head + 1, 1, 0)
                low_of(v, head + 1, 1, 1)
                low_parts(v, head, i - 1, 3)
                low_of(v, head + 1, 1, 2)
                low_of(v, head + 1, 1, 3)
                continue
            for b in range(NKB):
                if i + 1 < NT:
                    maximum(v, head, i + 1, b)
                if i and b in (1, 2):
                    low_parts(v, head, i - 1, b + 1)
            low_parts(v, head, i, 0)
            low_parts(v, head, i, 1)
            if i == NT - 1:
                for b in range(NKB):
                    low_of(v, head + 1, 0, b)
            if g is not None:
                add_result(v, head, g)
            if h2 and i in (4, 6, 8, 10):
                sum_squares(v, pair + 1, (i - 4) // 2)
            if h2 and i == 10:
                mean_squares(v, pair + 1)
        for b in range(NKB):
            maximum(v, head + 1, 0, b)
        add_result(v, head, NGR - 2)
        add_result(v, head, NGR - 1)

    def gpsimd(pool):
        for s in (v_lo, squared, rinv_sb, qk_sb):
            s.start(pool)
        layernorm_gpsimd(pool, var1, rstd1, small, minus_half)
        layernorm_gpsimd(pool, var2, rstd2, small, minus_half)
        pool.wait_ge(half_set, 1)
        norms(pool, 0)
        normalise(pool, 0, 0)
        with pool.Fori(0, HP) as pair:
            v_hi.wait(pool, pair + 1)
            pool.tensor_tensor(v2[:, :, :, 1, :], qkv[:, :, 2 * P:].rearrange("p t (h c) -> p t h c", c=DH),
                               v2[:, :, :, 0, :].bitcast(F32), ALU.subtract).then_inc(v_lo.sem, 1)
            normalise(pool, 2 * pair + 1, 1)
            norms(pool, pair + 1)
            normalise(pool, 2 * pair + 2, 0)

    def norms(pool, pair):
        dup_ps.wait(pool, pair * 16)
        for c in range(4):
            qkv_sb.wait(pool, pair * NT + 4 * c + 4)
            part = qkv[:, 4 * c:4 * c + 4, 0:2 * P]
            pool.tensor_tensor(square[:, 4 * c:4 * c + 4, :], part, part, ALU.mult).then_inc(squared.sem, 1)
        ss_sb.wait(pool, pair + 1)
        pool.tensor_tensor(rinv[:], ssq[:], half[:], ALU.pow).then_inc(rinv_sb.sem, 1)
        rinv_sb.wait(pool, pair + 1)

    def normalise(pool, head, h2):
        for u in range(2):
            dup_ps.wait(pool, head * 8 - 4 + 4 * u if h2 else head * 8)
            first = u * P + DH * h2
            pool.tensor_tensor(
                twice[u].rearrange("p t (r c) -> p t r c", c=DH),
                qkv[:, :, first:first + DH].unsqueeze(2).broadcast_to([P, NT, 2, DH]),
                rinv[:].rearrange("p (t s) -> p t s", s=4)[:, :, 2 * u + h2:2 * u + h2 + 1]
                .unsqueeze(3).broadcast_to([P, NT, 2, DH]), ALU.mult).then_inc(qk_sb.sem, 1)

    add_phase(sync=sync, tensor=tensor, scalar=scalar, vector=vector, gpsimd=gpsimd)


def shape_constants():
    half = np.arange(0, DH, 2, dtype=np.float32)
    inv_freq = (1.0 / np.float32(10000.0) ** (half / np.float32(DH))).astype(np.float32)
    t = np.arange(T, dtype=np.float32)
    freqs = (t[:, None] * inv_freq[None, :]).astype(np.float32)
    cos, sin = np.cos(freqs.astype(np.float64)), np.sin(freqs.astype(np.float64))
    base = ((half + np.float32(0.4 * DH)) / np.float32(1.4 * DH)).astype(np.float64)
    power = (np.arange(T) % P - P // 2) / (WIN // 2)
    scale = base[None, :] ** power[:, None]
    tabs = np.zeros((T, 2, 2, DH))
    for u, s in enumerate((8.0 * scale, 1.0 / scale)):
        tabs[:, u, 0, :] = np.concatenate([cos * s, cos * s], -1)
        tabs[:, u, 1, :] = np.concatenate([sin * s, -sin * s], -1)
    tabs = tabs.reshape(NT, P, 2, 2, DH).transpose(1, 0, 2, 3, 4).astype(np.float32)
    i = np.arange(P) % WIN
    key = np.arange(2 * WIN)[None, :] - WIN
    masked = (key > i[:, None]) | (key < i[:, None] - WIN)
    general = np.where(masked, NEG, 0.0)
    first = np.where(masked | ((np.arange(P)[:, None] < WIN) & (key < 0)), NEG, 0.0)
    masks = np.stack([first, general], 1)
    decay = np.tile(np.concatenate([base, base]) ** (P / (WIN // 2)), 2)[:, None]
    return {
        "tabs": tabs, "masks": masks.astype(np.float32), "decay": decay.astype(np.float32),
        "ident": np.eye(P, dtype=np.float32),
    }


def kernel(**inputs):
    import concourse.bacc as bacc
    from concourse.bass_utils import run_bass_kernel_spmd as run

    a = {k.removeprefix("L0_"): np.asarray(v) for k, v in inputs.items()}
    arrays = {
        "x": a["attn_a_x"].reshape(T, P),
        "hawk_gamma": a["attn_a_hawk_norm_gamma"], "gmlp_gamma": a["attn_a_gmlp_norm_gamma"],
        "input_wT": a["attn_a_input_w"].T, "gates_wT": a["attn_a_gates_w"].T,
        "output_wT": a["attn_a_output_w"].T, "grow_wT": a["attn_a_grow_w"].T,
        "shrink_wT": a["attn_a_shrink_w"].T,
        "conv_w": a["attn_a_conv_w"].reshape(P, 4), "conv_b": a["attn_a_conv_b"],
        "gates_b": a["attn_a_gates_b"], "forget_base": a["attn_a_forget_base"],
        "b_ln_w": a["attn_b_ln_w"], "b_ln_b": a["attn_b_ln_b"], "b_Wq": a["attn_b_Wq"],
        "b_Wkv": a["attn_b_Wkv"], "b_q_gamma": a["attn_b_q_gamma"].reshape(H, DH),
        "b_k_gamma": a["attn_b_k_gamma"].reshape(H, DH), "b_Wo": a["attn_b_Wo"],
        "Wqkv": a["ffn_Wqkv"], "q_scale": a["ffn_q_scale"], "k_scale": a["ffn_k_scale"],
        "Wo": a["ffn_Wo"], "ln_g": a["ffn_ln_g"], "ln_b": a["ffn_ln_b"], "W1": a["ffn_W1"],
        "b1": a["ffn_b1"], "W2": a["ffn_W2"], "b2": a["ffn_b2"],
    }
    arrays.update(shape_constants())
    arrays = {k: np.ascontiguousarray(v) for k, v in arrays.items()}
    nc = bacc.Bacc("TRN2", target_bir_lowering=False, num_devices=1)
    d = {k: nc.dram_tensor("in_" + k, v.shape, mybir.dt.from_np(v.dtype), kind="ExternalInput").ap()
         for k, v in arrays.items()}
    out = nc.dram_tensor("out", (T, P), F32, kind="ExternalOutput").ap()
    build_program(nc, d, out)
    r = run(nc, [{"in_" + k: v for k, v in arrays.items()}], core_ids=[0])
    return r.results[0]["out"].reshape(1, T, P)
```
